# Optimizing a Trainium2 kernel written in Bass

```python
import numpy as np
import jax
import jax.numpy as jnp

def _softmax(x, axis=-1):
    return jax.nn.softmax(x, axis=axis)

def _gelu(x):
    return jax.nn.gelu(x, approximate=True)

def _silu(x):
    return jax.nn.silu(x)

def _sigmoid(x):
    return jax.nn.sigmoid(x)

def _layernorm(x, axis=-1, eps=1e-05):
    m = jnp.mean(x, axis=axis, keepdims=True)
    v = jnp.var(x, axis=axis, keepdims=True)
    return (x - m) / jnp.sqrt(v + eps)

def _scatter_add(tgt, idx, src, axis=0):
    return tgt.at[idx].add(src)

def _segment_sum(src, seg, n):
    return jax.ops.segment_sum(src, seg, n)
kernel_name = 'mk_conv_attn_hybrid_d4_conv_nchw384_r4_535f80'

def setup_inputs(seed: int=0):
    np.random.seed(seed)
    _w = jnp.asarray

    def _rec_inputs():
        import jax
        import jax.numpy as jnp
        _gk = jax.random.key(seed)
        x = -0.0002221 + 1 * jax.random.normal(jax.random.fold_in(_gk, 1), (16, 96, 16, 16), jnp.float32)
        return x
    x = _rec_inputs()

    def _L0_conv_setup():
        import jax, jax.numpy as jnp
        import numpy as np
        from jax import lax
        NUM_HEADS = 8
        EPS = 1e-12

        def _l2norm(t):
            n = jnp.sqrt(jnp.sum(t * t, axis=-1, keepdims=True))
            return t / jnp.maximum(n, EPS)
        key = jax.random.key(seed)
        k1, k2, k3, k4 = jax.random.split(key, 4)
        b, c, h, w = (16, 96, 16, 16)
        x = jax.random.normal(k1, (b, c, h, w), dtype=jnp.float32)
        w_qkv = jax.random.normal(k2, (3 * c, c), dtype=jnp.float32) * (1.0 / np.sqrt(c))
        w_dw = jax.random.normal(k3, (3 * c, 1, 3, 3), dtype=jnp.float32) * (1.0 / 3.0)
        w_proj = jax.random.normal(k4, (c, c), dtype=jnp.float32) * (1.0 / np.sqrt(c))
        temperature = jnp.ones((1, NUM_HEADS, 1, 1), dtype=jnp.float32)
        return {'x': x, 'w_qkv': w_qkv, 'w_dw': w_dw, 'w_proj': w_proj, 'temperature': temperature}
    _L0_conv_all = _L0_conv_setup()
    _L0_conv_in = {k: v for k, v in _L0_conv_all.items() if k in ('w_qkv', 'w_dw', 'w_proj', 'temperature')}
    del _L0_conv_all

    def _L1_conv_setup():
        import jax, jax.numpy as jnp
        import numpy as np
        C = 96
        K = 13
        EPS = 1e-05

        def bn(y, g, b, m, v):
            scale = (g / jnp.sqrt(v + EPS)).reshape(1, -1, 1, 1)
            shift = (b - m * g / jnp.sqrt(v + EPS)).reshape(1, -1, 1, 1)
            return y * scale + shift

        def dwconv(x, w):
            p = w.shape[-1] // 2
            return jax.lax.conv_general_dilated(x, w, window_strides=(1, 1), padding=[(p, p), (p, p)], dimension_numbers=('NCHW', 'OIHW', 'NCHW'), feature_group_count=x.shape[1])
        key = jax.random.key(seed)
        ks = jax.random.split(key, 16)
        f32 = jnp.float32
        inp = {'x': jax.random.normal(ks[0], (16, C, 56, 56), dtype=f32), 'pw_w': jax.random.normal(ks[1], (C, C), dtype=f32) * 0.05, 'pw_g': jax.random.uniform(ks[2], (C,), dtype=f32) + 0.5, 'pw_b': jax.random.normal(ks[3], (C,), dtype=f32) * 0.1, 'pw_m': jax.random.normal(ks[4], (C,), dtype=f32) * 0.1, 'pw_v': jax.random.uniform(ks[5], (C,), dtype=f32) + 0.5, 'dwk_w': jax.random.normal(ks[6], (C, 1, K, K), dtype=f32) * 0.05, 'dwk_g': jax.random.uniform(ks[7], (C,), dtype=f32) + 0.5, 'dwk_b': jax.random.normal(ks[8], (C,), dtype=f32) * 0.1, 'dwk_m': jax.random.normal(ks[9], (C,), dtype=f32) * 0.1, 'dwk_v': jax.random.uniform(ks[10], (C,), dtype=f32) + 0.5, 'dw1_w': jax.random.normal(ks[11], (C,), dtype=f32) * 0.5, 'dw1_g': jax.random.uniform(ks[12], (C,), dtype=f32) + 0.5, 'dw1_b': jax.random.normal(ks[13], (C,), dtype=f32) * 0.1, 'dw1_m': jax.random.normal(ks[14], (C,), dtype=f32) * 0.1, 'dw1_v': jax.random.uniform(ks[15], (C,), dtype=f32) + 0.5}
        return inp
    _L1_conv_all = _L1_conv_setup()
    _L1_conv_in = {k: v for k, v in _L1_conv_all.items() if k in ('pw_w', 'pw_g', 'pw_b', 'pw_m', 'pw_v', 'dwk_w', 'dwk_g', 'dwk_b', 'dwk_m', 'dwk_v', 'dw1_w', 'dw1_g', 'dw1_b', 'dw1_m', 'dw1_v')}
    del _L1_conv_all

    def _L2_attn_setup():
        import jax, jax.numpy as jnp
        import numpy as np
        NUM_HEADS = 6
        key = jax.random.key(seed)
        k1, k2, k3, k4 = jax.random.split(key, 4)
        B, N, C = (8, 512, 96)
        x = jax.random.normal(k1, (B, N, C), dtype=jnp.float32)
        qkv_w = jax.random.normal(k2, (3 * C, C), dtype=jnp.float32) * C ** (-0.5)
        proj_w = jax.random.normal(k3, (C, C), dtype=jnp.float32) * C ** (-0.5)
        proj_b = jax.random.normal(k4, (C,), dtype=jnp.float32) * 0.01
        temperature = jnp.ones((NUM_HEADS, 1, 1), dtype=jnp.float32)
        return {'x': x, 'qkv_w': qkv_w, 'proj_w': proj_w, 'proj_b': proj_b, 'temperature': temperature}
    _L2_attn_all = _L2_attn_setup()
    _L2_attn_in = {k: v for k, v in _L2_attn_all.items() if k in ('qkv_w', 'proj_w', 'proj_b', 'temperature')}
    del _L2_attn_all

    def _L2_ffn_setup():
        import jax, jax.numpy as jnp
        import numpy as np
        NUM_EXPERTS = 4
        TOP_K = 2
        DIM = 96
        HID = 4 * DIM
        key = jax.random.key(seed)
        ks = jax.random.split(key, 5)
        B, S = (16, 512)
        scale_in = 1.0 / np.sqrt(DIM)
        scale_hid = 1.0 / np.sqrt(HID)
        return {'x': jax.random.normal(ks[0], (B, S, DIM), dtype=jnp.float32), 'gate_w': jax.random.normal(ks[1], (DIM, NUM_EXPERTS), dtype=jnp.float32) * scale_in, 'gate_b': jnp.zeros((NUM_EXPERTS,), dtype=jnp.float32), 'w1': jax.random.normal(ks[2], (NUM_EXPERTS, DIM, HID), dtype=jnp.float32) * scale_in, 'b1': jnp.zeros((NUM_EXPERTS, HID), dtype=jnp.float32), 'w2': jax.random.normal(ks[3], (NUM_EXPERTS, HID, DIM), dtype=jnp.float32) * scale_hid, 'b2': jnp.zeros((NUM_EXPERTS, DIM), dtype=jnp.float32)}
    _L2_ffn_all = _L2_ffn_setup()
    _L2_ffn_in = {k: v for k, v in _L2_ffn_all.items() if k in ('gate_w', 'gate_b', 'w1', 'b1', 'w2', 'b2')}
    del _L2_ffn_all

    def _L3_attn_setup():
        import jax, jax.numpy as jnp
        import numpy as np
        N_HEADS = 6
        HEAD_SIZE = 16
        key = jax.random.key(seed)
        k1, k2, k3, k4 = jax.random.split(key, 4)
        B, T, C = (8, 512, N_HEADS * HEAD_SIZE)
        x = jax.random.normal(k1, (B, T, C), dtype=jnp.float32)
        w_qkv = jax.random.normal(k2, (C, 3 * C), dtype=jnp.float32) * 0.05
        w_proj = jax.random.normal(k3, (C, C), dtype=jnp.float32) * 0.05
        b_proj = jax.random.normal(k4, (C,), dtype=jnp.float32) * 0.05
        return {'x': x, 'w_qkv': w_qkv, 'w_proj': w_proj, 'b_proj': b_proj}
    _L3_attn_all = _L3_attn_setup()
    _L3_attn_in = {k: v for k, v in _L3_attn_all.items() if k in ('w_qkv', 'w_proj', 'b_proj')}
    del _L3_attn_all

    def _L3_ffn_setup():
        import jax, jax.numpy as jnp
        import numpy as np
        NUM_EXPERTS = 4
        TOP_K = 2
        DIM = 96
        HID = 4 * DIM
        key = jax.random.key(seed)
        ks = jax.random.split(key, 5)
        B, S = (16, 512)
        scale_in = 1.0 / np.sqrt(DIM)
        scale_hid = 1.0 / np.sqrt(HID)
        return {'x': jax.random.normal(ks[0], (B, S, DIM), dtype=jnp.float32), 'gate_w': jax.random.normal(ks[1], (DIM, NUM_EXPERTS), dtype=jnp.float32) * scale_in, 'gate_b': jnp.zeros((NUM_EXPERTS,), dtype=jnp.float32), 'w1': jax.random.normal(ks[2], (NUM_EXPERTS, DIM, HID), dtype=jnp.float32) * scale_in, 'b1': jnp.zeros((NUM_EXPERTS, HID), dtype=jnp.float32), 'w2': jax.random.normal(ks[3], (NUM_EXPERTS, HID, DIM), dtype=jnp.float32) * scale_hid, 'b2': jnp.zeros((NUM_EXPERTS, DIM), dtype=jnp.float32)}
    _L3_ffn_all = _L3_ffn_setup()
    _L3_ffn_in = {k: v for k, v in _L3_ffn_all.items() if k in ('gate_w', 'gate_b', 'w1', 'b1', 'w2', 'b2')}
    del _L3_ffn_all
    return {'x': x, 'L0_conv_w_qkv': _L0_conv_in['w_qkv'], 'L0_conv_w_dw': _L0_conv_in['w_dw'], 'L0_conv_w_proj': _L0_conv_in['w_proj'], 'L0_conv_temperature': _L0_conv_in['temperature'], 'L1_conv_pw_w': _L1_conv_in['pw_w'], 'L1_conv_pw_g': _L1_conv_in['pw_g'], 'L1_conv_pw_b': _L1_conv_in['pw_b'], 'L1_conv_pw_m': _L1_conv_in['pw_m'], 'L1_conv_pw_v': _L1_conv_in['pw_v'], 'L1_conv_dwk_w': _L1_conv_in['dwk_w'], 'L1_conv_dwk_g': _L1_conv_in['dwk_g'], 'L1_conv_dwk_b': _L1_conv_in['dwk_b'], 'L1_conv_dwk_m': _L1_conv_in['dwk_m'], 'L1_conv_dwk_v': _L1_conv_in['dwk_v'], 'L1_conv_dw1_w': _L1_conv_in['dw1_w'], 'L1_conv_dw1_g': _L1_conv_in['dw1_g'], 'L1_conv_dw1_b': _L1_conv_in['dw1_b'], 'L1_conv_dw1_m': _L1_conv_in['dw1_m'], 'L1_conv_dw1_v': _L1_conv_in['dw1_v'], 'L2_attn_qkv_w': _L2_attn_in['qkv_w'], 'L2_attn_proj_w': _L2_attn_in['proj_w'], 'L2_attn_proj_b': _L2_attn_in['proj_b'], 'L2_attn_temperature': _L2_attn_in['temperature'], 'L2_ffn_gate_w': _L2_ffn_in['gate_w'], 'L2_ffn_gate_b': _L2_ffn_in['gate_b'], 'L2_ffn_w1': _L2_ffn_in['w1'], 'L2_ffn_b1': _L2_ffn_in['b1'], 'L2_ffn_w2': _L2_ffn_in['w2'], 'L2_ffn_b2': _L2_ffn_in['b2'], 'L3_attn_w_qkv': _L3_attn_in['w_qkv'], 'L3_attn_w_proj': _L3_attn_in['w_proj'], 'L3_attn_b_proj': _L3_attn_in['b_proj'], 'L3_ffn_gate_w': _L3_ffn_in['gate_w'], 'L3_ffn_gate_b': _L3_ffn_in['gate_b'], 'L3_ffn_w1': _L3_ffn_in['w1'], 'L3_ffn_b1': _L3_ffn_in['b1'], 'L3_ffn_w2': _L3_ffn_in['w2'], 'L3_ffn_b2': _L3_ffn_in['b2']}

def reference(x, L0_conv_w_qkv, L0_conv_w_dw, L0_conv_w_proj, L0_conv_temperature, L1_conv_pw_w, L1_conv_pw_g, L1_conv_pw_b, L1_conv_pw_m, L1_conv_pw_v, L1_conv_dwk_w, L1_conv_dwk_g, L1_conv_dwk_b, L1_conv_dwk_m, L1_conv_dwk_v, L1_conv_dw1_w, L1_conv_dw1_g, L1_conv_dw1_b, L1_conv_dw1_m, L1_conv_dw1_v, L2_attn_qkv_w, L2_attn_proj_w, L2_attn_proj_b, L2_attn_temperature, L2_ffn_gate_w, L2_ffn_gate_b, L2_ffn_w1, L2_ffn_b1, L2_ffn_w2, L2_ffn_b2, L3_attn_w_qkv, L3_attn_w_proj, L3_attn_b_proj, L3_ffn_gate_w, L3_ffn_gate_b, L3_ffn_w1, L3_ffn_b1, L3_ffn_w2, L3_ffn_b2):
    import jax
    import jax.numpy as jnp

    def _L0_conv_ref(x, w_qkv, w_dw, w_proj, temperature):
        import jax, jax.numpy as jnp
        import numpy as np
        from jax import lax
        NUM_HEADS = 8
        EPS = 1e-12

        def _l2norm(t):
            n = jnp.sqrt(jnp.sum(t * t, axis=-1, keepdims=True))
            return t / jnp.maximum(n, EPS)
        b, c, h, w = x.shape
        hw = h * w
        d = c // NUM_HEADS
        qkv = jnp.einsum('bchw,oc->bohw', x, w_qkv)
        qkv = lax.conv_general_dilated(qkv, w_dw, window_strides=(1, 1), padding='SAME', feature_group_count=3 * c, dimension_numbers=('NCHW', 'OIHW', 'NCHW'))
        q, k, v = jnp.split(qkv, 3, axis=1)
        q = q.reshape(b, NUM_HEADS, d, hw)
        k = k.reshape(b, NUM_HEADS, d, hw)
        v = v.reshape(b, NUM_HEADS, d, hw)
        q = _l2norm(q)
        k = _l2norm(k)
        scores = jnp.einsum('bhdn,bhen->bhde', q, k) * temperature
        attn = jax.nn.softmax(scores, axis=-1)
        out = jnp.einsum('bhde,bhen->bhdn', attn, v).reshape(b, c, h, w)
        out = jnp.einsum('bchw,oc->bohw', out, w_proj)
        return out

    def _L1_conv_ref(x, pw_w, pw_g, pw_b, pw_m, pw_v, dwk_w, dwk_g, dwk_b, dwk_m, dwk_v, dw1_w, dw1_g, dw1_b, dw1_m, dw1_v):
        import jax, jax.numpy as jnp
        import numpy as np
        C = 96
        K = 13
        EPS = 1e-05

        def bn(y, g, b, m, v):
            scale = (g / jnp.sqrt(v + EPS)).reshape(1, -1, 1, 1)
            shift = (b - m * g / jnp.sqrt(v + EPS)).reshape(1, -1, 1, 1)
            return y * scale + shift

        def dwconv(x, w):
            p = w.shape[-1] // 2
            return jax.lax.conv_general_dilated(x, w, window_strides=(1, 1), padding=[(p, p), (p, p)], dimension_numbers=('NCHW', 'OIHW', 'NCHW'), feature_group_count=x.shape[1])
        y = jnp.einsum('bchw,oc->bohw', x, pw_w)
        x_pw = bn(y, pw_g, pw_b, pw_m, pw_v) + x
        out = bn(dwconv(x_pw, dwk_w), dwk_g, dwk_b, dwk_m, dwk_v)
        out = out + bn(x_pw * dw1_w.reshape(1, -1, 1, 1), dw1_g, dw1_b, dw1_m, dw1_v)
        return jax.nn.gelu(out, approximate=False)

    def _L2_attn_ref(x, qkv_w, proj_w, proj_b, temperature):
        import jax, jax.numpy as jnp
        import numpy as np
        NUM_HEADS = 6
        B, N, C = x.shape
        H = NUM_HEADS
        Dh = C // H
        qkv = (x @ qkv_w.T).reshape(B, N, 3, H, Dh)
        qkv = jnp.transpose(qkv, (2, 0, 3, 1, 4))
        q, k, v = (qkv[0], qkv[1], qkv[2])
        attn = jnp.einsum('bhnd,bhmd->bhnm', q, k) / C ** 0.5
        attn = attn / temperature
        diag = jnp.eye(N, dtype=bool)
        attn = jnp.where(diag, -jnp.inf, attn)
        attn = jax.nn.softmax(attn, axis=-1)
        out = jnp.einsum('bhnm,bhmd->bhnd', attn, v)
        out = jnp.transpose(out, (0, 2, 1, 3)).reshape(B, N, C)
        return out @ proj_w.T + proj_b

    def _L2_ffn_ref(x, gate_w, gate_b, w1, b1, w2, b2):
        import jax, jax.numpy as jnp
        import numpy as np
        NUM_EXPERTS = 4
        TOP_K = 2
        DIM = 96
        HID = 4 * DIM
        scores = jnp.einsum('bsd,de->bse', x, gate_w) + gate_b
        probs = jax.nn.softmax(scores, axis=-1)
        topk_vals, topk_idx = jax.lax.top_k(probs, TOP_K)
        mask = jnp.sum(jax.nn.one_hot(topk_idx, NUM_EXPERTS, dtype=probs.dtype), axis=-2)
        masked = probs * mask
        masked = masked / (jnp.sum(masked, axis=-1, keepdims=True) + 1e-09)
        h = jax.nn.gelu(jnp.einsum('bsd,edh->ebsh', x, w1) + b1[:, None, None, :], approximate=False)
        y = jnp.einsum('ebsh,ehd->ebsd', h, w2) + b2[:, None, None, :]
        out = jnp.einsum('bse,ebsd->bsd', masked, y)
        return out

    def _L3_attn_ref(x, w_qkv, w_proj, b_proj):
        import jax, jax.numpy as jnp
        import numpy as np
        N_HEADS = 6
        HEAD_SIZE = 16
        B, T, C = x.shape
        qkv = x @ w_qkv
        q, k, v = jnp.split(qkv, 3, axis=2)

        def heads(t):
            return t.reshape(B, T, N_HEADS, HEAD_SIZE).transpose(0, 2, 1, 3)
        q, k, v = (heads(q), heads(k), heads(v))
        scale = HEAD_SIZE ** (-0.5)
        scores = jnp.einsum('bhqd,bhkd->bhqk', q, k) * scale
        causal = jnp.tril(jnp.ones((T, T), dtype=bool))
        scores = jnp.where(causal[None, None], scores, jnp.float32(-jnp.inf))
        weights = jax.nn.softmax(scores, axis=-1)
        out = jnp.einsum('bhqk,bhkd->bhqd', weights, v)
        out = out.transpose(0, 2, 1, 3).reshape(B, T, C)
        return out @ w_proj + b_proj

    def _L3_ffn_ref(x, gate_w, gate_b, w1, b1, w2, b2):
        import jax, jax.numpy as jnp
        import numpy as np
        NUM_EXPERTS = 4
        TOP_K = 2
        DIM = 96
        HID = 4 * DIM
        scores = jnp.einsum('bsd,de->bse', x, gate_w) + gate_b
        probs = jax.nn.softmax(scores, axis=-1)
        topk_vals, topk_idx = jax.lax.top_k(probs, TOP_K)
        mask = jnp.sum(jax.nn.one_hot(topk_idx, NUM_EXPERTS, dtype=probs.dtype), axis=-2)
        masked = probs * mask
        masked = masked / (jnp.sum(masked, axis=-1, keepdims=True) + 1e-09)
        h = jax.nn.gelu(jnp.einsum('bsd,edh->ebsh', x, w1) + b1[:, None, None, :], approximate=False)
        y = jnp.einsum('ebsh,ehd->ebsd', h, w2) + b2[:, None, None, :]
        out = jnp.einsum('bse,ebsd->bsd', masked, y)
        return out

    def _gn(v, G=32, eps=1e-05):
        B_, C_, H_, W_ = v.shape
        g = v.reshape(B_, G, C_ // G, H_, W_)
        m = jnp.mean(g, axis=(2, 3, 4), keepdims=True)
        s = jnp.var(g, axis=(2, 3, 4), keepdims=True)
        return ((g - m) / jnp.sqrt(s + eps)).reshape(v.shape)

    def _ln_c(v, eps=1e-06):
        m = jnp.mean(v, axis=1, keepdims=True)
        s = jnp.var(v, axis=1, keepdims=True)
        return (v - m) / jnp.sqrt(s + eps)

    def _ln_t(v, eps=1e-05):
        m = jnp.mean(v, axis=-1, keepdims=True)
        s = jnp.var(v, axis=-1, keepdims=True)
        return (v - m) / jnp.sqrt(s + eps)

    def _to_tokens(v):
        B_, C_, H_, W_ = v.shape
        return v.reshape(B_, C_, H_ * W_).transpose(0, 2, 1)

    def _from_tokens(t, like):
        B_, C_, H_, W_ = like.shape
        return t.transpose(0, 2, 1).reshape(B_, C_, H_, W_)
    x = x + _L0_conv_ref(_gn(x), L0_conv_w_qkv, L0_conv_w_dw, L0_conv_w_proj, L0_conv_temperature)
    x = _L1_conv_ref(x, L1_conv_pw_w, L1_conv_pw_g, L1_conv_pw_b, L1_conv_pw_m, L1_conv_pw_v, L1_conv_dwk_w, L1_conv_dwk_g, L1_conv_dwk_b, L1_conv_dwk_m, L1_conv_dwk_v, L1_conv_dw1_w, L1_conv_dw1_g, L1_conv_dw1_b, L1_conv_dw1_m, L1_conv_dw1_v)
    t = _to_tokens(x)
    t = t + _L2_attn_ref(_ln_t(t), L2_attn_qkv_w, L2_attn_proj_w, L2_attn_proj_b, L2_attn_temperature)
    t = t + _L2_ffn_ref(_ln_t(t), L2_ffn_gate_w, L2_ffn_gate_b, L2_ffn_w1, L2_ffn_b1, L2_ffn_w2, L2_ffn_b2)
    t = t + _L3_attn_ref(_ln_t(t), L3_attn_w_qkv, L3_attn_w_proj, L3_attn_b_proj)
    t = t + _L3_ffn_ref(_ln_t(t), L3_ffn_gate_w, L3_ffn_gate_b, L3_ffn_w1, L3_ffn_b1, L3_ffn_w2, L3_ffn_b2)
    x = _from_tokens(t, x)
    return x

_drawn_inputs = setup_inputs


def setup_inputs(seed=0):
    import zlib

    import numpy as np

    out = dict(_drawn_inputs(seed))
    spreads = {'L0_conv_temperature': (1.0, 0.6),
     'L2_attn_temperature': (1.0, 0.2),
     'L2_ffn_gate_b': (0.0, 0.1),
     'L2_ffn_b1': (0.0, 0.1),
     'L2_ffn_b2': (0.0, 0.1),
     'L3_ffn_gate_b': (0.0, 0.1),
     'L3_ffn_b1': (0.0, 0.1),
     'L3_ffn_b2': (0.0, 0.1)}
    factors = {}
    for name, (base, spread) in spreads.items():
        noise = np.random.default_rng([zlib.crc32(name.encode()), seed]).standard_normal(out[name].shape)
        drawn = base * np.exp(spread * noise) if base else spread * noise
        out[name] = jnp.asarray(drawn.astype(out[name].dtype))
    for name, factor in factors.items():
        out[name] = (out[name] * factor).astype(out[name].dtype)
    return out
```

```python
from contextlib import ExitStack

import concourse.bass as bass
from concourse import mybir

F32 = mybir.dt.float32
BF16 = mybir.dt.bfloat16
ALU = mybir.AluOpType
ACT = mybir.ActivationFunctionType
AX = mybir.AxisListType

P = 128
B, C, HH, WW = 16, 96, 16, 16
N = HH * WW
T = B * N
NT = T // P
TPI = N // P
PAIRS = B // 2
GN_CH = 3
CA_H, CA_D = 8, 12
H, D = 6, 16
VD = D + 1
E, HID = 4, 384
HC = HID // P
KW = 13
R = KW // 2
CG = P // WW
G = C // CG
WIN = WW * KW
LEAD = WW - 1 - R
LINE = (2 * WW - 1) * KW
MASKED = -1.0e30

INS = ['x', 'L0_conv_w_qkv', 'L0_conv_w_dw', 'L0_conv_w_proj', 'L0_conv_temperature', 'L1_conv_pw_w', 'L1_conv_pw_g',
       'L1_conv_pw_b', 'L1_conv_pw_m', 'L1_conv_pw_v', 'L1_conv_dwk_w', 'L1_conv_dwk_g', 'L1_conv_dwk_b',
       'L1_conv_dwk_m', 'L1_conv_dwk_v', 'L1_conv_dw1_w', 'L1_conv_dw1_g', 'L1_conv_dw1_b', 'L1_conv_dw1_m',
       'L1_conv_dw1_v', 'L2_attn_qkv_w', 'L2_attn_proj_w', 'L2_attn_proj_b', 'L2_attn_temperature', 'L2_ffn_gate_w',
       'L2_ffn_gate_b', 'L2_ffn_w1', 'L2_ffn_b1', 'L2_ffn_w2', 'L2_ffn_b2', 'L3_attn_w_qkv', 'L3_attn_w_proj',
       'L3_attn_b_proj', 'L3_ffn_gate_w', 'L3_ffn_gate_b', 'L3_ffn_w1', 'L3_ffn_b1', 'L3_ffn_w2', 'L3_ffn_b2']

VECTORS = ['L1_conv_pw_v', 'L1_conv_dwk_v', 'L1_conv_dw1_v', 'L1_conv_pw_g', 'L1_conv_dwk_g', 'L1_conv_dw1_g',
           'L1_conv_pw_b', 'L1_conv_dwk_b', 'L1_conv_dw1_b', 'L1_conv_pw_m', 'L1_conv_dwk_m', 'L1_conv_dw1_m',
           'L1_conv_dw1_w', 'L2_attn_proj_b']
V_VAR, V_G, V_B, V_M, V_DW1, V_PROJ, V_T0, V_T2 = 0, 3, 6, 9, 12, 13, 14, 15
NV = 16
M_QKV0, M_PROJ0, M_PW, M_QKV2, M_PROJ2 = 0, 3, 4, 5, 8
NM = 9


class Names:
    pass


class Link:

    def __init__(self, eng, sem, base=0):
        self.eng, self.sem, self.base, self.n = eng, sem, base, 0

    def __call__(self, ins):
        self.n += 1
        ins.then_inc(self.sem, 1)
        self.eng.wait_ge(self.sem, self.base + self.n)


def alone(eng, m):
    eng.sem_inc(m.s_waited, 1)


def buffers(nc, ctx):
    def sb(name, shape, dt=F32):
        return ctx.enter_context(nc.sbuf_tensor(name, shape, dt))

    m = Names()
    m.ps = ctx.enter_context(nc.psum_tensor("ps", [P, 8, 512], F32))
    m.ident = sb("ident", [P, P])
    m.ident_b = sb("ident_b", [P, P], BF16)
    m.diag_b = sb("diag_b", [P, P], BF16)
    m.later_b = sb("later_b", [P, P], BF16)
    m.earlier_b = sb("earlier_b", [P, P], BF16)
    m.heads_b = sb("heads_b", [C, C], BF16)
    m.groups = sb("groups", [C, C])
    m.headmask = sb("headmask", [C, H])
    m.before = sb("before", [P, 4, E, E])
    m.power = sb("power", [P, 32])
    m.x = sb("x_sb", [C, B, N])
    m.x1 = sb("x1", [C + 1, T])
    m.tok = sb("tok", [P, NT, C])
    m.chan = sb("chan", [C + 1, T])
    m.mv = sb("mv", [P, NT, 2])
    m.eps = sb("eps", [P, 4])
    m.vecrows = sb("vecrows", [NV, C])
    m.vec = sb("vec", [C, NV])
    m.bn = sb("bn", [C, 2, 3])
    m.raw = sb("raw", [C, NM, C + 1])
    m.wT = sb("wT", [C + 1, NM, C])
    m.dw0 = sb("dw0", [C, 3, 9])
    m.dwk = sb("dwk", [C, KW * KW])
    m.lines = sb("lines", [C, LINE])
    m.lines_d = nc.dram_tensor("lines_d", [C, LINE], F32, kind="Internal").ap()
    m.bias_d = nc.dram_tensor("bias_d", [C, 1], F32, kind="Internal").ap()
    m.qkv3 = sb("qkv3", [C, 3 * C])
    m.proj3 = sb("proj3", [C + 1, C])
    m.ffn = []
    for l in (2, 3):
        f = Names()
        f.gate = sb(f"gate{l}", [C + 1, E])
        f.w1 = sb(f"w1_{l}", [C, E, HID])
        f.b1rows = sb(f"b1rows{l}", [E * HC, P])
        f.b1 = sb(f"b1_{l}", [P, E * HC])
        f.w2 = sb(f"w2_{l}", [P, E * HC, C])
        f.b2 = sb(f"b2_{l}", [P, E, C])
        m.ffn.append(f)
    return m


def setup(nc, m, a, sem):
    s_x, s_vec, s_mat, s_dw, s_rest = (sem(n) for n in ("in_x", "in_vectors", "in_matrices", "in_kernels", "in_rest"))
    m.s_waited = sem("waited")
    m.s_const, s_pool, s_vecT, s_vecS, s_rstd = (sem(n) for n in ("constants", "pool_own", "vectors_turned", "vectors_kept", "bn_rstd"))
    s_dve, s_ones, s_fold, s_wps, s_wT = (sem(n) for n in ("setup_dve", "ones_rows", "folded", "weights_turned", "weights_kept"))
    s_lines = sem("lines_stored")
    n_vec = len(VECTORS) + 2
    with nc.Block() as block:

        @block.sync
        def _(sp):
            for r, name in enumerate(VECTORS):
                sp.dma_start(m.vecrows[r:r + 1, :], a[name].rearrange("(o n) -> o n", o=1)).then_inc(s_vec, 16)
            for r, (name, heads) in ((V_T0, ('L0_conv_temperature', CA_H)), (V_T2, ('L2_attn_temperature', H))):
                sp.dma_start(m.vecrows[r:r + 1, :].rearrange("o (h d e) -> o h d e", h=heads, e=1),
                             bass.AP(a[name].tensor, 0, [[0, 1], [1, heads], [0, C // heads], [1, 1]])).then_inc(s_vec, 16)
            sp.dma_start(m.x[:, :, :], a['x'].rearrange("b c h w -> c b (h w)")).then_inc(s_x, 16)
            sp.dma_start(m.raw[:, M_QKV0:M_QKV0 + 3, 0:C], a['L0_conv_w_qkv'].rearrange("(t o) c -> o t c", t=3)).then_inc(s_mat, 16)
            sp.dma_start(m.raw[:, M_PROJ0, 0:C], a['L0_conv_w_proj']).then_inc(s_mat, 16)
            sp.dma_start(m.raw[:, M_PW, 0:C], a['L1_conv_pw_w']).then_inc(s_mat, 16)
            sp.dma_start(m.raw[:, M_QKV2:M_QKV2 + 3, 0:C], a['L2_attn_qkv_w'].rearrange("(t o) c -> o t c", t=3)).then_inc(s_mat, 16)
            sp.dma_start(m.raw[:, M_PROJ2, 0:C], a['L2_attn_proj_w']).then_inc(s_mat, 16)
            sp.dma_start(m.dw0[:, :, :], a['L0_conv_w_dw'].rearrange("(t o) i h w -> o t (i h w)", t=3)).then_inc(s_dw, 16)
            sp.dma_start(m.dwk[:, :], a['L1_conv_dwk_w'].rearrange("c i h w -> c (i h w)")).then_inc(s_dw, 16)
            for l, f in zip((2, 3), m.ffn):
                sp.dma_start(f.b1rows[:, :], a[f'L{l}_ffn_b1'].rearrange("e (j p) -> (e j) p", p=P)).then_inc(s_mat, 16)
            sp.dma_start(m.qkv3[:, :], a['L3_attn_w_qkv']).then_inc(s_rest, 16)
            sp.dma_start(m.proj3[0:C, :], a['L3_attn_w_proj']).then_inc(s_rest, 16)
            sp.dma_start(m.proj3[C:C + 1, :], a['L3_attn_b_proj'].rearrange("(o n) -> o n", o=1)).then_inc(s_rest, 16)
            for l, f in zip((2, 3), m.ffn):
                sp.dma_start(f.gate[0:C, :], a[f'L{l}_ffn_gate_w']).then_inc(s_rest, 16)
                sp.dma_start(f.gate[C:C + 1, :], a[f'L{l}_ffn_gate_b'].rearrange("(o n) -> o n", o=1)).then_inc(s_rest, 16)
                sp.dma_start(f.w1[:, :, :], a[f'L{l}_ffn_w1'].rearrange("e d h -> d e h")).then_inc(s_rest, 16)
                sp.dma_start(f.w2[:, :, :], a[f'L{l}_ffn_w2'].rearrange("e (j p) d -> p (e j) d", p=P)).then_inc(s_rest, 16)
                sp.dma_start(f.b2[:, :, :], bass.AP(a[f'L{l}_ffn_b2'].tensor, 0, [[0, P], [C, E], [1, C]])).then_inc(s_rest, 16)

            sp.wait_ge(s_fold, 2)
            sp.dma_start(m.lines_d, m.lines[:, :]).then_inc(s_lines, 16)
            sp.dma_start(m.bias_d, m.bn[:, 1, 1:2]).then_inc(s_lines, 16)
            sp.wait_ge(s_lines, 32)

        @block.gpsimd
        def _(pool):
            link = Link(pool, s_pool)
            link(pool.memset(m.ident[:, :], 1.0))
            link(pool.affine_select(out=m.ident[:, :], in_=m.ident[:, :], compare_op=ALU.is_equal, fill=0.0, base=0,
                                    pattern=[[-1, P]], channel_multiplier=1))
            pool.memset(m.power[:, :], -0.5)
            pool.memset(m.eps[:, :], 1e-5)
            link(pool.tensor_copy(m.ident_b[:, :], m.ident[:, :]))
            nc.gpsimd.sem_inc(m.s_const, 1)
            pool.wait_ge(s_vecS, 1)
            link(pool.tensor_scalar(m.bn[:, 0, :], m.vec[:, V_VAR:V_VAR + 3], 1e-5, 0.0, ALU.add, ALU.add))
            pool.tensor_tensor(m.bn[:, 1, :], m.bn[:, 0, :], m.power[0:C, 0:3], ALU.pow).then_inc(s_rstd, 1)
            link(pool.memset(m.diag_b[:, :], 0.0))
            link(pool.affine_select(out=m.diag_b[:, :], in_=m.diag_b[:, :], compare_op=ALU.not_equal, fill=MASKED,
                                    base=0, pattern=[[-1, P]], channel_multiplier=1))
            link(pool.memset(m.later_b[:, :], 0.0))
            link(pool.affine_select(out=m.later_b[:, :], in_=m.later_b[:, :], compare_op=ALU.is_ge, fill=MASKED,
                                    base=0, pattern=[[-1, P]], channel_multiplier=1))
            link(pool.memset(m.earlier_b[:, :], 0.0))
            link(pool.affine_select(out=m.earlier_b[:, :], in_=m.earlier_b[:, :], compare_op=ALU.is_ge, fill=MASKED,
                                    base=0, pattern=[[1, P]], channel_multiplier=-1))
            for tile, blocks, d, fill in ((m.heads_b, CA_H, CA_D, MASKED), (m.groups, C // GN_CH, GN_CH, 0.0)):
                v = tile[:, :].rearrange("p (g d) -> p g d", d=d)
                link(pool.memset(tile[:, :], 0.0 if fill else 1.0))
                link(pool.affine_select(out=v, in_=v, compare_op=ALU.is_ge, fill=fill, base=0,
                                        pattern=[[-d, blocks], [0, d]], channel_multiplier=1))
                link(pool.affine_select(out=v, in_=v, compare_op=ALU.is_ge, fill=fill, base=d - 1,
                                        pattern=[[d, blocks], [0, d]], channel_multiplier=-1))
            link(pool.memset(m.headmask[:, :], 1.0))
            link(pool.affine_select(out=m.headmask[:, :], in_=m.headmask[:, :], compare_op=ALU.is_ge, fill=0.0, base=0,
                                    pattern=[[-D, H]], channel_multiplier=1))
            link(pool.affine_select(out=m.headmask[:, :], in_=m.headmask[:, :], compare_op=ALU.is_ge, fill=0.0,
                                    base=D - 1, pattern=[[D, H]], channel_multiplier=-1))
            link(pool.memset(m.before[:, :, :, :], 1.0))
            link(pool.affine_select(out=m.before[:, :, :, :], in_=m.before[:, :, :, :], compare_op=ALU.is_gt, fill=0.0,
                                    base=0, pattern=[[0, 4], [1, E], [-1, E]], channel_multiplier=0))
            pool.memset(m.x1[C:C + 1, :], 1.0).then_inc(s_ones, 1)
            pool.memset(m.chan[C:C + 1, :], 1.0).then_inc(s_ones, 1)
            pool.wait_ge(s_ones, 2)

        @block.tensor
        def _(pe):
            pe.wait_ge(m.s_const, 1)
            pe.wait_ge(s_vec, 16 * n_vec)
            nc.tensor.transpose(m.ps[0:C, 0, 0:NV], m.vecrows[:, :], m.ident[0:NV, 0:NV]).then_inc(s_vecT, 1)
            pe.wait_ge(s_mat, 16 * 7)
            for k, f in enumerate(m.ffn):
                nc.tensor.transpose(m.ps[:, 1, 16 * k:16 * k + E * HC], f.b1rows[:, :],
                                    m.ident[0:E * HC, 0:E * HC]).then_inc(s_vecT, 1)
            pe.wait_ge(s_fold, 2)
            for k in range(NM):
                nc.tensor.transpose(m.ps[0:C + 1, 2 + k // 5, C * (k % 5):C * (k % 5 + 1)], m.raw[:, k, :],
                                    m.ident[0:C, 0:C]).then_inc(s_wps, 1)

        @block.vector
        def _(dve):
            link = Link(dve, s_dve)
            dve.wait_ge(s_vecT, 1)
            nc.vector.tensor_copy(m.vec[:, :], m.ps[0:C, 0, 0:NV]).then_inc(s_vecS, 1)
            for k in (M_QKV0, M_QKV0 + 1, M_QKV0 + 2, M_PROJ0, M_QKV2, M_QKV2 + 1, M_QKV2 + 2):
                nc.vector.memset(m.raw[:, k, C:C + 1], 0.0).then_inc(s_dve, 1)
            link.n = 7
            dve.wait_ge(s_vecT, 3)
            for k, f in enumerate(m.ffn):
                nc.vector.tensor_copy(f.b1[:, :], m.ps[:, 1, 16 * k:16 * k + E * HC]).then_inc(s_wT, 1)
            dve.wait_ge(s_rstd, 1)
            link(nc.vector.tensor_tensor(m.bn[:, 0, :], m.bn[:, 1, :], m.vec[:, V_G:V_G + 3], ALU.mult))
            link(nc.vector.tensor_tensor(m.bn[:, 1, :], m.bn[:, 0, :], m.vec[:, V_M:V_M + 3], ALU.mult))
            link(nc.vector.tensor_tensor(m.bn[:, 1, :], m.vec[:, V_B:V_B + 3], m.bn[:, 1, :], ALU.subtract))
            dve.wait_ge(s_mat, 16 * 7)
            link(nc.vector.scalar_tensor_tensor(m.raw[:, M_PW, 0:C], m.raw[:, M_PW, 0:C], m.bn[:, 0, 0:1],
                                                m.ident[0:C, 0:C], ALU.mult, ALU.add))
            link(nc.vector.tensor_copy(m.raw[:, M_PW, C:C + 1], m.bn[:, 1, 0:1]))
            link(nc.vector.tensor_copy(m.raw[:, M_PROJ2, C:C + 1], m.vec[:, V_PROJ:V_PROJ + 1]))
            link(nc.vector.reciprocal(m.vec[:, V_T2:V_T2 + 1], m.vec[:, V_T2:V_T2 + 1]))
            link(nc.vector.tensor_scalar(m.raw[:, M_QKV2, 0:C], m.raw[:, M_QKV2, 0:C], m.vec[:, V_T2:V_T2 + 1],
                                         float(C) ** -0.5, ALU.mult, ALU.mult))
            dve.wait_ge(s_dw, 32)
            link(nc.vector.tensor_scalar(m.dwk[:, :], m.dwk[:, :], m.bn[:, 0, 1:2], None, ALU.mult))
            centre = R * KW + R
            link(nc.vector.scalar_tensor_tensor(m.dwk[:, centre:centre + 1], m.vec[:, V_DW1:V_DW1 + 1], m.bn[:, 0, 2:3],
                                                m.dwk[:, centre:centre + 1], ALU.mult, ALU.add))
            link(nc.vector.memset(m.lines[:, :], 0.0))
            nc.vector.tensor_copy(m.lines[:, LEAD * KW:(LEAD + KW) * KW].rearrange("c (k j) -> c k j", j=KW),
                                  m.dwk[:, :].rearrange("c (j k) -> c k j", k=KW)).then_inc(s_fold, 1)
            nc.vector.tensor_tensor(m.bn[:, 1, 1:2], m.bn[:, 1, 1:2], m.bn[:, 1, 2:3], ALU.add).then_inc(s_fold, 1)
            dve.wait_ge(s_wps, NM)
            nc.vector.tensor_copy(m.wT[:, 0:5, :], m.ps[0:C + 1, 2, 0:5 * C].rearrange("p (k c) -> p k c", c=C)).then_inc(s_wT, 1)
            nc.vector.tensor_copy(m.wT[:, 5:NM, :], m.ps[0:C + 1, 3, 0:4 * C].rearrange("p (k c) -> p k c", c=C)).then_inc(s_wT, 1)
            dve.wait_ge(s_rest, 16 * 13)
            dve.wait_ge(s_wT, 4)
            link(nc.vector.tensor_scalar(m.qkv3[:, 0:C], m.qkv3[:, 0:C], float(D) ** -0.5, None, ALU.mult))
            dve.wait_ge(s_x, 16)


def channel_attention(nc, m, sem):
    s_st, s_gm, s_gdve, s_grs, s_xn = (sem(n) for n in ("gn_means", "gn_psum", "gn_dve", "gn_rstd", "gn_done"))
    s_qkv, s_raw, s_ss = (sem(n) for n in ("ca_qkv", "ca_qkv_kept", "ca_squares"))
    s_tap = [sem(f"ca_tap{t}") for t in range(3)]
    s_rn, s_qk, s_tr, s_trs, s_sc, s_nm, s_ex, s_at, s_ap, s_aps, s_out, s_x1, s_pw, s_rc = (sem(n) for n in (
        "ca_norms", "ca_scaled", "ca_turned", "ca_turned_kept", "ca_scores", "ca_max", "ca_exp", "ca_attn",
        "ca_attnproj", "ca_attnproj_kept", "ca_out", "ca_x1", "ca_pool", "ca_recip"))
    ps = m.ps
    with ExitStack() as ctx:
        def sb(name, shape, dt=F32):
            return ctx.enter_context(nc.sbuf_tensor(name, shape, dt))
        st = sb("gn_stats", [C, B, 6])
        mv = sb("gn_mv", [C, B, 2])
        gm = sb("gn_gm", [C, 4, B])
        xn = sb("gn_x", [C, B, N])
        qkv = sb("ca_qkv_raw", [C, 2, 3, N])
        qkc = sb("ca_qk", [C, B, 2, N])
        vc = sb("ca_v", [C, B, N])
        sq = sb("ca_sq", [C, 2, N])
        ss = sb("ca_ss", [C, B, 2])
        rn = sb("ca_rn", [C, B, 2])
        qks = sb("ca_qks", [C, 2, 2, N])
        qkT = sb("ca_qkT", [P, 2, 4, C])
        nm = sb("ca_nm", [C, 2, 1])
        rs = sb("ca_rs", [C, 2, 2])
        at = sb("ca_at", [C, 2, 2, C])
        apT = sb("ca_apT", [C, 2, C])
        with nc.Block() as block:

            @block.gpsimd
            def _(pool):
                pool.wait_ge(s_gdve, 5)
                pool.tensor_scalar(gm[:, 3, :], gm[:, 3, :], 1e-5, 0.0, ALU.add, ALU.add).then_inc(s_pw, 1)
                pool.wait_ge(s_pw, 1)
                pool.tensor_tensor(gm[:, 1, :], gm[:, 3, :], m.power[0:C, 0:B], ALU.pow).then_inc(s_grs, 1)
                pool.wait_ge(s_ss, 2 * B)
                pool.tensor_scalar(ss[:, :, :], ss[:, :, :], 1e-24, 1e-24, ALU.max, ALU.max).then_inc(s_pw, 1)
                pool.wait_ge(s_pw, 2)
                pool.tensor_tensor(rn[:, :, :].rearrange("p b t -> p (b t)"), ss[:, :, :].rearrange("p b t -> p (b t)"),
                                   m.power[0:C, 0:2 * B], ALU.pow).then_inc(s_pw, 1)
                pool.wait_ge(s_pw, 3)
                pool.tensor_scalar(rn[:, :, 0], rn[:, :, 0], m.vec[:, V_T0:V_T0 + 1], 1.0, ALU.mult, ALU.mult).then_inc(s_rn, 1)

            @block.tensor
            def _(pe):
                for s in (s_tr, s_sc, s_ap, s_out):
                    pe.sem_inc(s, 1)
                pe.wait_ge(s_gdve, 1)
                nc.tensor.matmul(ps[0:C, 6, 0:B], m.groups[:, :], gm[:, 0, :], start=True, stop=True).then_inc(s_gm, 1)
                pe.wait_ge(s_gdve, 4)
                nc.tensor.matmul(ps[0:C, 7, 0:B], m.groups[:, :], gm[:, 3, :], start=True, stop=True).then_inc(s_gm, 1)
                pe.wait_ge(s_xn, B)
                with pe.Fori(0, PAIRS) as i:
                    for u in range(2):
                        pe.wait_ge(s_raw, i * 4 + 2 * u)
                        for t in range(3):
                            nc.tensor.matmul(ps[0:C, 2 * u + t // 2, N * (t % 2):N * (t % 2 + 1)], m.wT[0:C, M_QKV0 + t, :],
                                             xn[:, bass.ds(2 * i + u, 1), :].rearrange("p b n -> p (b n)"),
                                             start=True, stop=True).then_inc(s_qkv, 1)
                with pe.Fori(0, PAIRS) as i:
                    for u in range(2):
                        pe.wait_ge(s_qk, i * 4 + 2 * u + 2)
                        for t in range(2):
                            for h in range(2):
                                nc.tensor.transpose(ps[:, u, C * (2 * t + h):C * (2 * t + h + 1)], qks[:, u, t, P * h:P * (h + 1)],
                                                    m.ident[0:C, 0:C]).then_inc(s_tr, 1)
                    for u in range(2):
                        pe.wait_ge(s_trs, i * 2 + u + 1)
                        for h in range(2):
                            nc.tensor.matmul(ps[0:C, 2 + u, 0:C], qkT[:, u, h, :], qkT[:, u, 2 + h, :], start=(h == 0), stop=False)
                        nc.tensor.matmul(ps[0:C, 2 + u, 0:C], m.ident_b[0:C, 0:C], m.heads_b[:, :], start=False,
                                         stop=True).then_inc(s_sc, 1)
                    for u in range(2):
                        pe.wait_ge(s_at, i * 2 + u + 1)
                        nc.tensor.matmul(ps[0:C, 4 + u, 0:C], at[:, u, 1, :], m.wT[0:C, M_PROJ0, :], start=True, stop=True).then_inc(s_ap, 1)
                    for u in range(2):
                        pe.wait_ge(s_aps, i * 2 + u + 1)
                        nc.tensor.matmul(ps[0:C, 6 + u, 0:N], apT[:, u, :], vc[:, bass.ds(2 * i + u, 1), :].rearrange("p b n -> p (b n)"),
                                         start=True, stop=True).then_inc(s_out, 1)

            @block.scalar
            def _(act):
                for s in (s_ex,):
                    act.sem_inc(s, 1)
                nc.scalar.preload_act_table(ACT.Exp)
                with act.Fori(0, PAIRS) as i:
                    for u in range(2):
                        for t in range(3):
                            act.wait_ge(s_tap[t], i * 18 + 1)
                        act.wait_ge(s_qkv, i * 6 + 3 * u + 3)
                        nc.scalar.copy(qkv[:, u, 0:2, :].rearrange("p t n -> p (t n)"), ps[0:C, 2 * u, :]).then_inc(s_raw, 1)
                        nc.scalar.copy(qkv[:, u, 2, :], ps[0:C, 2 * u + 1, 0:N]).then_inc(s_raw, 1)
                with act.Fori(0, PAIRS) as i:
                    for u in range(2):
                        act.wait_ge(s_tap[0], i * 18 + 9 * u + 9 + 1)
                        act.wait_ge(s_tap[1], i * 18 + 9 * u + 9 + 1)
                        for t in range(2):
                            act.wait_ge(s_ss, i * 4 + 2 * u)
                            nc.scalar.activation(sq[:, t, :], qkc[:, bass.ds(2 * i + u, 1), t, :].rearrange("p b n -> p (b n)"), ACT.Square,
                                                 accum_out=ss[:, bass.ds(2 * i + u, 1), t]).then_inc(s_ss, 1)
                act.wait_ge(s_rn, 1)
                with act.Fori(0, PAIRS) as i:
                    for u in range(2):
                        act.wait_ge(s_tr, i * 8 + 1)
                        for t in range(2):
                            nc.scalar.activation(qks[:, u, t, :], qkc[:, bass.ds(2 * i + u, 1), t, :].rearrange("p b n -> p (b n)"),
                                                 ACT.Copy, scale=rn[:, bass.ds(2 * i + u, 1), t]).then_inc(s_qk, 1)
                    for u in range(2):
                        act.wait_ge(s_tr, i * 8 + 4 * u + 4 + 1)
                        act.wait_ge(s_sc, i * 2 + 1)
                        nc.scalar.copy(qkT[:, u, :, :].rearrange("p k c -> p (k c)"), ps[:, u, 0:4 * C]).then_inc(s_trs, 1)
                    for u in range(2):
                        act.wait_ge(s_nm, i * 2 + u + 1)
                        nc.scalar.activation(at[:, u, 0, :], ps[0:C, 2 + u, 0:C], ACT.Exp, bias=nm[:, u, :],
                                             accum_out=rs[:, u, 0:1]).then_inc(s_ex, 1)

            @block.vector
            def _(dve):
                for s in s_tap:
                    dve.sem_inc(s, 1)
                for b in range(B):
                    nc.vector.bn_stats(st[:, b, :], m.x[:, b, :]).then_inc(s_st, 1)
                dve.wait_ge(s_st, B)
                for b in range(B):
                    nc.vector.bn_aggr(mv[:, b, :], st[:, b, :]).then_inc(s_st, 1)
                dve.wait_ge(s_st, 2 * B)
                nc.vector.tensor_copy(gm[:, 0, :], mv[:, :, 0]).then_inc(s_gdve, 1)
                link = Link(dve, s_gdve, 1)
                dve.wait_ge(s_gm, 1)
                link(nc.vector.tensor_scalar(gm[:, 2, :], ps[0:C, 6, 0:B], 1.0 / GN_CH, None, ALU.mult))
                link(nc.vector.tensor_tensor(gm[:, 3, :], gm[:, 0, :], gm[:, 2, :], ALU.subtract))
                nc.vector.tensor_tensor(gm[:, 1, :], gm[:, 3, :], gm[:, 3, :], ALU.mult).then_inc(s_st, 1)
                dve.wait_ge(s_st, 2 * B + 1)
                link(nc.vector.tensor_tensor(gm[:, 3, :], gm[:, 1, :], mv[:, :, 1], ALU.add))
                dve.wait_ge(s_gm, 2)
                link(nc.vector.tensor_scalar(gm[:, 3, :], ps[0:C, 7, 0:B], 1.0 / GN_CH, None, ALU.mult))
                dve.wait_ge(s_grs, 1)
                for b in range(B):
                    nc.vector.tensor_scalar(xn[:, b, :], m.x[:, b, :], gm[:, 2, b:b + 1], gm[:, 1, b:b + 1],
                                            ALU.subtract, ALU.mult).then_inc(s_xn, 1)
                taps = [(0, 0)] + [(dy, dx) for dy in (-1, 0, 1) for dx in (-1, 0, 1) if dy or dx]
                with dve.Fori(0, PAIRS) as i:
                    for u in range(2):
                        dve.wait_ge(s_raw, i * 4 + 2 * u + 2)
                        for n, (dy, dx) in enumerate(taps):
                            y0, y1, x0, x1 = max(0, -dy), HH - max(0, dy), max(0, -dx), WW - max(0, dx)
                            k = 3 * (dy + 1) + dx + 1
                            for t in range(3):
                                src = qkv[:, u, t, :].rearrange("p (y x) -> p y x", x=WW)
                                if t < 2:
                                    dst = qkc[:, bass.ds(2 * i + u, 1), t, :]
                                else:
                                    dst = vc[:, bass.ds(2 * i + u, 1), :]
                                dst = dst.rearrange("p b (y x) -> p (b y) x", x=WW)
                                if n == 0:
                                    nc.vector.tensor_scalar(dst, src, m.dw0[:, t, k:k + 1], None, ALU.mult).then_inc(s_tap[t], 1)
                                    continue
                                dve.wait_ge(s_tap[t], i * 18 + 9 * u + n + 1)
                                ins = nc.vector.scalar_tensor_tensor(
                                    dst[:, y0:y1, x0:x1], src[:, y0 + dy:y1 + dy, x0 + dx:x1 + dx], m.dw0[:, t, k:k + 1],
                                    dst[:, y0:y1, x0:x1], ALU.mult, ALU.add)
                                ins.then_inc(s_tap[t], 1)
                with dve.Fori(0, PAIRS) as i:
                    for u in range(2):
                        dve.wait_ge(s_sc, i * 2 + u + 1 + 1)
                        dve.wait_ge(s_ex, i * 2 + 1)
                        nc.vector.tensor_reduce(nm[:, u, :], ps[0:C, 2 + u, 0:C], AX.X, ALU.max, negate=True).then_inc(s_nm, 1)
                    for u in range(2):
                        dve.wait_ge(s_ex, i * 2 + u + 1 + 1)
                        nc.vector.reciprocal(rs[:, u, 1:2], rs[:, u, 0:1]).then_inc(s_rc, 1)
                        dve.wait_ge(s_rc, i * 2 + u + 1)
                        dve.wait_ge(s_ap, i * 2 + 1)
                        nc.vector.tensor_scalar(at[:, u, 1, :], at[:, u, 0, :], rs[:, u, 1:2], None, ALU.mult).then_inc(s_at, 1)
                    for u in range(2):
                        dve.wait_ge(s_ap, i * 2 + u + 1 + 1)
                        dve.wait_ge(s_out, i * 2 + 1)
                        nc.vector.tensor_copy(apT[:, u, :], ps[0:C, 4 + u, 0:C]).then_inc(s_aps, 1)
                    for u in range(2):
                        dve.wait_ge(s_out, i * 2 + u + 1 + 1)
                        nc.vector.tensor_tensor(m.x1[0:C, bass.ds((2 * i + u) * N, N)], ps[0:C, 6 + u, 0:N],
                                                m.x[:, bass.ds(2 * i + u, 1), :].rearrange("p b n -> p (b n)"), ALU.add).then_inc(s_x1, 1)
                dve.wait_ge(s_x1, B)



def large_conv(nc, m, sem):
    s_win = [sem(f"cv_windows{k}") for k in range(3)]
    s_zero, s_bias, s_pw, s_pwk, s_ct, s_cin = (sem(n) for n in (
        "cv_zeroed", "cv_bias", "cv_pointwise", "cv_pointwise_kept", "cv_turned", "cv_columns"))
    s_cv, s_gl, s_bt, s_btk, s_cm, s_cmk, s_tm, s_tmk, s_st, s_mv = (sem(n) for n in (
        "cv_conv", "cv_gelu", "cv_back", "cv_back_kept", "cv_chan", "cv_chan_kept", "cv_tok", "cv_tok_kept", "cv_stats", "cv_mv"))
    ps = m.ps
    SLOTS = 3
    with ExitStack() as ctx:
        def sb(name, shape, dt=F32):
            return ctx.enter_context(nc.sbuf_tensor(name, shape, dt))
        win = sb("cv_win", [P, SLOTS, CG, WIN])
        rows = sb("cv_rows", [P, 2, C, WW])
        cin = sb("cv_cin", [P, G, B, HH])
        cb = sb("cv_cb", [P, G])
        gl = sb("cv_gl", [P, G, 2, P])
        back = sb("cv_backs", [P, 2, WW, C])
        st = sb("cv_st", [P, NT, 6])

        def load_windows(sp, g, k):
            for c in range(CG):
                sp.dma_start(win[WW * c:WW * (c + 1), k, c, :],
                             bass.AP(m.lines_d.tensor, g * (CG * LINE) + c * LINE, [[KW, WW], [1, WIN]])).then_inc(s_win[k], 16)

        with nc.Block() as block:

            @block.sync
            def _(sp):
                for c in range(CG):
                    sp.dma_start(cb[WW * c:WW * (c + 1), :], bass.AP(m.bias_d.tensor, c, [[0, WW], [CG, G]]),
                                 allow_slow_non_contiguous=True).then_inc(s_bias, 16)
                sp.wait_ge(s_zero, 1)
                for k in range(SLOTS):
                    load_windows(sp, k, k)
                with sp.Fori(1, G // SLOTS) as i:
                    for k in range(SLOTS):
                        sp.wait_ge(s_cv, i * SLOTS + (k + 1 - SLOTS))
                        load_windows(sp, i * SLOTS + k, k)

            @block.gpsimd
            def _(pool):
                pool.memset(win[:, :, :, :], 0.0).then_inc(s_zero, 1)

            @block.tensor
            def _(pe):
                x1v = m.x1[:, :].rearrange("c (h n x) -> c h n x", h=2, x=WW)
                for h in range(2):
                    for x in range(WW):
                        nc.tensor.matmul(ps[:, 4 * h + x // 4, C * (x % 4):C * (x % 4 + 1)], x1v[:, h, :, x],
                                         m.wT[:, M_PW, :], start=True, stop=True).then_inc(s_pw, 1)
                for g in range(G):
                    if g % 2 == 0:
                        pe.wait_ge(s_pwk, 8)
                        if g >= 8:
                            pe.wait_ge(s_cin, g // 2 - 3)
                    for h in range(2):
                        k = 2 * (g % 2) + h
                        nc.tensor.transpose(ps[:, g // 2 % 4, P * k:P * (k + 1)],
                                            rows[:, h, CG * g:CG * (g + 1), :].rearrange("p c x -> p (c x)"),
                                            m.ident[:, :]).then_inc(s_ct, 1)
                pe.wait_ge(s_cin, G // 2)
                with pe.Fori(0, G // SLOTS) as i:
                    for k in range(SLOTS):
                        pe.wait_ge(s_win[k], (i + 1) * (16 * CG))
                        pe.wait_ge(s_gl, i * SLOTS + 1)
                        order = [R] + [j for j in range(KW) if j != R]
                        for n, j in enumerate(order):
                            y0, y1 = max(0, R - j), HH - max(0, j - R)
                            ins = nc.tensor.matmul(
                                ps[:, 4 + k, 0:B * HH].rearrange("p (b y) -> p b y", y=HH)[:, :, y0:y1],
                                win[:, k, :, :].rearrange("p c w -> p (c w)")[:, j:CG * WIN:KW],
                                cin[:, bass.ds(i * SLOTS + k, 1), :, y0 + j - R:y1 + j - R].rearrange("p g b y -> p (g b) y"),
                                start=(n == 0), stop=(n == KW - 1))
                        ins.then_inc(s_cv, 1)
                for g in range(G):
                    pe.wait_ge(s_gl, g + 1 + 1)
                    if g % 2 == 0 and g >= 8:
                        pe.wait_ge(s_btk, g // 2 - 3)
                    for h in range(2):
                        k = 2 * h + g % 2
                        nc.tensor.transpose(ps[:, g // 2 % 4, P * k:P * (k + 1)], gl[:, g, h, :], m.ident[:, :]).then_inc(s_bt, 1)
                pe.wait_ge(s_btk, G // 2)
                for h in range(2):
                    for x in range(WW):
                        nc.tensor.transpose(ps[0:C, 4 * h + x // 4, P * (x % 4):P * (x % 4 + 1)], back[:, h, WW - 1 - x, :],
                                            m.ident[:, :]).then_inc(s_cm, 1)
                pe.wait_ge(s_cmk, 8)
                for t in range(NT):
                    nc.tensor.transpose(ps[:, t // 4, C * (t % 4):C * (t % 4 + 1)], m.chan[0:C, P * t:P * (t + 1)],
                                        m.ident[0:C, 0:C]).then_inc(s_tm, 1)

            @block.scalar
            def _(act):
                for s in (s_gl,):
                    act.sem_inc(s, 1)
                nc.scalar.preload_act_table(ACT.Gelu)
                for q in range(0, 8, 2):
                    act.wait_ge(s_pw, 4 * (q + 1))
                    nc.scalar.copy(rows[:, q // 4, :, 4 * (q % 4):4 * (q % 4 + 1)].rearrange("p c x -> p x c"),
                                   ps[:, q, 0:4 * C].rearrange("p (x c) -> p x c", c=C)).then_inc(s_pwk, 1)
                act.wait_ge(s_bias, 16 * CG)
                with act.Fori(0, G // SLOTS) as i:
                    for k in range(SLOTS):
                        act.wait_ge(s_cv, i * SLOTS + k + 1)
                        nc.scalar.activation(gl[:, bass.ds(i * SLOTS + k, 1), :, :].rearrange("p g h n -> p (g h n)"),
                                             ps[:, 4 + k, 0:B * HH], ACT.Gelu,
                                             bias=cb[:, bass.ds(i * SLOTS + k, 1)]).then_inc(s_gl, 1)

                for q in range(0, 8, 2):
                    act.wait_ge(s_cm, 4 * (q + 1))
                    nc.scalar.copy(m.chan[0:C, :].rearrange("c (h n x) -> c h x n", h=2, x=WW)[:, q // 4, 4 * (q % 4):4 * (q % 4 + 1), :],
                                   ps[0:C, q, :].rearrange("p (x n) -> p x n", x=4)).then_inc(s_cmk, 1)
                for q in range(0, 8, 2):
                    act.wait_ge(s_tm, 4 * (q + 1))
                    nc.scalar.copy(m.tok[:, 4 * q:4 * (q + 1), :].rearrange("p t c -> p (t c)"), ps[:, q, 0:4 * C]).then_inc(s_tmk, 1)

            @block.vector
            def _(dve):
                for q in range(1, 8, 2):
                    dve.wait_ge(s_pw, 4 * (q + 1))
                    nc.vector.tensor_copy(rows[:, q // 4, :, 4 * (q % 4):4 * (q % 4 + 1)].rearrange("p c x -> p x c"),
                                          ps[:, q, 0:4 * C].rearrange("p (x c) -> p x c", c=C)).then_inc(s_pwk, 1)
                for q in range(G // 2):
                    dve.wait_ge(s_ct, 4 * (q + 1))
                    nc.vector.tensor_copy(cin[:, 2 * q:2 * q + 2, :, :].rearrange("p g b y -> p (g b y)"), ps[:, q % 4, :]).then_inc(s_cin, 1)
                for q in range(G // 2):
                    dve.wait_ge(s_bt, 4 * (q + 1))
                    for h in range(2):
                        ins = nc.vector.tensor_copy(
                            back[:, h, :, 2 * CG * q:2 * CG * (q + 1)].rearrange("p x c -> p c x"),
                            ps[:, q % 4, 2 * P * h:2 * P * (h + 1)].rearrange("p (c x) -> p c x", x=WW))
                    ins.then_inc(s_btk, 1)
                for q in range(1, 8, 2):
                    dve.wait_ge(s_cm, 4 * (q + 1))
                    nc.vector.tensor_copy(m.chan[0:C, :].rearrange("c (h n x) -> c h x n", h=2, x=WW)[:, q // 4, 4 * (q % 4):4 * (q % 4 + 1), :],
                                          ps[0:C, q, :].rearrange("p (x n) -> p x n", x=4)).then_inc(s_cmk, 1)
                for q in range(1, 8, 2):
                    dve.wait_ge(s_tm, 4 * (q + 1))
                    nc.vector.tensor_copy(m.tok[:, 4 * q:4 * (q + 1), :].rearrange("p t c -> p (t c)"), ps[:, q, 0:4 * C]).then_inc(s_tmk, 1)
                dve.wait_ge(s_tmk, 8)
                for t in range(NT):
                    nc.vector.bn_stats(st[:, t, :], m.tok[:, t, :]).then_inc(s_st, 1)
                dve.wait_ge(s_st, NT)
                for t in range(NT):
                    nc.vector.bn_aggr(m.mv[:, t, :], st[:, t, :]).then_inc(s_mv, 1)
                dve.wait_ge(s_mv, NT)


def layer_norm(nc, m, pool, i, xn, v, s_own, s_xn, s_free):
    link = Link(pool, s_own, i * 3)
    mean, var = m.mv[:, bass.ds(4 * i, 4), 0], m.mv[:, bass.ds(4 * i, 4), 1]
    alone(pool, m)
    link(pool.tensor_tensor(v[:, 0, :], var, m.eps[:, :], ALU.add))
    link(pool.tensor_tensor(v[:, 1, :], v[:, 0, :], m.power[:, 0:4], ALU.pow))
    pool.wait_ge(*s_free)
    alone(pool, m)
    link(pool.tensor_tensor(xn[:, :, :], m.tok[:, bass.ds(4 * i, 4), :], mean.to_broadcast([P, 4, C]), ALU.subtract))
    alone(pool, m)
    pool.tensor_tensor(xn[:, :, :], xn[:, :, :], v[:, 1, :].to_broadcast([P, 4, C]), ALU.mult).then_inc(s_xn, 1)


def statistics(nc, m, dve, i, st, mv, s_st, s_mv):
    alone(dve, m)
    for t in range(4):
        nc.vector.bn_stats(st[:, t, :], m.tok[:, bass.ds(4 * i + t, 1), :].rearrange("p t c -> p (t c)")).then_inc(s_st, 1)
    dve.wait_ge(s_st, i * 8 + 4)
    alone(dve, m)
    for t in range(4):
        nc.vector.bn_aggr(mv[:, t, :], st[:, t, :]).then_inc(s_st, 1)
    dve.wait_ge(s_st, i * 8 + 8)
    nc.vector.tensor_copy(m.mv[:, bass.ds(4 * i, 4), :], mv[:, :, :]).then_inc(s_mv, 1)


def token_attention(nc, m, sem, layer, w, proj):
    (s_own, s_xn, s_T, s_xT, s_qk, s_qc, s_v, s_vp, s_S, s_mx, s_M, s_mr, s_ST, s_ex, s_O, s_rc, s_on, s_OT, s_oT, s_pr, s_tk,
     s_st, s_mv, s_c) = (sem(f"at{layer}_{n}") for n in (
         "pool_own", "normed", "normed_turned", "xT", "qk", "qk_kept", "v", "v_kept", "scores", "max", "max_turned", "max_rows",
         "scoresT", "exp", "out", "recip", "out_normed", "out_turned", "outT", "proj", "tok", "stats", "mv", "constants"))
    causal = layer == 3
    mask, maskT = (m.later_b, m.earlier_b) if causal else (m.diag_b, m.diag_b)
    ps = m.ps
    A, BB = 0, 3
    CM = C + H
    OW = H * VD
    with ExitStack() as ctx:
        def sb(name, shape, dt=F32):
            return ctx.enter_context(nc.sbuf_tensor(f"at{layer}_b_{name}", shape, dt))
        xn = sb("xn", [P, 4, C])
        v2 = sb("v2", [P, 2, 4])
        xT = sb("xT", [C, 2, N])
        qa = sb("qa", [CM, 2, N])
        km = sb("km", [CM, 2, H, N])
        vp = sb("vp", [P, 2, TPI, H, OW])
        mxp = sb("mxp", [P, 2, TPI, CM])
        pT = sb("pT", [P, 2, TPI, H, N])
        rec = sb("rec", [P, 2, TPI, H])
        on = sb("on", [P, 2, TPI, C])
        oT = sb("oT", [C + 1, 2, N])
        st = sb("st", [P, 4, 6])
        mv = sb("mv", [P, 4, 2])

        def heads(k):
            return ps[:, k:k + 3, :].rearrange("p k n -> p (k n)").rearrange("p (h n) -> p h n", h=H)

        with nc.Block() as block:

            @block.gpsimd
            def _(pool):
                link = Link(pool, s_c)
                link(pool.memset(km[C:CM, :, :, :], 1.0))
                for u in range(2):
                    link(pool.affine_select(out=km[C:CM, u, :, :], in_=km[C:CM, u, :, :], compare_op=ALU.is_equal, fill=0.0,
                                            base=0, pattern=[[-1, H], [0, N]], channel_multiplier=1))
                link(pool.memset(oT[C:C + 1, :, :], 1.0))
                link(pool.memset(mxp[:, :, :, :], 0.0))
                link(pool.memset(vp[:, :, :, :, :], 0.0))
                for u in range(2):
                    for t in range(TPI):
                        blocks = vp[:, u, t, :, :].rearrange("p h w -> p (h w)")
                        link(pool.memset(bass.AP(blocks.tensor, blocks.offset + D, [blocks.ap[0], [OW + VD, H], [1, 1]]), 1.0))
                with pool.Fori(0, PAIRS) as i:
                    layer_norm(nc, m, pool, i, xn, v2, s_own, s_xn, (s_T, i * 2 + 1))

            @block.tensor
            def _(pe):
                for s in (s_T,):
                    pe.sem_inc(s, 1)
                pe.wait_ge(s_c, 10)
                with pe.Fori(0, PAIRS) as i:
                    pe.wait_ge(s_xn, i + 1)
                    pe.wait_ge(s_on, i * 2 + 1)
                    for u in range(2):
                        for t in range(TPI):
                            ins = nc.tensor.transpose(ps[0:C, 6 + u, P * t:P * (t + 1)], xn[:, 2 * u + t, :], m.ident[:, :])
                        ins.then_inc(s_T, 1)
                    pe.wait_ge(s_oT, i * 2 + 1)
                    pe.wait_ge(s_tk, i * 2 + 1)
                    for u in range(2):
                        pe.wait_ge(s_xT, i * 2 + u + 1)
                        for t in range(2):
                            ins = nc.tensor.matmul(ps[0:C, 3 * u, N * t:N * (t + 1)], w[t], xT[:, u, :], start=True, stop=True)
                        ins.then_inc(s_qk, 1)
                        for t in range(TPI):
                            ins = nc.tensor.matmul(ps[:, 3 * u + 1, C * t:C * (t + 1)], xT[:, u, P * t:P * (t + 1)], w[2],
                                                   start=True, stop=True)
                        ins.then_inc(s_v, 1)
                    for u in range(2):
                        for t in range(TPI):
                            bank = heads(3 * t)
                            nk = P if causal and t == 0 else N
                            if u == 0:
                                pe.wait_ge(s_qc, i * 2 + t + 1)
                                pe.wait_ge(s_vp, i * 2 + t + 1)
                            else:
                                pe.wait_ge(s_qc, i * 2 + 2)
                                pe.wait_ge(s_mx, i * 4 + t + 1)
                            for h in range(H):
                                nc.tensor.matmul(bank[:, h, 0:nk], qa[0:C, u, P * t:P * (t + 1)], km[0:C, u, h, 0:nk],
                                                 start=True, stop=False)
                                ins = nc.tensor.matmul(bank[:, h, P * t:P * (t + 1)], m.ident_b[:, :], mask[:, :],
                                                       start=False, stop=True)
                            ins.then_inc(s_S, 1)
                    for u in range(2):
                        pe.wait_ge(s_mx, i * 4 + 2 * u + 2)
                        for t in range(TPI):
                            ins = nc.tensor.transpose(ps[0:CM, 6 + u, P * t:P * (t + 1)], mxp[:, u, t, :], m.ident[:, :])
                        ins.then_inc(s_M, 1)
                        pe.wait_ge(s_mr, i * 2 + u + 1)
                        for t in range(TPI):
                            bank = heads(3 * t)
                            n0 = P if causal and t == 1 else 0
                            if u == 0:
                                pe.wait_ge(s_mx, i * 4 + t + 3)
                            else:
                                pe.wait_ge(s_ex, i * 4 + t + 1)
                            for h in range(H):
                                nc.tensor.matmul(bank[:, h, n0:N], km[:, u, h, P * t:P * (t + 1)], qa[:, u, n0:N],
                                                 start=True, stop=False)
                                ins = nc.tensor.matmul(bank[:, h, P * t:P * (t + 1)], m.ident_b[:, :], maskT[:, :],
                                                       start=False, stop=True)
                            ins.then_inc(s_ST, 1)
                    for u in range(2):
                        pe.wait_ge(s_ex, i * 4 + 2 * u + 2)
                        for t in range(TPI):
                            terms = [(k, h) for k in range(1 if causal and t == 0 else TPI) for h in range(H)]
                            for n, (k, h) in enumerate(terms):
                                ins = nc.tensor.matmul(ps[:, 6 + u, OW * t:OW * (t + 1)], pT[:, u, k, h, P * t:P * (t + 1)],
                                                       vp[:, u, k, h, :], start=(n == 0), stop=(n == len(terms) - 1))
                        ins.then_inc(s_O, 1)
                    for u in range(2):
                        pe.wait_ge(s_on, i * 2 + u + 1 + 1)
                        pe.wait_ge(s_ex, i * 4 + 3 + u)
                        for t in range(TPI):
                            ins = nc.tensor.transpose(ps[0:C, 3 * u, P * t:P * (t + 1)], on[:, u, t, :], m.ident[:, :])
                        ins.then_inc(s_OT, 1)
                    for u in range(2):
                        pe.wait_ge(s_oT, i * 2 + u + 1 + 1)
                        for t in range(TPI):
                            ins = nc.tensor.matmul(ps[:, 3 * u + 1, C * t:C * (t + 1)], oT[:, u, P * t:P * (t + 1)], proj,
                                                   start=True, stop=True)
                        ins.then_inc(s_pr, 1)

            @block.scalar
            def _(act):
                for s in (s_oT,):
                    act.sem_inc(s, 1)
                nc.scalar.preload_act_table(ACT.Exp)
                with act.Fori(0, PAIRS) as i:
                    for u in range(2):
                        act.wait_ge(s_T, i * 2 + u + 1 + 1)
                        nc.scalar.copy(xT[:, u, :], ps[0:C, 6 + u, 0:N]).then_inc(s_xT, 1)
                    for u in range(2):
                        act.wait_ge(s_qk, i * 2 + u + 1)
                        nc.scalar.copy(qa[0:C, u, :], ps[0:C, 3 * u, 0:N])
                        for h in range(H):
                            ins = nc.scalar.activation(km[0:C, u, h, :], ps[0:C, 3 * u, N:2 * N], ACT.Copy,
                                                       scale=m.headmask[:, h:h + 1])
                        ins.then_inc(s_qc, 1)
                    for u in range(2):
                        act.wait_ge(s_M, i * 2 + u + 1)
                        nc.scalar.copy(qa[C:CM, u, :], ps[C:CM, 6 + u, 0:N]).then_inc(s_mr, 1)
                        for t in range(TPI):
                            n0 = P if causal and t == 1 else 0
                            act.wait_ge(s_ST, i * 4 + 2 * u + t + 1)
                            nc.scalar.activation(pT[:, u, t, :, n0:N], heads(3 * t)[:, :, n0:N], ACT.Exp).then_inc(s_ex, 1)
                    for u in range(2):
                        act.wait_ge(s_OT, i * 2 + u + 1)
                        nc.scalar.copy(oT[0:C, u, :], ps[0:C, 3 * u, 0:N]).then_inc(s_oT, 1)

            @block.vector
            def _(dve):
                for s in (s_on, s_tk):
                    dve.sem_inc(s, 1)
                dve.wait_ge(s_c, 10)
                with dve.Fori(0, PAIRS) as i:
                    for u in range(2):
                        dve.wait_ge(s_v, i * 2 + u + 1)
                        for t in range(TPI):
                            blocks = vp[:, u, t, :, :].rearrange("p h w -> p (h w)")
                            ins = nc.vector.tensor_copy(
                                bass.AP(blocks.tensor, blocks.offset, [blocks.ap[0], [OW + VD, H], [1, D]]),
                                ps[:, 3 * u + 1, C * t:C * (t + 1)].rearrange("p (h d) -> p h d", d=D))
                        ins.then_inc(s_vp, 1)
                    for u in range(2):
                        for t in range(TPI):
                            nk = P if causal and t == 0 else N
                            dve.wait_ge(s_S, i * 4 + 2 * u + t + 1)
                            nc.vector.tensor_reduce(mxp[:, u, t, C:CM], heads(3 * t)[:, :, 0:nk], AX.X, ALU.max,
                                                    negate=True).then_inc(s_mx, 1)
                    for u in range(2):
                        dve.wait_ge(s_O, i * 2 + u + 1)
                        o = ps[:, 6 + u, 0:TPI * OW].rearrange("p (t h w) -> p t h w", t=TPI, h=H)
                        nc.vector.reciprocal(rec[:, u, :, :], o[:, :, :, D]).then_inc(s_rc, 1)
                        dve.wait_ge(s_rc, i * 2 + u + 1)
                        nc.vector.tensor_tensor(on[:, u, :, :].rearrange("p t (h d) -> p t h d", d=D), o[:, :, :, 0:D],
                                                rec[:, u, :, :].to_broadcast([P, TPI, H, D]), ALU.mult).then_inc(s_on, 1)
                    for u in range(2):
                        dve.wait_ge(s_pr, i * 2 + u + 1)
                        tok = m.tok[:, bass.ds(4 * i + 2 * u, 2), :]
                        nc.vector.tensor_tensor(tok, ps[:, 3 * u + 1, 0:2 * C].rearrange("p (t c) -> p t c", c=C), tok,
                                                ALU.add).then_inc(s_tk, 1)
                    dve.wait_ge(s_tk, i * 2 + 2 + 1)
                    statistics(nc, m, dve, i, st, mv, s_st, s_mv)
                dve.wait_ge(s_mv, PAIRS)


def experts(nc, m, sem, layer, f, out=None):
    (s_own, s_xn, s_T, s_xT, s_g, s_gc, s_gt, s_sc, s_nm, s_ex, s_gd, s_bt, s_F, s_h, s_Y, s_ac, s_st, s_mv, s_OT, s_oc, s_bc) = (
        sem(f"ff{layer}_{n}") for n in (
            "pool_own", "normed", "normed_turned", "xT", "gate", "gate_kept", "gate_turned", "gate_scores", "gate_shifted",
            "gate_exp", "gate_dve", "biased", "hidden", "gelu", "result", "added", "stats", "mv", "out_turned", "out_kept",
            "pool_bias"))
    s_store = [sem(f"ff{layer}_stored{k}") for k in range(2)]
    last = out is not None
    ps = m.ps
    Q = 4 * P
    with ExitStack() as ctx:
        def sb(name, shape, dt=F32):
            return ctx.enter_context(nc.sbuf_tensor(f"ff{layer}_b_{name}", shape, dt))
        xn = sb("xn", [P, 4, C])
        v2 = sb("v2", [P, 2, 4])
        gs = sb("gs", [E, 2, Q])
        sc = sb("sc", [P, NT, E])
        pr = sb("pr", [P, NT, E])
        gt = sb("gt", [P, NT, E, E])
        eq = sb("eq", [P, NT, E, E])
        one = sb("one", [P, 3, NT])
        gate = sb("gate", [P, NT, E])
        bias = sb("bias", [P, 2, 4, C])
        h = sb("h", [P, 2, HC, Q])
        st = sb("st", [P, 4, 6])
        mv = sb("mv", [P, 4, 2])
        fin = sb("fin", [P, 4, C])
        fT = sb("fT", [C, 2, Q])
        with nc.Block() as block:

            @block.gpsimd
            def _(pool):
                with pool.Fori(0, PAIRS) as i:
                    layer_norm(nc, m, pool, i, xn, v2, s_own, s_xn, (s_T, i + 1))
                pool.wait_ge(s_gd, GATE_STEPS)
                with pool.Fori(0, PAIRS) as i:
                    link = Link(pool, s_bc, i * (2 * E))
                    tok = m.tok[:, bass.ds(4 * i, 4), :]
                    for e in range(E):
                        b2 = f.b2[:, e:e + 1, :]
                        alone(pool, m)
                        link(pool.tensor_tensor(bias[:, e % 2, :, :], gate[:, bass.ds(4 * i, 4), e].to_broadcast([P, 4, C]),
                                                bass.AP(b2.tensor, b2.offset, [b2.ap[0], [0, 4], [1, C]]), ALU.mult))
                        alone(pool, m)
                        link(pool.tensor_tensor(tok, tok, bias[:, e % 2, :, :], ALU.add))
                    pool.sem_inc(s_bt, 1)

            @block.tensor
            def _(pe):
                for s in (s_T, s_gt, s_Y, s_OT):
                    pe.sem_inc(s, 1)
                with pe.Fori(0, PAIRS) as i:
                    pe.wait_ge(s_xn, i + 1)
                    pe.wait_ge(s_xT, i + 1)
                    for t in range(4):
                        ins = nc.tensor.transpose(ps[0:C, 0, P * t:P * (t + 1)], xn[:, t, :], m.ident[:, :])
                    ins.then_inc(s_T, 1)
                    pe.wait_ge(s_xT, i + 1 + 1)
                    pe.wait_ge(s_gc, i + 1)
                    nc.tensor.matmul(ps[0:E, 1, :], f.gate[:, :], m.chan[:, bass.ds(Q * i, Q)], start=True, stop=True).then_inc(s_g, 1)
                    pe.wait_ge(s_gc, i + 1 + 1)
                    pe.wait_ge(s_sc, i + 1)
                    alone(pe, m)
                    for t in range(4):
                        ins = nc.tensor.transpose(ps[:, 2, E * t:E * (t + 1)], gs[:, 0, P * t:P * (t + 1)], m.ident[0:E, 0:E])
                    ins.then_inc(s_gt, 1)

                def hidden(i, e):
                    for j in range(HC):
                        k = 3 * (e % 2) + j
                        if e >= 2:
                            pe.wait_ge(s_h, i * (E * HC) + ((e - 2) * HC + j + 1) + 1)
                        elif j == 0:
                            pe.wait_ge(s_h, i * (E * HC) + 1)
                        nc.tensor.matmul(ps[:, k, :], f.w1[:, e, P * j:P * (j + 1)], m.chan[0:C, bass.ds(Q * i, Q)],
                                         start=True, stop=True).then_inc(s_F, 1)

                def result(i, e):
                    pe.wait_ge(s_h, i * (E * HC) + (e + 1) * HC + 1)
                    if e >= 2:
                        pe.wait_ge(s_ac, i * E + (e - 1) + 1)
                    else:
                        pe.wait_ge(s_ac, i * E + 1)
                    for t in range(4):
                        for j in range(HC):
                            ins = nc.tensor.matmul(ps[:, 6 + e % 2, C * t:C * (t + 1)], h[:, e % 2, j, P * t:P * (t + 1)],
                                                   f.w2[:, e * HC + j, :], start=(j == 0), stop=(j == HC - 1))
                    ins.then_inc(s_Y, 1)

                pe.wait_ge(s_xT, PAIRS + 1)
                pe.wait_ge(s_gc, PAIRS + 1)
                pe.wait_ge(s_sc, PAIRS + 1)
                with pe.Fori(0, PAIRS) as i:
                    if last:
                        pe.wait_ge(s_oc, i + 1)
                    hidden(i, 0)
                    hidden(i, 1)
                    result(i, 0)
                    hidden(i, 2)
                    result(i, 1)
                    hidden(i, 3)
                    result(i, 2)
                    result(i, 3)
                    if last:
                        pe.wait_ge(s_ac, i * E + E + 1)
                        for t in range(4):
                            ins = nc.tensor.transpose(ps[0:C, 0, P * t:P * (t + 1)], fin[:, t, :], m.ident[:, :])
                        ins.then_inc(s_OT, 1)

            @block.scalar
            def _(act):
                for s in (s_gc, s_h, s_oc):
                    act.sem_inc(s, 1)
                nc.scalar.preload_act_table(ACT.Exp)
                with act.Fori(0, PAIRS) as i:
                    act.wait_ge(s_g, i + 1)
                    act.wait_ge(s_gt, i + 1)
                    nc.scalar.copy(gs[:, 0, :], ps[0:E, 1, :]).then_inc(s_gc, 1)
                act.wait_ge(s_nm, 1)
                nc.scalar.activation(pr[:, :, :], sc[:, :, :], ACT.Exp).then_inc(s_ex, 1)
                nc.scalar.preload_act_table(ACT.Gelu)
                with act.Fori(0, PAIRS) as i:
                    for e in range(E):
                        for j in range(HC):
                            act.wait_ge(s_F, i * (E * HC) + (e * HC + j + 1))
                            if j == 0:
                                act.wait_ge(s_Y, i * E + (e - 1) + 1) if e >= 2 else act.wait_ge(s_Y, i * E + 1)
                            nc.scalar.activation(h[:, e % 2, j, :], ps[:, 3 * (e % 2) + j, :], ACT.Gelu,
                                                 bias=f.b1[:, e * HC + j:e * HC + j + 1]).then_inc(s_h, 1)
                    if last:
                        act.wait_ge(s_OT, i + 1 + 1)
                        nc.scalar.copy(fT[:, 0, :], ps[0:C, 0, :]).then_inc(s_oc, 1)
                        act.wait_ge(s_oc, i + 1 + 1)
                        act.dma_start(out.rearrange("b c h w -> c b (h w)")[:, bass.ds(2 * i, 2), :],
                                      fT[:, 0, :].rearrange("c (b n) -> c b n", n=N)).then_inc(s_store[0], 16)
                        act.wait_ge(s_store[0], i * 16 + 16)

            @block.vector
            def _(dve):
                for s in (s_xT, s_sc, s_ac):
                    dve.sem_inc(s, 1)
                with dve.Fori(0, PAIRS) as i:
                    dve.wait_ge(s_T, i + 1 + 1)
                    nc.vector.tensor_copy(m.chan[0:C, bass.ds(Q * i, Q)], ps[0:C, 0, :]).then_inc(s_xT, 1)
                    dve.wait_ge(s_gt, i + 1 + 1)
                    nc.vector.tensor_copy(sc[:, bass.ds(4 * i, 4), :], ps[:, 2, 0:4 * E].rearrange("p (t e) -> p t e", e=E)).then_inc(s_sc, 1)
                dve.wait_ge(s_sc, PAIRS + 1)
                link = Link(dve, s_gd)
                link(nc.vector.tensor_reduce(one[:, 0, :], sc[:, :, :], AX.X, ALU.max))
                nc.vector.tensor_tensor(sc[:, :, :], sc[:, :, :], one[:, 0, :].to_broadcast([P, NT, E]), ALU.subtract).then_inc(s_nm, 1)
                dve.wait_ge(s_ex, 1)
                link(nc.vector.tensor_reduce(one[:, 1, :], pr[:, :, :], AX.X, ALU.add))
                link(nc.vector.reciprocal(one[:, 2, :], one[:, 1, :]))
                link(nc.vector.tensor_tensor(pr[:, :, :], pr[:, :, :], one[:, 2, :].to_broadcast([P, NT, E]), ALU.mult))
                own = pr[:, :, :].to_broadcast([P, NT, E, E])
                other = bass.AP(pr[:, :, :].tensor, pr[:, :, :].offset, [pr[:, :, :].ap[0], [E, NT], [0, E], [1, E]])
                before = m.before[:, 0, :, :].rearrange("p a b -> p (a b)")
                link(nc.vector.tensor_tensor(eq[:, :, :, :], other, own, ALU.is_equal))
                link(nc.vector.tensor_tensor(eq[:, :, :, :].rearrange("p t a b -> p t (a b)"), eq[:, :, :, :].rearrange("p t a b -> p t (a b)"),
                                             bass.AP(before.tensor, before.offset, [before.ap[0], [0, NT], [1, E * E]]), ALU.mult))
                link(nc.vector.tensor_tensor(gt[:, :, :, :], other, own, ALU.is_gt))
                link(nc.vector.tensor_tensor(gt[:, :, :, :], gt[:, :, :, :], eq[:, :, :, :], ALU.add))
                link(nc.vector.tensor_reduce(gate[:, :, :], gt[:, :, :, :], AX.X, ALU.add))
                link(nc.vector.scalar_tensor_tensor(gate[:, :, :], gate[:, :, :], 1.5, pr[:, :, :], ALU.is_lt, ALU.mult))
                link(nc.vector.tensor_reduce(one[:, 0, :], gate[:, :, :], AX.X, ALU.add))
                link(nc.vector.tensor_scalar(one[:, 1, :], one[:, 0, :], 1e-9, None, ALU.add))
                link(nc.vector.reciprocal(one[:, 2, :], one[:, 1, :]))
                link(nc.vector.tensor_tensor(gate[:, :, :], gate[:, :, :], one[:, 2, :].to_broadcast([P, NT, E]), ALU.mult))
                assert link.n == GATE_STEPS
                with dve.Fori(0, PAIRS) as i:
                    dve.wait_ge(s_bt, i + 1)
                    if last:
                        dve.wait_ge(s_OT, i + 1)
                    for e in range(E):
                        dve.wait_ge(s_Y, i * E + (e + 1) + 1)
                        if e:
                            dve.wait_ge(s_ac, i * E + e + 1)
                        for t in range(4):
                            tok = m.tok[:, bass.ds(4 * i + t, 1), :].rearrange("p t c -> p (t c)")
                            dst = fin[:, t, :] if last and e == E - 1 else tok
                            ins = nc.vector.scalar_tensor_tensor(
                                dst, ps[:, 6 + e % 2, C * t:C * (t + 1)],
                                gate[:, bass.ds(4 * i + t, 1), e], tok, ALU.mult, ALU.add)
                        ins.then_inc(s_ac, 1)
                    if not last:
                        dve.wait_ge(s_ac, i * E + E + 1)
                        statistics(nc, m, dve, i, st, mv, s_st, s_mv)
                if not last:
                    dve.wait_ge(s_mv, PAIRS)


GATE_STEPS = 14


def program(nc, a, out):
    with ExitStack() as ctx:
        m = buffers(nc, ctx)

        def sem(name):
            return ctx.enter_context(nc.semaphore(name))
        setup(nc, m, a, sem)
        channel_attention(nc, m, sem)
        large_conv(nc, m, sem)
        token_attention(nc, m, sem, 2, [m.wT[0:C, M_QKV2 + t, :] for t in range(3)], m.wT[:, M_PROJ2, :])
        experts(nc, m, sem, 2, m.ffn[0])
        token_attention(nc, m, sem, 3, [m.qkv3[:, C * t:C * (t + 1)] for t in range(3)], m.proj3[:, :])
        experts(nc, m, sem, 3, m.ffn[1], out)


def kernel(**inputs):
    import numpy as np
    import concourse.bacc as bacc
    from concourse.bass_utils import run_bass_kernel_spmd

    nc = bacc.Bacc("TRN2", target_bir_lowering=False, num_devices=1)
    arrays, a = {}, {}
    for name in INS:
        arrays[f"in_{name}"] = np.ascontiguousarray(inputs[name])
        a[name] = nc.dram_tensor(f"in_{name}", arrays[f"in_{name}"].shape, F32, kind="ExternalInput").ap()
    out = nc.dram_tensor("out", (B, C, HH, WW), F32, kind="ExternalOutput").ap()
    program(nc, a, out)
    return run_bass_kernel_spmd(nc, [arrays], core_ids=[0]).results[0]["out"]
```

```python
from contextlib import ExitStack

import concourse.bass as bass
from concourse import mybir

F32 = mybir.dt.float32
BF16 = mybir.dt.bfloat16
F32R = mybir.dt.float32r
ALU = mybir.AluOpType
ACT = mybir.ActivationFunctionType
AX = mybir.AxisListType

P = 128
B, C, HH, WW = 16, 96, 16, 16
N = HH * WW
T = B * N
NT = T // P
TPI = N // P
PAIRS = B // 2
GN_CH = 3
CA_H, CA_D = 8, 12
H, D = 6, 16
VD = D + 1
MAX_ROWS = 3 * H
OW = H * VD
Q = 4 * P
E, HID = 4, 384
HC = HID // P
KW = 13
R = KW // 2
CG = P // WW
G = C // CG
WIN = WW * KW
LEAD = WW - 1 - R
LINE = (2 * WW - 1) * KW
MASKED = -1.0e30

INS = ['x', 'L0_conv_w_qkv', 'L0_conv_w_dw', 'L0_conv_w_proj', 'L0_conv_temperature', 'L1_conv_pw_w', 'L1_conv_pw_g',
       'L1_conv_pw_b', 'L1_conv_pw_m', 'L1_conv_pw_v', 'L1_conv_dwk_w', 'L1_conv_dwk_g', 'L1_conv_dwk_b',
       'L1_conv_dwk_m', 'L1_conv_dwk_v', 'L1_conv_dw1_w', 'L1_conv_dw1_g', 'L1_conv_dw1_b', 'L1_conv_dw1_m',
       'L1_conv_dw1_v', 'L2_attn_qkv_w', 'L2_attn_proj_w', 'L2_attn_proj_b', 'L2_attn_temperature', 'L2_ffn_gate_w',
       'L2_ffn_gate_b', 'L2_ffn_w1', 'L2_ffn_b1', 'L2_ffn_w2', 'L2_ffn_b2', 'L3_attn_w_qkv', 'L3_attn_w_proj',
       'L3_attn_b_proj', 'L3_ffn_gate_w', 'L3_ffn_gate_b', 'L3_ffn_w1', 'L3_ffn_b1', 'L3_ffn_w2', 'L3_ffn_b2']

VECTORS = ['L1_conv_pw_v', 'L1_conv_dwk_v', 'L1_conv_dw1_v', 'L1_conv_pw_g', 'L1_conv_dwk_g', 'L1_conv_dw1_g',
           'L1_conv_pw_b', 'L1_conv_dwk_b', 'L1_conv_dw1_b', 'L1_conv_pw_m', 'L1_conv_dwk_m', 'L1_conv_dw1_m',
           'L1_conv_dw1_w', 'L2_attn_proj_b']
V_VAR, V_G, V_B, V_M, V_DW1, V_PROJ, V_T0, V_T2 = 0, 3, 6, 9, 12, 13, 14, 15
NV = 16
M_QK0, M_V0, M_PROJ0, M_PW, M_QKV2, M_PROJ2 = 0, 2, 11, 12, 13, 16
NM = 17
SLOTS = 3
TAPS = [(0, 0)] + [(dy, dx) for dy in (-1, 0, 1) for dx in (-1, 0, 1) if dy or dx]


class Names:
    pass


class Link:

    def __init__(self, eng, sem, base=0):
        self.eng, self.sem, self.base, self.n = eng, sem, base, 0

    def __call__(self, ins):
        self.n += 1
        ins.then_inc(self.sem, 1)
        self.eng.wait_ge(self.sem, self.base + self.n)


def alone(eng, m):
    eng.sem_inc(m.s_waited, 1)


def buffers(nc, ctx):
    def sb(name, shape, dt=F32):
        return ctx.enter_context(nc.sbuf_tensor(name, shape, dt))

    m = Names()
    m.ps = ctx.enter_context(nc.psum_tensor("ps", [P, 8, 512], F32))
    m.ident = sb("ident", [P, P])
    m.ident_b = sb("ident_b", [P, P], BF16)
    m.diag_b = sb("diag_b", [P, P], BF16)
    m.later_b = sb("later_b", [P, P], BF16)
    m.earlier_b = sb("earlier_b", [P, P], BF16)
    m.heads_b = sb("heads_b", [C, C], BF16)
    m.groups = sb("groups", [C, C])
    m.before = sb("before", [P, 4, E, E])
    m.power = sb("power", [P, 32])
    m.tok = sb("tok", [P, NT, C])
    m.mv = sb("mv", [P, NT, 2])
    m.var = sb("var", [P, NT])
    m.eps = sb("eps", [P, 4])
    m.rstd = sb("rstd", [P, NT])
    m.ks = sb("keys", [C + MAX_ROWS, 2, H, 2, N], BF16)
    m.vp = sb("values", [P, 2, 2, TPI, H, OW])
    m.mxp = sb("maxima", [P, 2, TPI, C + MAX_ROWS], BF16)
    m.oT = sb("outT", [C + 1, 2, N])
    m.vec = sb("vec", [C, NV])
    m.bn = sb("bn", [C, 2, 3])
    m.wT = sb("wT", [C + 1, NM, C])
    m.dw0 = sb("dw0", [C, 3, 9])
    m.qkv3 = sb("qkv3", [C, 3 * C])
    m.proj3 = sb("proj3", [C + 1, C])
    m.ffn = []
    for l in (2, 3):
        f = Names()
        f.gate = sb(f"gate{l}", [C + 1, E])
        f.w1 = sb(f"w1_{l}", [C, E, HID])
        f.b1rows = sb(f"b1rows{l}", [E * HC, P])
        f.b1 = sb(f"b1_{l}", [P, E * HC])
        f.w2 = sb(f"w2_{l}", [P, E * HC, C])
        f.b2 = sb(f"b2_{l}", [P, E, C])
        m.ffn.append(f)
    return m


def early_buffers(nc, m, ctx):
    def sb(name, shape, dt=F32):
        return ctx.enter_context(nc.sbuf_tensor(name, shape, dt))

    m.x1 = sb("x1", [C + 1, T])
    m.chan = sb("chan", [C, T])
    m.x = m.chan[:, :].rearrange("c (b n) -> c b n", n=N)
    m.vecrows = sb("vecrows", [NV, C])
    m.raw = sb("raw", [C, NM, C + 1])
    m.rawv = sb("rawv", [C, C])
    m.dwk = sb("dwk", [C, KW * KW])
    m.lines = sb("lines", [C, LINE])
    m.win = sb("windows", [P, SLOTS, CG, WIN])
    m.cb = sb("conv_bias", [P, G])
    m.lines_d = nc.dram_tensor("lines_d", [C, LINE], F32, kind="Internal").ap()
    m.bias_d = nc.dram_tensor("bias_d", [C, 1], F32, kind="Internal").ap()


def load_windows(sp, m, s_win, g, k):
    for c in range(CG):
        sp.dma_start(m.win[WW * c:WW * (c + 1), k, c, :],
                     bass.AP(m.lines_d.tensor, g * (CG * LINE) + c * LINE, [[KW, WW], [1, WIN]])).then_inc(s_win, 16)


def channel_attention(nc, m, a, sem):
    s_x = [sem(f"in_x{k}") for k in range(4)]
    s_w0, s_vec, s_mat, s_b1, s_dwk, s_rest = (sem(f"in_{n}") for n in (
        "weights0", "vectors", "matrices", "b1", "dwk", "rest"))
    m.s_waited = sem("waited")
    s_const, s_pool, s_vecT, s_vecS, s_rstd = (sem(n) for n in ("constants", "pool_own", "vectors_turned", "vectors_kept", "bn_rstd"))
    s_dve, s_taps, s_fold, s_wps, s_wT, s_zero = (sem(n) for n in (
        "setup_dve", "v_taps", "folded", "weights_turned", "weights_kept", "windows_zeroed"))
    s_lines, s_bias = sem("lines_stored"), sem("conv_bias")
    s_win = [sem(f"windows{k}") for k in range(SLOTS)]
    s_st, s_gm, s_gdve, s_grs, s_shift = (sem(n) for n in ("gn_means", "gn_psum", "gn_dve", "gn_rstd", "gn_shift"))
    s_tap = [sem(f"ca_tap{t}") for t in range(2)]
    (s_xn, s_qk, s_raw, s_v, s_vc, s_ss, s_rn, s_kn, s_T, s_trs, s_sc, s_mx, s_nm, s_ex, s_rc, s_at, s_ap, s_aps, s_out, s_x1) = (
        sem(f"ca_{n}") for n in ("normed", "qk", "qk_kept", "v", "v_kept", "squares", "norms", "k_scaled", "turned", "turned_kept",
                                 "scores", "max", "shift", "exp", "recip", "attn", "attnproj", "attnproj_kept", "out", "x1"))
    n_vec = len(VECTORS) + 2
    ps = m.ps
    with ExitStack() as ctx:
        def sb(name, shape, dt=F32):
            return ctx.enter_context(nc.sbuf_tensor(name, shape, dt))
        st = sb("gn_stats", [C, B, 6])
        mv = sb("gn_mv", [C, B, 2])
        gm = sb("gn_gm", [C, 4, B])
        shift = sb("gn_shift", [C, B])
        xn = sb("ca_xn", [C, 2, N])
        raw = sb("ca_raw", [C, 2, 2, N])
        qkc = sb("ca_qk", [C, 2, 2, N])
        vc = sb("ca_v", [C, 2, N])
        sq = sb("ca_sq", [C, 2, N])
        ss = sb("ca_ss", [C, 2, 2])
        rn = sb("ca_rn", [C, 2, 3])
        kn = sb("ca_kn", [C, N])
        qkT = sb("ca_qkT", [P, 4, C])
        nm = sb("ca_nm", [C, 2])
        rs = sb("ca_rs", [C, 2])
        at = sb("ca_at", [C, 2, C])
        apT = sb("ca_apT", [C, C])

        def steps(eng, step):
            step(0, 0, False, True)
            with eng.Fori(0, B // 2 - 1) as j:
                step(2 * j + 1, 1, True, True)
                step(2 * j + 2, 0, True, True)
            step(B - 1, 1, True, False)

        with nc.Block() as block:

            @block.sync
            def _(sp):
                for k in range(4):
                    sp.dma_start(m.x[:, 4 * k:4 * k + 4, :], a['x'].rearrange("b c h w -> c b (h w)")[:, 4 * k:4 * k + 4, :]).then_inc(s_x[k], 16)
                    if k == 0:
                        sp.dma_start(m.raw[:, M_QK0:M_QK0 + 2, 0:C], a['L0_conv_w_qkv'][0:2 * C, :].rearrange("(t o) c -> o t c", t=2)).then_inc(s_w0, 16)
                        sp.dma_start(m.rawv[:, :], a['L0_conv_w_qkv'][2 * C:3 * C, :]).then_inc(s_w0, 16)
                        sp.dma_start(m.dw0[:, :, :], a['L0_conv_w_dw'].rearrange("(t o) i h w -> o t (i h w)", t=3)).then_inc(s_w0, 16)
                        sp.dma_start(m.raw[:, M_PROJ0, 0:C], a['L0_conv_w_proj']).then_inc(s_w0, 16)
                for r, name in enumerate(VECTORS):
                    sp.dma_start(m.vecrows[r:r + 1, :], a[name].rearrange("(o n) -> o n", o=1)).then_inc(s_vec, 16)
                for r, (name, heads) in ((V_T0, ('L0_conv_temperature', CA_H)), (V_T2, ('L2_attn_temperature', H))):
                    sp.dma_start(m.vecrows[r:r + 1, :].rearrange("o (h d e) -> o h d e", h=heads, e=1),
                                 bass.AP(a[name].tensor, 0, [[0, 1], [1, heads], [0, C // heads], [1, 1]])).then_inc(s_vec, 16)
                sp.dma_start(m.dwk[:, :], a['L1_conv_dwk_w'].rearrange("c i h w -> c (i h w)")).then_inc(s_dwk, 16)
                sp.dma_start(m.raw[:, M_PW, 0:C], a['L1_conv_pw_w']).then_inc(s_mat, 16)
                sp.dma_start(m.raw[:, M_QKV2:M_QKV2 + 3, 0:C], a['L2_attn_qkv_w'].rearrange("(t o) c -> o t c", t=3)).then_inc(s_mat, 16)
                sp.dma_start(m.raw[:, M_PROJ2, 0:C], a['L2_attn_proj_w']).then_inc(s_mat, 16)
                for l, f in zip((2, 3), m.ffn):
                    sp.dma_start(f.b1rows[:, :], a[f'L{l}_ffn_b1'].rearrange("e (j p) -> (e j) p", p=P)).then_inc(s_b1, 16)
                sp.wait_ge(s_fold, 2)
                sp.dma_start(m.lines_d, m.lines[:, :]).then_inc(s_lines, 16)
                sp.dma_start(m.bias_d, m.bn[:, 1, 1:2]).then_inc(s_lines, 16)
                sp.dma_start(m.qkv3[:, :], a['L3_attn_w_qkv']).then_inc(s_rest, 16)
                sp.dma_start(m.proj3[0:C, :], a['L3_attn_w_proj']).then_inc(s_rest, 16)
                sp.dma_start(m.proj3[C:C + 1, :], a['L3_attn_b_proj'].rearrange("(o n) -> o n", o=1)).then_inc(s_rest, 16)
                for l, f in zip((2, 3), m.ffn):
                    sp.dma_start(f.gate[0:C, :], a[f'L{l}_ffn_gate_w']).then_inc(s_rest, 16)
                    sp.dma_start(f.gate[C:C + 1, :], a[f'L{l}_ffn_gate_b'].rearrange("(o n) -> o n", o=1)).then_inc(s_rest, 16)
                    sp.dma_start(f.w1[:, :, :], a[f'L{l}_ffn_w1'].rearrange("e d h -> d e h")).then_inc(s_rest, 16)
                    sp.dma_start(f.w2[:, :, :], a[f'L{l}_ffn_w2'].rearrange("e (j p) d -> p (e j) d", p=P)).then_inc(s_rest, 16)
                    sp.dma_start(f.b2[:, :, :], bass.AP(a[f'L{l}_ffn_b2'].tensor, 0, [[0, P], [C, E], [1, C]])).then_inc(s_rest, 16)
                sp.wait_ge(s_lines, 32)
                for c in range(CG):
                    sp.dma_start(m.cb[WW * c:WW * (c + 1), :], bass.AP(m.bias_d.tensor, c, [[0, WW], [CG, G]]),
                                 allow_slow_non_contiguous=True).then_inc(s_bias, 16)
                sp.wait_ge(s_zero, 1)
                for k in range(SLOTS):
                    load_windows(sp, m, s_win[k], k, k)
                sp.wait_ge(s_bias, 16 * CG)

            @block.gpsimd
            def _(pool):
                link = Link(pool, s_pool)
                link(pool.memset(m.ident[:, :], 1.0))
                link(pool.affine_select(out=m.ident[:, :], in_=m.ident[:, :], compare_op=ALU.is_equal, fill=0.0, base=0,
                                        pattern=[[-1, P]], channel_multiplier=1))
                pool.memset(m.power[:, :], -0.5)
                pool.memset(m.eps[:, :], 1e-5)
                link(pool.tensor_copy(m.ident_b[:, :], m.ident[:, :]))

                def blocks_of(tile, blocks, d, fill):
                    v = tile[:, :].rearrange("p (g d) -> p g d", d=d)
                    link(pool.memset(tile[:, :], 0.0 if fill else 1.0))
                    link(pool.affine_select(out=v, in_=v, compare_op=ALU.is_ge, fill=fill, base=0,
                                            pattern=[[-d, blocks], [0, d]], channel_multiplier=1))
                    link(pool.affine_select(out=v, in_=v, compare_op=ALU.is_ge, fill=fill, base=d - 1,
                                            pattern=[[d, blocks], [0, d]], channel_multiplier=-1))
                blocks_of(m.groups, C // GN_CH, GN_CH, 0.0)
                blocks_of(m.heads_b, CA_H, CA_D, MASKED)
                nc.gpsimd.sem_inc(s_const, 1)
                pool.wait_ge(s_gdve, 5)
                link(pool.tensor_scalar(gm[:, 3, :], gm[:, 3, :], 1e-5, 0.0, ALU.add, ALU.add))
                pool.tensor_tensor(gm[:, 1, :], gm[:, 3, :], m.power[0:C, 0:B], ALU.pow).then_inc(s_grs, 1)
                pool.wait_ge(s_vecS, 1)
                link(pool.tensor_scalar(m.bn[:, 0, :], m.vec[:, V_VAR:V_VAR + 3], 1e-5, 0.0, ALU.add, ALU.add))
                pool.tensor_tensor(m.bn[:, 1, :], m.bn[:, 0, :], m.power[0:C, 0:3], ALU.pow).then_inc(s_rstd, 1)

                def step(b, slot, back, front):
                    if back:
                        norms(b - 1, 1 - slot)

                def norms(c, slot):
                    pool.wait_ge(s_ss, 2 * c + 3)
                    alone(pool, m)
                    pool.tensor_scalar(rn[:, slot, 0:2], ss[:, slot, :], 1e-24, 1e-24, ALU.max, ALU.max).then_inc(s_rn, 1)
                    pool.wait_ge(s_rn, 3 * c + 1)
                    pool.tensor_tensor(rn[:, slot, 0:2], rn[:, slot, 0:2], m.power[0:C, 0:2], ALU.pow).then_inc(s_rn, 1)
                    pool.wait_ge(s_rn, 3 * c + 2)
                    pool.tensor_tensor(rn[:, slot, 2:3], rn[:, slot, 1:2], m.vec[:, V_T0:V_T0 + 1], ALU.mult).then_inc(s_rn, 1)

                pool.memset(m.win[:, :, :, :], 0.0).then_inc(s_zero, 1)
                steps(pool, step)
                norms(B - 1, 1)
                link(pool.memset(m.diag_b[:, :], 0.0))
                link(pool.affine_select(out=m.diag_b[:, :], in_=m.diag_b[:, :], compare_op=ALU.not_equal, fill=MASKED,
                                        base=0, pattern=[[-1, P]], channel_multiplier=1))
                for tile, sign in ((m.later_b, -1), (m.earlier_b, 1)):
                    link(pool.memset(tile[:, :], 0.0))
                    link(pool.affine_select(out=tile[:, :], in_=tile[:, :], compare_op=ALU.is_ge, fill=MASKED,
                                            base=0, pattern=[[sign, P]], channel_multiplier=-sign))
                link(pool.memset(m.before[:, :, :, :], 1.0))
                link(pool.affine_select(out=m.before[:, :, :, :], in_=m.before[:, :, :, :], compare_op=ALU.is_gt, fill=0.0,
                                        base=0, pattern=[[0, 4], [1, E], [-1, E]], channel_multiplier=0))
                link(pool.memset(m.x1[C:C + 1, :], 1.0))

            @block.tensor
            def _(pe):
                for s in (s_T, s_sc, s_ap, s_out):
                    pe.sem_inc(s, 1)
                pe.wait_ge(s_const, 1)

                def turn_weights(first, count, bank):
                    for k in range(count):
                        ins = nc.tensor.transpose(ps[0:C + 1, bank, C * k:C * (k + 1)], m.raw[:, first + k, :], m.ident[0:C, 0:C])
                    ins.then_inc(s_wps, 1)
                pe.wait_ge(s_gdve, 1)
                nc.tensor.matmul(ps[0:C, 6, 0:B], m.groups[:, :], gm[:, 0, :], start=True, stop=True).then_inc(s_gm, 1)
                pe.wait_ge(s_taps, 9)
                pe.wait_ge(s_w0, 64)
                turn_weights(0, 5, 2)
                turn_weights(5, 5, 3)
                turn_weights(10, 2, 4)
                pe.wait_ge(s_gdve, 4)
                nc.tensor.matmul(ps[0:C, 7, 0:B], m.groups[:, :], gm[:, 3, :], start=True, stop=True).then_inc(s_gm, 1)
                pe.wait_ge(s_vec, 16 * n_vec)
                nc.tensor.transpose(ps[0:C, 0, 0:NV], m.vecrows[:, :], m.ident[0:NV, 0:NV]).then_inc(s_vecT, 1)
                pe.wait_ge(s_b1, 32)
                for k, f in enumerate(m.ffn):
                    nc.tensor.transpose(ps[:, 1, 16 * k:16 * k + E * HC], f.b1rows[:, :],
                                        m.ident[0:E * HC, 0:E * HC]).then_inc(s_vecT, 1)
                pe.wait_ge(s_fold, 2)
                turn_weights(M_PW, 5, 5)
                pe.wait_ge(s_wT, 6)

                def queries_keys(b, slot):
                    pe.wait_ge(s_xn, b + 1)
                    for t in range(2):
                        ins = nc.tensor.matmul(ps[0:C, slot, N * t:N * (t + 1)], m.wT[0:C, M_QK0 + t, :], xn[:, slot, :],
                                               start=True, stop=True)
                    ins.then_inc(s_qk, 1)

                def value_taps(slot, first, last):
                    x = xn[:, slot, :].rearrange("p (y x) -> p y x", x=WW)
                    dst = ps[0:C, 2 + slot, 0:N].rearrange("p (y x) -> p y x", x=WW)
                    for n in range(first, last):
                        dy, dx = TAPS[n]
                        y0, y1, x0, x1 = max(0, -dy), HH - max(0, dy), max(0, -dx), WW - max(0, dx)
                        ins = nc.tensor.matmul(dst[:, y0:y1, x0:x1], m.wT[0:C, M_V0 + 3 * (dy + 1) + dx + 1, :],
                                               x[:, y0 + dy:y1 + dy, x0 + dx:x1 + dx], start=(n == 0), stop=(n == len(TAPS) - 1))
                    return ins

                def step(b, slot, back, front):
                    c, other = b - 1, 1 - slot
                    if front:
                        if back:
                            pe.wait_ge(s_raw, b)
                        queries_keys(b + 1, other)
                        if back:
                            pe.wait_ge(s_vc, b)
                        value_taps(other, 0, 3)
                    if back:
                        turn(c, other)
                    if front:
                        value_taps(other, 3, 4)
                    if back:
                        scores(c)
                    if front:
                        value_taps(other, 4, 9).then_inc(s_v, 1)
                    if back:
                        result(c, other)

                def turn(c, slot):
                    pe.wait_ge(s_kn, c + 1)
                    pe.wait_ge(s_trs, c + 1)
                    for t, src in enumerate((qkc[:, slot, 0, :], kn[:, :])):
                        for h in range(2):
                            ins = nc.tensor.transpose(ps[:, 4, C * (2 * t + h):C * (2 * t + h + 1)], src[:, P * h:P * (h + 1)],
                                                      m.ident[0:C, 0:C])
                    ins.then_inc(s_T, 1)

                def scores(c):
                    pe.wait_ge(s_trs, c + 2)
                    pe.wait_ge(s_ex, c + 1)
                    for h in range(2):
                        nc.tensor.matmul(ps[0:C, 5, 0:C], qkT[:, h, :], qkT[:, 2 + h, :], start=(h == 0), stop=False)
                    nc.tensor.matmul(ps[0:C, 5, 0:C], m.ident_b[0:C, 0:C], m.heads_b[:, :], start=False, stop=True).then_inc(s_sc, 1)

                def result(c, slot):
                    pe.wait_ge(s_at, c + 1)
                    pe.wait_ge(s_aps, c + 1)
                    nc.tensor.matmul(ps[0:C, 6, 0:C], at[:, 1, :], m.wT[0:C, M_PROJ0, :], start=True, stop=True).then_inc(s_ap, 1)
                    pe.wait_ge(s_aps, c + 2)
                    pe.wait_ge(s_vc, c + 1)
                    pe.wait_ge(s_x1, c + 1)
                    nc.tensor.matmul(ps[0:C, 7, 0:N], apT[:, :], vc[:, slot, :], start=True, stop=True).then_inc(s_out, 1)

                queries_keys(0, 0)
                value_taps(0, 0, 9).then_inc(s_v, 1)
                steps(pe, step)
                turn(B - 1, 1)
                scores(B - 1)
                result(B - 1, 1)

            @block.scalar
            def _(act):
                for s in (s_ss, s_trs, s_ex, s_aps):
                    act.sem_inc(s, 1)
                nc.scalar.preload_act_table(ACT.Exp)

                def normed(b, slot):
                    nc.scalar.activation(xn[:, slot, :], m.x[:, bass.ds(b, 1), :].rearrange("p b n -> p (b n)"), ACT.Identity,
                                         bias=shift[:, bass.ds(b, 1)], scale=gm[:, 1, bass.ds(b, 1)]).then_inc(s_xn, 1)

                def keep(b, slot):
                    act.wait_ge(s_qk, b + 1)
                    nc.scalar.copy(raw[:, slot, :, :].rearrange("p t n -> p (t n)"), ps[0:C, slot, :]).then_inc(s_raw, 1)

                def squares(c, slot):
                    for t in range(2):
                        act.wait_ge(s_tap[t], 9 * c + 9)
                        act.wait_ge(s_ss, 2 * c + 1 + t)
                        nc.scalar.activation(sq[:, t, :], qkc[:, slot, t, :], ACT.Square, accum_out=ss[:, slot, t:t + 1]).then_inc(s_ss, 1)

                def keep_v(b, slot):
                    act.wait_ge(s_v, b + 1)
                    nc.scalar.copy(vc[:, slot, :], ps[0:C, 2 + slot, 0:N]).then_inc(s_vc, 1)

                def scale_k(c, slot):
                    act.wait_ge(s_rn, 3 * c + 3)
                    act.wait_ge(s_T, c + 1)
                    nc.scalar.activation(kn[:, :], qkc[:, slot, 1, :], ACT.Copy, scale=rn[:, slot, 2:3]).then_inc(s_kn, 1)

                def keep_turned(c):
                    act.wait_ge(s_T, c + 2)
                    act.wait_ge(s_sc, c + 1)
                    nc.scalar.copy(qkT[:, :, :].rearrange("p k c -> p (k c)"), ps[:, 4, 0:4 * C]).then_inc(s_trs, 1)

                def exponential(c, slot):
                    act.wait_ge(s_nm, c + 1)
                    nc.scalar.activation(at[:, 0, :], ps[0:C, 5, 0:C], ACT.Exp, bias=nm[:, 1:2], scale=rn[:, slot, 0:1],
                                         accum_out=rs[:, 0:1]).then_inc(s_ex, 1)

                def keep_product(c):
                    act.wait_ge(s_ap, c + 2)
                    act.wait_ge(s_out, c + 1)
                    nc.scalar.copy(apT[:, :], ps[0:C, 6, 0:C]).then_inc(s_aps, 1)

                def step(b, slot, back, front):
                    c, other = b - 1, 1 - slot
                    if front:
                        if back:
                            act.wait_ge(s_v, b)
                        normed(b + 1, other)
                    if back:
                        squares(c, other)
                        act.wait_ge(s_out, b)
                    keep_v(b, slot)
                    if back:
                        scale_k(c, other)
                    if front:
                        if back:
                            for t in range(2):
                                act.wait_ge(s_tap[t], 9 * b)
                        keep(b + 1, other)
                    if back:
                        keep_turned(c)
                    if back:
                        exponential(c, other)
                        keep_product(c)

                act.wait_ge(s_grs, 1)
                act.wait_ge(s_shift, 1)
                normed(0, 0)
                keep(0, 0)
                steps(act, step)
                squares(B - 1, 1)
                scale_k(B - 1, 1)
                keep_turned(B - 1)
                exponential(B - 1, 1)
                keep_product(B - 1)

            @block.vector
            def _(dve):
                dve.sem_inc(s_x1, 1)
                link = Link(dve, s_dve)
                for b in range(B):
                    if b % 4 == 0:
                        dve.wait_ge(s_x[b // 4], 16)
                    nc.vector.bn_stats(st[:, b, :], m.x[:, b, :]).then_inc(s_st, 1)
                dve.wait_ge(s_st, B)
                for b in range(B):
                    nc.vector.bn_aggr(mv[:, b, :], st[:, b, :]).then_inc(s_st, 1)
                dve.wait_ge(s_st, 2 * B)
                nc.vector.tensor_copy(gm[:, 0, :], mv[:, :, 0]).then_inc(s_gdve, 1)
                dve.wait_ge(s_w0, 64)
                link(nc.vector.memset(m.raw[:, :, C:C + 1], 0.0))
                for k in range(9):
                    nc.vector.tensor_scalar(m.raw[:, M_V0 + k, 0:C], m.rawv[:, :], m.dw0[:, 2, k:k + 1], None, ALU.mult).then_inc(s_taps, 1)
                group = Link(dve, s_gdve, 1)
                dve.wait_ge(s_gm, 1)
                group(nc.vector.tensor_scalar(gm[:, 2, :], ps[0:C, 6, 0:B], 1.0 / GN_CH, None, ALU.mult))
                group(nc.vector.tensor_tensor(gm[:, 3, :], gm[:, 0, :], gm[:, 2, :], ALU.subtract))
                nc.vector.tensor_tensor(gm[:, 1, :], gm[:, 3, :], gm[:, 3, :], ALU.mult).then_inc(s_st, 1)
                dve.wait_ge(s_st, 2 * B + 1)
                group(nc.vector.tensor_tensor(gm[:, 3, :], gm[:, 1, :], mv[:, :, 1], ALU.add))
                dve.wait_ge(s_gm, 2)
                group(nc.vector.tensor_scalar(gm[:, 3, :], ps[0:C, 7, 0:B], 1.0 / GN_CH, None, ALU.mult))
                for n, (first, count, bank) in enumerate(((0, 5, 2), (5, 5, 3), (10, 2, 4))):
                    dve.wait_ge(s_wps, n + 1)
                    nc.vector.tensor_copy(m.wT[:, first:first + count, :],
                                          ps[0:C + 1, bank, 0:count * C].rearrange("p (k c) -> p k c", c=C)).then_inc(s_wT, 1)
                dve.wait_ge(s_grs, 1)
                nc.vector.scalar_tensor_tensor(shift[:, :], gm[:, 2, :], -1.0, gm[:, 1, :], ALU.mult, ALU.mult).then_inc(s_shift, 1)
                dve.wait_ge(s_vecT, 1)
                nc.vector.tensor_copy(m.vec[:, :], ps[0:C, 0, 0:NV]).then_inc(s_vecS, 1)
                dve.wait_ge(s_vecT, 3)
                for k, f in enumerate(m.ffn):
                    nc.vector.tensor_copy(f.b1[:, :], ps[:, 1, 16 * k:16 * k + E * HC]).then_inc(s_wT, 1)
                dve.wait_ge(s_rstd, 1)
                link(nc.vector.tensor_tensor(m.bn[:, 0, :], m.bn[:, 1, :], m.vec[:, V_G:V_G + 3], ALU.mult))
                link(nc.vector.tensor_tensor(m.bn[:, 1, :], m.bn[:, 0, :], m.vec[:, V_M:V_M + 3], ALU.mult))
                link(nc.vector.tensor_tensor(m.bn[:, 1, :], m.vec[:, V_B:V_B + 3], m.bn[:, 1, :], ALU.subtract))
                dve.wait_ge(s_mat, 16 * 3)
                link(nc.vector.scalar_tensor_tensor(m.raw[:, M_PW, 0:C], m.raw[:, M_PW, 0:C], m.bn[:, 0, 0:1],
                                                    m.ident[0:C, 0:C], ALU.mult, ALU.add))
                link(nc.vector.tensor_copy(m.raw[:, M_PW, C:C + 1], m.bn[:, 1, 0:1]))
                link(nc.vector.tensor_copy(m.raw[:, M_PROJ2, C:C + 1], m.vec[:, V_PROJ:V_PROJ + 1]))
                link(nc.vector.reciprocal(m.vec[:, V_T2:V_T2 + 1], m.vec[:, V_T2:V_T2 + 1]))
                link(nc.vector.tensor_scalar(m.raw[:, M_QKV2, 0:C], m.raw[:, M_QKV2, 0:C], m.vec[:, V_T2:V_T2 + 1],
                                             float(C) ** -0.5, ALU.mult, ALU.mult))
                dve.wait_ge(s_dwk, 16)
                link(nc.vector.tensor_scalar(m.dwk[:, :], m.dwk[:, :], m.bn[:, 0, 1:2], None, ALU.mult))
                centre = R * KW + R
                link(nc.vector.scalar_tensor_tensor(m.dwk[:, centre:centre + 1], m.vec[:, V_DW1:V_DW1 + 1], m.bn[:, 0, 2:3],
                                                    m.dwk[:, centre:centre + 1], ALU.mult, ALU.add))
                link(nc.vector.memset(m.lines[:, :], 0.0))
                nc.vector.tensor_copy(m.lines[:, LEAD * KW:(LEAD + KW) * KW].rearrange("c (k j) -> c k j", j=KW),
                                      m.dwk[:, :].rearrange("c (j k) -> c k j", k=KW)).then_inc(s_fold, 1)
                nc.vector.tensor_tensor(m.bn[:, 1, 1:2], m.bn[:, 1, 1:2], m.bn[:, 1, 2:3], ALU.add).then_inc(s_fold, 1)
                dve.wait_ge(s_wps, 4)
                nc.vector.tensor_copy(m.wT[:, M_PW:NM, :], ps[0:C + 1, 5, 0:5 * C].rearrange("p (k c) -> p k c", c=C)).then_inc(s_wT, 1)

                def convolve(b, slot, first, last):
                    for n in range(first, last):
                        dy, dx = TAPS[n]
                        y0, y1, x0, x1 = max(0, -dy), HH - max(0, dy), max(0, -dx), WW - max(0, dx)
                        k = 3 * (dy + 1) + dx + 1
                        for t in range(2):
                            src = raw[:, slot, t, :].rearrange("p (y x) -> p y x", x=WW)
                            dst = qkc[:, slot, t, :].rearrange("p (y x) -> p y x", x=WW)
                            if n == 0:
                                nc.vector.tensor_scalar(dst, src, m.dw0[:, t, k:k + 1], None, ALU.mult).then_inc(s_tap[t], 1)
                                continue
                            dve.wait_ge(s_tap[t], 9 * b + n)
                            nc.vector.scalar_tensor_tensor(
                                dst[:, y0:y1, x0:x1], src[:, y0 + dy:y1 + dy, x0 + dx:x1 + dx], m.dw0[:, t, k:k + 1],
                                dst[:, y0:y1, x0:x1], ALU.mult, ALU.add).then_inc(s_tap[t], 1)

                def maximum(c, slot):
                    dve.wait_ge(s_sc, c + 2)
                    nc.vector.tensor_reduce(nm[:, 0:1], ps[0:C, 5, 0:C], AX.X, ALU.max, negate=True).then_inc(s_mx, 1)
                    dve.wait_ge(s_mx, c + 1)
                    nc.vector.tensor_tensor(nm[:, 1:2], nm[:, 0:1], rn[:, slot, 0:1], ALU.mult).then_inc(s_nm, 1)

                def attention(c):
                    dve.wait_ge(s_ex, c + 2)
                    nc.vector.reciprocal(rs[:, 1:2], rs[:, 0:1]).then_inc(s_rc, 1)
                    dve.wait_ge(s_rc, c + 1)
                    dve.wait_ge(s_ap, c + 1)
                    nc.vector.tensor_scalar(at[:, 1, :], at[:, 0, :], rs[:, 1:2], None, ALU.mult).then_inc(s_at, 1)

                def add(c):
                    dve.wait_ge(s_out, c + 2)
                    nc.vector.tensor_tensor(m.x1[0:C, bass.ds(c * N, N)], ps[0:C, 7, 0:N],
                                            m.x[:, bass.ds(c, 1), :].rearrange("p b n -> p (b n)"), ALU.add).then_inc(s_x1, 1)

                def step(b, slot, back, front):
                    c = b - 1
                    dve.wait_ge(s_raw, b + 1)
                    convolve(b, slot, 0, 5)
                    if back:
                        maximum(c, 1 - slot)
                    convolve(b, slot, 5, 6)
                    if back:
                        attention(c)
                    convolve(b, slot, 6, 9)
                    if back:
                        add(c)

                steps(dve, step)
                maximum(B - 1, 1)
                attention(B - 1)
                add(B - 1)
                dve.wait_ge(s_x1, B + 1)
                dve.wait_ge(s_rest, 16 * 13)
                link(nc.vector.tensor_scalar(m.qkv3[:, 0:C], m.qkv3[:, 0:C], float(D) ** -0.5, None, ALU.mult))


def large_conv(nc, m, sem):
    s_win = [sem(f"windows{k}") for k in range(SLOTS)]
    s_pw, s_pwk, s_ct, s_cin = (sem(n) for n in (
        "cv_pointwise", "cv_pointwise_kept", "cv_turned", "cv_columns"))
    s_tmk_act = sem("cv_tok_kept_act")
    s_cv, s_gl, s_bt, s_btk, s_cm, s_cmk, s_tm, s_tmk, s_st, s_mv = (sem(n) for n in (
        "cv_conv", "cv_gelu", "cv_back", "cv_back_kept", "cv_chan", "cv_chan_kept", "cv_tok", "cv_tok_kept", "cv_stats", "cv_mv"))
    ps = m.ps
    win, cb = m.win, m.cb
    with ExitStack() as ctx:
        def sb(name, shape, dt=F32):
            return ctx.enter_context(nc.sbuf_tensor(name, shape, dt))
        rows = sb("cv_rows", [P, 2, C, WW])
        cin = sb("cv_cin", [P, G, B, HH])
        gl = sb("cv_gl", [P, G, 2, P])
        back = sb("cv_backs", [P, 2, WW, C])
        st = sb("cv_st", [P, NT, 6])

        with nc.Block() as block:

            @block.sync
            def _(sp):
                with sp.Fori(1, G // SLOTS) as i:
                    for k in range(SLOTS):
                        sp.wait_ge(s_cv, i * SLOTS + (k + 1 - SLOTS))
                        load_windows(sp, m, s_win[k], i * SLOTS + k, k)

            @block.gpsimd
            def _(pool):
                attention_constants(m, pool, sem("at_constants"))

            @block.tensor
            def _(pe):
                x1v = m.x1[:, :].rearrange("c (h n x) -> c h n x", h=2, x=WW)
                for h in range(2):
                    for x in range(WW):
                        nc.tensor.matmul(ps[:, 4 * h + x // 4, C * (x % 4):C * (x % 4 + 1)], x1v[:, h, :, x],
                                         m.wT[:, M_PW, :], start=True, stop=True).then_inc(s_pw, 1)
                for g in range(G):
                    if g % 2 == 0:
                        pe.wait_ge(s_pwk, 8)
                        if g >= 8:
                            pe.wait_ge(s_cin, g // 2 - 3)
                    for h in range(2):
                        k = 2 * (g % 2) + h
                        nc.tensor.transpose(ps[:, g // 2 % 4, P * k:P * (k + 1)],
                                            rows[:, h, CG * g:CG * (g + 1), :].rearrange("p c x -> p (c x)"),
                                            m.ident[:, :]).then_inc(s_ct, 1)
                pe.wait_ge(s_cin, G // 2)
                with pe.Fori(0, G // SLOTS) as i:
                    for k in range(SLOTS):
                        pe.wait_ge(s_win[k], (i + 1) * (16 * CG))
                        pe.wait_ge(s_gl, i * SLOTS + 1)
                        order = [R] + [j for j in range(KW) if j != R]
                        for n, j in enumerate(order):
                            y0, y1 = max(0, R - j), HH - max(0, j - R)
                            ins = nc.tensor.matmul(
                                ps[:, 4 + k, 0:B * HH].rearrange("p (b y) -> p b y", y=HH)[:, :, y0:y1],
                                win[:, k, :, :].rearrange("p c w -> p (c w)")[:, j:CG * WIN:KW],
                                cin[:, bass.ds(i * SLOTS + k, 1), :, y0 + j - R:y1 + j - R].rearrange("p g b y -> p (g b) y"),
                                start=(n == 0), stop=(n == KW - 1))
                        ins.then_inc(s_cv, 1)
                for g in range(G):
                    pe.wait_ge(s_gl, g + 1 + 1)
                    if g % 2 == 0 and g >= 8:
                        pe.wait_ge(s_btk, g // 2 - 3)
                    for h in range(2):
                        k = 2 * h + g % 2
                        nc.tensor.transpose(ps[:, g // 2 % 4, P * k:P * (k + 1)], gl[:, g, h, :], m.ident[:, :]).then_inc(s_bt, 1)
                pe.wait_ge(s_btk, G // 2)
                for h in range(2):
                    for x in range(WW):
                        nc.tensor.transpose(ps[0:C, 4 * h + x // 4, P * (x % 4):P * (x % 4 + 1)], back[:, h, WW - 1 - x, :],
                                            m.ident[:, :]).then_inc(s_cm, 1)
                pe.wait_ge(s_cmk, 8)
                for t in range(NT):
                    nc.tensor.transpose(ps[:, t // 4, C * (t % 4):C * (t % 4 + 1)], m.chan[0:C, P * t:P * (t + 1)],
                                        m.ident[0:C, 0:C]).then_inc(s_tm, 1)

            @block.scalar
            def _(act):
                for s in (s_gl,):
                    act.sem_inc(s, 1)
                nc.scalar.preload_act_table(ACT.Gelu)
                for q in range(0, 8, 2):
                    act.wait_ge(s_pw, 4 * (q + 1))
                    nc.scalar.copy(rows[:, q // 4, :, 4 * (q % 4):4 * (q % 4 + 1)].rearrange("p c x -> p x c"),
                                   ps[:, q, 0:4 * C].rearrange("p (x c) -> p x c", c=C)).then_inc(s_pwk, 1)
                with act.Fori(0, G // SLOTS) as i:
                    for k in range(SLOTS):
                        act.wait_ge(s_cv, i * SLOTS + k + 1)
                        nc.scalar.activation(gl[:, bass.ds(i * SLOTS + k, 1), :, :].rearrange("p g h n -> p (g h n)"),
                                             ps[:, 4 + k, 0:B * HH], ACT.Gelu,
                                             bias=cb[:, bass.ds(i * SLOTS + k, 1)]).then_inc(s_gl, 1)

                for q in range(0, 8, 2):
                    act.wait_ge(s_cm, 4 * (q + 1))
                    nc.scalar.copy(m.chan[0:C, :].rearrange("c (h n x) -> c h x n", h=2, x=WW)[:, q // 4, 4 * (q % 4):4 * (q % 4 + 1), :],
                                   ps[0:C, q, :].rearrange("p (x n) -> p x n", x=4)).then_inc(s_cmk, 1)
                for q in range(0, 8, 2):
                    act.wait_ge(s_tm, 4 * (q + 1))
                    nc.scalar.copy(m.tok[:, 4 * q:4 * (q + 1), :].rearrange("p t c -> p (t c)"), ps[:, q, 0:4 * C]).then_inc(s_tmk_act, 1)

            @block.vector
            def _(dve):
                for q in range(1, 8, 2):
                    dve.wait_ge(s_pw, 4 * (q + 1))
                    nc.vector.tensor_copy(rows[:, q // 4, :, 4 * (q % 4):4 * (q % 4 + 1)].rearrange("p c x -> p x c"),
                                          ps[:, q, 0:4 * C].rearrange("p (x c) -> p x c", c=C)).then_inc(s_pwk, 1)
                for q in range(G // 2):
                    dve.wait_ge(s_ct, 4 * (q + 1))
                    nc.vector.tensor_copy(cin[:, 2 * q:2 * q + 2, :, :].rearrange("p g b y -> p (g b y)"), ps[:, q % 4, :]).then_inc(s_cin, 1)
                for q in range(G // 2):
                    dve.wait_ge(s_bt, 4 * (q + 1))
                    for h in range(2):
                        ins = nc.vector.tensor_copy(
                            back[:, h, :, 2 * CG * q:2 * CG * (q + 1)].rearrange("p x c -> p c x"),
                            ps[:, q % 4, 2 * P * h:2 * P * (h + 1)].rearrange("p (c x) -> p c x", x=WW))
                    ins.then_inc(s_btk, 1)
                for q in range(1, 8, 2):
                    dve.wait_ge(s_cm, 4 * (q + 1))
                    nc.vector.tensor_copy(m.chan[0:C, :].rearrange("c (h n x) -> c h x n", h=2, x=WW)[:, q // 4, 4 * (q % 4):4 * (q % 4 + 1), :],
                                          ps[0:C, q, :].rearrange("p (x n) -> p x n", x=4)).then_inc(s_cmk, 1)

                def moments(q):
                    dve.wait_ge(s_tmk_act, (q + 1) // 2)
                    dve.wait_ge(s_tmk, (q + 1) // 2)
                    for t in range(4 * q - 4, 4 * q + 4):
                        nc.vector.bn_stats(st[:, t, :], m.tok[:, t, :]).then_inc(s_st, 1)
                    dve.wait_ge(s_st, 4 * q + 4)
                    for t in range(4 * q - 4, 4 * q + 4):
                        nc.vector.bn_aggr(m.mv[:, t, :], st[:, t, :]).then_inc(s_mv, 1)

                for q in range(1, 8, 2):
                    dve.wait_ge(s_tm, 4 * (q + 1))
                    nc.vector.tensor_copy(m.tok[:, 4 * q:4 * (q + 1), :].rearrange("p t c -> p (t c)"), ps[:, q, 0:4 * C]).then_inc(s_tmk, 1)
                    moments(q)
                dve.wait_ge(s_mv, NT)


def attention_constants(m, pool, s_c):
    link = Link(pool, s_c)
    for slot in range(2):
        ones = m.ks[C:, slot, :, :, :]
        link(pool.memset(ones, 0.0))
        for k in range(3):
            link(pool.affine_select(out=ones, in_=ones, compare_op=ALU.not_equal, fill=1.0,
                                    base=-H * k, pattern=[[-1, H], [0, 2], [0, N]], channel_multiplier=1))
    link(pool.memset(m.oT[C:C + 1, :, :], 1.0))
    link(pool.memset(m.mxp[:, :, :, :], 0.0))
    link(pool.memset(m.vp[:, :, :, :, :, :], 0.0))
    for slot in range(2):
        for k in range(2 * TPI):
            blocks = m.vp[:, slot, k // TPI, k % TPI, :, :].rearrange("p h w -> p (h w)")
            link(pool.memset(bass.AP(blocks.tensor, blocks.offset + D, [blocks.ap[0], [OW + VD, H], [1, 1]]), 1.0))


def token_rstd(m, pool, i, n, s_rstd, s_mv=None):
    tiles = bass.ds(4 * i, 4)
    if s_mv is not None:
        pool.wait_ge(s_mv, n + 1)
        alone(pool, m)
    pool.tensor_tensor(m.var[:, tiles], m.mv[:, tiles, 1], m.eps[:, :], ALU.add).then_inc(s_rstd, 1)
    pool.wait_ge(s_rstd, 2 * n + 1)
    alone(pool, m)
    pool.tensor_tensor(m.rstd[:, tiles], m.var[:, tiles], m.power[:, 0:4], ALU.pow).then_inc(s_rstd, 1)


def layer_norm(m, pool, n, i, xn, s_own, s_xn, s_free):
    tiles = bass.ds(4 * i, 4)
    pool.wait_ge(*s_free)
    alone(pool, m)
    pool.tensor_tensor(xn[:, :, :], m.tok[:, tiles, :], m.mv[:, tiles, 0].to_broadcast([P, 4, C]),
                       ALU.subtract).then_inc(s_own, 1)
    pool.wait_ge(s_own, n + 1)
    alone(pool, m)
    pool.tensor_tensor(xn[:, :, :], xn[:, :, :], m.rstd[:, tiles].to_broadcast([P, 4, C]), ALU.mult).then_inc(s_xn, 1)


def statistics(nc, m, dve, n, i, st, mv, s_st, s_mv):
    alone(dve, m)
    for t in range(4):
        nc.vector.bn_stats(st[:, t, :], m.tok[:, bass.ds(4 * i + t, 1), :].rearrange("p t c -> p (t c)")).then_inc(s_st, 1)
    dve.wait_ge(s_st, n * 8 + 4)
    alone(dve, m)
    for t in range(4):
        nc.vector.bn_aggr(mv[:, t, :], st[:, t, :]).then_inc(s_st, 1)
    dve.wait_ge(s_st, n * 8 + 8)
    nc.vector.tensor_copy(m.mv[:, bass.ds(4 * i, 4), :], mv[:, :, :]).then_inc(s_mv, 1)


def token_attention(nc, m, sem, layer, w, proj):
    (s_own, s_xn, s_T, s_xT, s_qk, s_p1, s_r1, s_p2, s_p3, s_v, s_vp, s_S, s_mx, s_mp, s_M, s_mr0, s_mr1, s_ST, s_ex, s_O, s_rc,
     s_on, s_OT, s_oT, s_pr, s_tk, s_st, s_mv, s_rstd, s_part) = (sem(f"at_{n}") for n in (
         "pool_own", "normed", "normed_turned", "xT", "qk", "part1", "rest1", "part2", "part3", "v", "v_kept", "scores",
         "max", "max_parts", "max_turned", "max_rows0", "max_rows1", "scoresT", "exp", "out", "recip", "out_normed", "out_turned", "outT",
         "proj", "tok", "stats", "mv", "rstd", "parts_stored"))
    s_rstd_in = sem("at_rstd_in")
    s_stack = [sem(f"at_stacks{k}") for k in range(2)]
    s_own_dve = sem("at_dve_own")
    causal = layer == 3
    first = PAIRS if causal else 0
    end = first + PAIRS
    mask, maskT = (m.later_b, m.earlier_b) if causal else (m.diag_b, m.diag_b)
    ps = m.ps
    KR = C + MAX_ROWS
    W = 2 * N
    ks, vp, mxp, oT = m.ks, m.vp, m.mxp, m.oT
    with ExitStack() as ctx:
        def sb(name, shape, dt=F32):
            return ctx.enter_context(nc.sbuf_tensor(f"at{layer}_b_{name}", shape, dt))
        xn = sb("xn", [P, 4, C])
        xT = sb("xT", [C, 2, 2, N])
        part = sb("part", [C, 3, 2, 2, N], BF16)
        rest = sb("rest", [C, 2, 2, N])
        qs = sb("qs", [KR, 2, H, 2, N], BF16)
        mf = sb("mf", [P, 2, 2, TPI, H])
        pT = sb("pT", [P, 2, TPI, H, N])
        rec = sb("rec", [P, 2, TPI, H])
        on = sb("on", [P, 2, TPI, C])
        st = sb("st", [P, 4, 6])
        mv = sb("mv", [P, 4, 2])
        parts_d = nc.dram_tensor(f"at{layer}_parts", [2, 3, D, PAIRS, H, W], BF16, kind="Internal").ap()

        def heads(k):
            return ps[:, k:k + 3, :].rearrange("p k n -> p (k n)").rearrange("p (h n) -> p h n", h=H)

        def turned_max(u):
            return ps[0:KR, 6 + u, 0:P].bitcast(BF16)

        def max_rows(u):
            rows = turned_max(u)[C:KR, :]
            return bass.AP(rows.tensor, rows.offset, [rows.ap[0], [0, H], [1, N]])

        with nc.Block() as block:

            @block.sync
            def _(sp):
                def stacks(i, slot):
                    for k, s in enumerate((s_p1, s_p2, s_p3)):
                        sp.wait_ge(s, 2 * i + 2)
                        for t in range(2):
                            sp.dma_start(parts_d[t, 2 - k if t else k, :, bass.ds(i - first, 1), :, :].rearrange("d i h n -> h (d i) n"),
                                         part[:, k, t, :, :].rearrange("c u n -> c (u n)")).then_inc(s_part, 16)
                    sp.wait_ge(s_part, 96 * i + 96)
                    for row, count in ((0, 3), (3, 2), (5, 1)):
                        for t, stack in enumerate((qs, ks)):
                            start = 3 - count if t else 0
                            sp.dma_start(stack[D * row:D * (row + count), slot, :, :, :].rearrange("r h u n -> r (h u n)"),
                                         parts_d[t, start:start + count, :, bass.ds(i - first, 1), :, :].rearrange(
                                             "k d i h n -> (k d) (i h n)")).then_inc(s_stack[slot], 16)

                with sp.Fori(first // 2, end // 2) as j:
                    for slot in range(2):
                        stacks(2 * j + slot, slot)

            @block.gpsimd
            def _(pool):
                def normed(i):
                    token_rstd(m, pool, i - first, i, s_rstd_in)
                    pool.wait_ge(s_rstd_in, 2 * i + 2)
                    layer_norm(m, pool, i, i - first, xn, s_own, s_xn, (s_T, i * 2 + 1))

                for i in range(first, first + 3):
                    normed(i)
                with pool.Fori(first, end - 3) as i:
                    normed(i + 3)
                    token_rstd(m, pool, i - first, i, s_rstd, s_mv)
                for i in range(end - 3, end):
                    token_rstd(m, pool, i - first, i, s_rstd, s_mv)
                pool.wait_ge(s_rstd, 2 * end)

            @block.tensor
            def _(pe):
                if first == 0:
                    pe.sem_inc(s_T, 1)

                def turn(i):
                    pe.wait_ge(s_xn, i + 1)
                    for u in range(2):
                        for t in range(TPI):
                            ins = nc.tensor.transpose(ps[0:C, 6 + u, P * t:P * (t + 1)], xn[:, 2 * u + t, :], m.ident[:, :])
                        ins.then_inc(s_T, 1)

                def queries_keys(i, slot):
                    for u in range(2):
                        pe.wait_ge(s_xT, 2 * i + u + 1)
                        for t in range(2):
                            ins = nc.tensor.matmul(ps[0:C, 3 * u, N * t:N * (t + 1)], w[t], xT[:, slot, u, :], start=True, stop=True)
                        ins.then_inc(s_qk, 1)

                def values(i, slot):
                    for u in range(2):
                        for t in range(TPI):
                            ins = nc.tensor.matmul(ps[:, 3 * u + 1, C * t:C * (t + 1)], xT[:, slot, u, P * t:P * (t + 1)], w[2],
                                                   start=True, stop=True)
                        ins.then_inc(s_v, 1)

                def scores(i, slot, u, t):
                    bank = heads(3 * t)
                    nk = P if causal and t == 0 else N
                    for h in range(H):
                        nc.tensor.matmul(bank[:, h, 0:nk], qs[0:C, slot, h, u, P * t:P * (t + 1)], ks[0:C, slot, h, u, 0:nk],
                                         start=True, stop=False)
                        ins = nc.tensor.matmul(bank[:, h, P * t:P * (t + 1)], m.ident_b[:, :], mask[:, :],
                                               start=False, stop=True)
                    ins.then_inc(s_S, 1)

                def transposed_scores(i, slot, u, t):
                    bank = heads(3 * t)
                    n0 = P if causal and t == 1 else 0
                    for h in range(H):
                        nc.tensor.matmul(bank[:, h, n0:N], ks[:, slot, h, u, P * t:P * (t + 1)], qs[:, slot, h, u, n0:N],
                                         start=True, stop=False)
                        ins = nc.tensor.matmul(bank[:, h, P * t:P * (t + 1)], m.ident_b[:, :], maskT[:, :],
                                               start=False, stop=True)
                    ins.then_inc(s_ST, 1)

                def turn_maxima(i, u):
                    pe.wait_ge(s_mp, 2 * i + u + 1)
                    for t in range(TPI):
                        ins = nc.tensor.transpose(turned_max(u)[:, P * t:P * (t + 1)], mxp[:, u, t, :], m.ident_b[:, :])
                    ins.then_inc(s_M, 1)

                def weighted_values(i, slot, u, t):
                    if t == 0:
                        pe.wait_ge(s_ex, 4 * i + 2 * u + 2)
                    terms = [(k, h) for k in range(1 if causal and t == 0 else TPI) for h in range(H)]
                    for n, (k, h) in enumerate(terms):
                        ins = nc.tensor.matmul(ps[:, 6 + u, OW * t:OW * (t + 1)], pT[:, u, k, h, P * t:P * (t + 1)],
                                               vp[:, slot, u, k, h, :], start=(n == 0), stop=(n == len(terms) - 1))
                    if t == TPI - 1:
                        ins.then_inc(s_O, 1)

                def turn_out(i, u):
                    pe.wait_ge(s_on, 2 * i + u + 1)
                    for t in range(TPI):
                        ins = nc.tensor.transpose(ps[0:C, 6 + u, P * t:P * (t + 1)], on[:, u, t, :], m.ident[:, :])
                    ins.then_inc(s_OT, 1)

                def project(i, u):
                    pe.wait_ge(s_oT, 2 * i + u + 1)
                    for t in range(TPI):
                        ins = nc.tensor.matmul(ps[:, 6 + u, C * t:C * (t + 1)], oT[:, u, P * t:P * (t + 1)], proj,
                                               start=True, stop=True)
                    ins.then_inc(s_pr, 1)

                def back_and_front(i, slot):
                    back = i is not first
                    pe.wait_ge(s_stack[slot], 48 * (i - slot) + 96)
                    pe.wait_ge(s_vp, 2 * i + 1)
                    scores(i, slot, 0, 0)
                    if back:
                        turn_out(i - 1, 0)
                    pe.wait_ge(s_vp, 2 * i + 2)
                    scores(i, slot, 0, 1)
                    if back:
                        project(i - 1, 0)
                        weighted_values(i - 1, 1 - slot, 1, 0)
                    pe.wait_ge(s_mx, 4 * i + 1)
                    scores(i, slot, 1, 0)
                    if back:
                        weighted_values(i - 1, 1 - slot, 1, 1)
                        pe.wait_ge(s_tk, 2 * i - 1)
                    turn_maxima(i, 0)
                    pe.wait_ge(s_mx, 4 * i + 2)
                    scores(i, slot, 1, 1)
                    if back:
                        turn_out(i - 1, 1)
                    pe.wait_ge(s_mx, 4 * i + 3)
                    pe.wait_ge(s_mr0, i + 1)
                    transposed_scores(i, slot, 0, 0)
                    if back:
                        project(i - 1, 1)
                        pe.wait_ge(s_tk, 2 * i)
                    turn_maxima(i, 1)
                    pe.wait_ge(s_mx, 4 * i + 4)
                    transposed_scores(i, slot, 0, 1)
                    pe.wait_ge(s_mr1, i + 1)

                def middle(i, slot, ahead):
                    if ahead == 2:
                        turn(i + 2)
                    pe.wait_ge(s_ex, 4 * i + 1)
                    transposed_scores(i, slot, 1, 0)
                    pe.wait_ge(s_ex, 4 * i + 2)
                    transposed_scores(i, slot, 1, 1)
                    if ahead == 2:
                        pe.wait_ge(s_xT, 2 * i + 5)
                    weighted_values(i, slot, 0, 0)
                    pe.wait_ge(s_ex, 4 * i + 4)
                    if ahead == 2:
                        queries_keys(i + 2, slot)
                    if ahead:
                        values(i + 1, 1 - slot)
                    weighted_values(i, slot, 0, 1)

                turn(first)
                queries_keys(first, 0)
                values(first, 0)
                turn(first + 1)
                pe.wait_ge(s_r1, 2 * first + 2)
                queries_keys(first + 1, 1)
                pe.wait_ge(s_r1, 2 * first + 4)
                back_and_front(first, 0)
                with pe.Fori(first // 2, end // 2 - 1) as j:
                    for slot in range(2):
                        middle(2 * j + slot, slot, 2)
                        back_and_front(2 * j + slot + 1, 1 - slot)
                middle(end - 2, 0, 1)
                back_and_front(end - 1, 1)
                middle(end - 1, 1, 0)
                turn_out(end - 1, 0)
                project(end - 1, 0)
                weighted_values(end - 1, 1, 1, 0)
                weighted_values(end - 1, 1, 1, 1)
                turn_out(end - 1, 1)
                project(end - 1, 1)

            @block.scalar
            def _(act):
                nc.scalar.preload_act_table(ACT.Exp)

                def parts(i, waits=True):
                    if waits:
                        act.wait_ge(s_part, 96 * i)
                    for u in range(2):
                        act.wait_ge(s_qk, 2 * i + u + 1)
                        nc.scalar.copy(part[:, 0, :, u, :], ps[0:C, 3 * u, :].rearrange("c (t n) -> c t n", t=2)).then_inc(s_p1, 1)
                    for u in range(2):
                        act.wait_ge(s_r1, 2 * i + u + 1)
                        nc.scalar.copy(part[:, 1, :, u, :], rest[:, u, :, :]).then_inc(s_p2, 1)

                def weights(i, u):
                    for t in range(TPI):
                        n0 = P if causal and t == 1 else 0
                        act.wait_ge(s_ST, 4 * i + 2 * u + t + 1)
                        nc.scalar.activation(pT[:, u, t, :, n0:N], heads(3 * t)[:, :, n0:N], ACT.Exp).then_inc(s_ex, 1)

                def rows(i, slot):
                    act.wait_ge(s_M, 2 * i + 1)
                    nc.scalar.copy(qs[C:KR, slot, :, 0, :], max_rows(0)).then_inc(s_mr0, 1)

                def out(i, u):
                    act.wait_ge(s_OT, 2 * i + u + 1)
                    nc.scalar.copy(oT[0:C, u, :], ps[0:C, 6 + u, 0:N]).then_inc(s_oT, 1)

                def step(i, slot, ahead):
                    weights(i, 1)
                    if ahead == 2:
                        parts(i + 2)
                    out(i, 0)
                    if ahead:
                        rows(i + 1, 1 - slot)
                    out(i, 1)
                    if ahead:
                        weights(i + 1, 0)

                parts(first, waits=first > 0)
                parts(first + 1)
                rows(first, 0)
                weights(first, 0)
                with act.Fori(first // 2, end // 2 - 1) as j:
                    for slot in range(2):
                        step(2 * j + slot, slot, 2)
                step(end - 2, 0, 1)
                step(end - 1, 1, 0)

            @block.vector
            def _(dve):

                def normed(i, slot):
                    for u in range(2):
                        dve.wait_ge(s_T, 2 * i + u + 2)
                        nc.vector.tensor_copy(xT[:, slot, u, :], ps[0:C, 6 + u, 0:N]).then_inc(s_xT, 1)

                def parts(i):
                    for u in range(2):
                        dve.wait_ge(s_p1, 2 * i + u + 1)
                        nc.vector.tensor_tensor(rest[:, u, :, :], ps[0:C, 3 * u, :].rearrange("c (t n) -> c t n", t=2),
                                                part[:, 0, :, u, :], ALU.subtract).then_inc(s_r1, 1)
                    for u in range(2):
                        dve.wait_ge(s_p2, 2 * i + u + 1)
                        nc.vector.tensor_tensor(part[:, 2, :, u, :], rest[:, u, :, :], part[:, 1, :, u, :],
                                                ALU.subtract).then_inc(s_p3, 1)

                def values(i, slot):
                    for u in range(2):
                        dve.wait_ge(s_v, 2 * i + u + 1)
                        for t in range(TPI):
                            blocks = vp[:, slot, u, t, :, :].rearrange("p h w -> p (h w)")
                            ins = nc.vector.tensor_copy(
                                bass.AP(blocks.tensor, blocks.offset, [blocks.ap[0], [OW + VD, H], [1, D]]),
                                ps[:, 3 * u + 1, C * t:C * (t + 1)].rearrange("p (h d) -> p h d", d=D))
                        ins.then_inc(s_vp, 1)

                def maximum(i, u, t):
                    nk = P if causal and t == 0 else N
                    dve.wait_ge(s_S, 4 * i + 2 * u + t + 1)
                    nc.vector.tensor_reduce(mf[:, u, 0, t, :], heads(3 * t)[:, :, 0:nk], AX.X, ALU.max,
                                            negate=True).then_inc(s_mx, 1)

                def maxima_parts(i, u):
                    own = 6 * i + 3 * u
                    dve.wait_ge(s_mx, 4 * i + 2 * u + 2)
                    nc.vector.tensor_copy(mxp[:, u, :, C:C + H], mf[:, u, 0, :, :]).then_inc(s_own_dve, 1)
                    dve.wait_ge(s_own_dve, own + 1)
                    nc.vector.tensor_tensor(mf[:, u, 1, :, :], mf[:, u, 0, :, :], mxp[:, u, :, C:C + H],
                                            ALU.subtract).then_inc(s_own_dve, 1)
                    dve.wait_ge(s_own_dve, own + 2)
                    nc.vector.tensor_copy(mxp[:, u, :, C + H:C + 2 * H], mf[:, u, 1, :, :]).then_inc(s_own_dve, 1)
                    dve.wait_ge(s_own_dve, own + 3)
                    nc.vector.tensor_tensor(mxp[:, u, :, C + 2 * H:KR], mf[:, u, 1, :, :], mxp[:, u, :, C + H:C + 2 * H],
                                            ALU.subtract).then_inc(s_mp, 1)

                def rows(i, slot):
                    dve.wait_ge(s_M, 2 * i + 2)
                    nc.vector.tensor_copy(qs[C:KR, slot, :, 1, :], max_rows(1)).then_inc(s_mr1, 1)

                def out(i, u):
                    dve.wait_ge(s_O, 2 * i + u + 1)
                    o = ps[:, 6 + u, 0:TPI * OW].rearrange("p (t h w) -> p t h w", t=TPI, h=H)
                    nc.vector.reciprocal(rec[:, u, :, :], o[:, :, :, D]).then_inc(s_rc, 1)
                    dve.wait_ge(s_rc, 2 * i + u + 1)
                    nc.vector.tensor_tensor(on[:, u, :, :].rearrange("p t (h d) -> p t h d", d=D), o[:, :, :, 0:D],
                                            rec[:, u, :, :].to_broadcast([P, TPI, H, D]), ALU.mult).then_inc(s_on, 1)

                def add(i, u):
                    dve.wait_ge(s_pr, 2 * i + u + 1)
                    tok = m.tok[:, bass.ds(4 * (i - first) + 2 * u, 2), :]
                    nc.vector.tensor_tensor(tok, ps[:, 6 + u, 0:2 * C].rearrange("p (t c) -> p t c", c=C), tok,
                                            ALU.add).then_inc(s_tk, 1)

                def moments(i):
                    dve.wait_ge(s_tk, 2 * i + 2)
                    statistics(nc, m, dve, i, i - first, st, mv, s_st, s_mv)

                def maxima(i, slot):
                    back = i is not first
                    maximum(i, 0, 0)
                    if back:
                        add(i - 1, 0)
                    maximum(i, 0, 1)
                    maxima_parts(i, 0)
                    maximum(i, 1, 0)
                    if back:
                        out(i - 1, 1)
                    maximum(i, 1, 1)
                    maxima_parts(i, 1)
                    if back:
                        add(i - 1, 1)
                    rows(i, slot)
                    if back:
                        moments(i - 1)

                normed(first, 0)
                parts(first)
                values(first, 0)
                normed(first + 1, 1)
                parts(first + 1)
                maxima(first, 0)
                with dve.Fori(first // 2, end // 2 - 1) as j:
                    for slot in range(2):
                        i = 2 * j + slot
                        normed(i + 2, slot)
                        parts(i + 2)
                        values(i + 1, 1 - slot)
                        out(i, 0)
                        maxima(i + 1, 1 - slot)
                values(end - 1, 1)
                out(end - 2, 0)
                maxima(end - 1, 1)
                for u in range(2):
                    out(end - 1, u)
                    add(end - 1, u)
                moments(end - 1)
                dve.wait_ge(s_mv, end)


def experts(nc, m, sem, layer, f, out=None):
    (s_ones, s_xn, s_own, s_T, s_xT, s_gc, s_gt, s_sc, s_nm, s_ex, s_gd, s_bt, s_F, s_h, s_Y, s_ac, s_st, s_mv, s_OT, s_oc, s_bc, s_rstd, s_xl, s_w) = (
        sem(f"ff_{n}") for n in (
            "ones", "normed", "dve_own", "normed_turned", "xT", "chan", "gate_products", "gate_scores", "gate_shifted",
            "gate_exp", "gate_dve", "biased", "hidden", "gelu", "result", "added", "stats", "mv", "out_turned", "out_kept",
            "pool_bias", "rstd", "x_low", "w_parts"))
    s_store = sem("ff_stored")
    last = out is not None
    first = PAIRS if last else 0
    end = first + PAIRS
    ps = m.ps
    with ExitStack() as ctx:
        def sb(name, shape, dt=F32):
            return ctx.enter_context(nc.sbuf_tensor(f"ff{layer}_b_{name}", shape, dt))
        xn = sb("xn", [P, 2, 4, C])
        xT = sb("xT", [C + 1, 2, Q])
        xh = sb("xh", [C, T], F32R)
        xl = sb("xl", [C, T], F32R)
        wh = sb("wh", [C, E, HID], F32R)
        wl = sb("wl", [C, E, HID], F32R)
        sc = sb("sc", [P, NT, E])
        pr = sb("pr", [P, NT, E])
        gt = sb("gt", [P, NT, E, E])
        eq = sb("eq", [P, NT, E, E])
        one = sb("one", [P, 3, NT])
        gate = sb("gate", [P, NT, E])
        bias = sb("bias", [P, 2, 4, C])
        h = sb("h", [P, 2, HC, Q])
        st = sb("st", [P, 4, 6])
        mv = sb("mv", [P, 4, 2])
        fin = sb("fin", [P, 4, C])
        fT = sb("fT", [C, Q])
        with nc.Block() as block:

            if last:
                @block.sync
                def _(sp):
                    sp.sem_inc(s_store, 1)
                    with sp.Fori(first, end) as i:
                        sp.wait_ge(s_oc, i - first + 1)
                        sp.dma_start(out.rearrange("b c h w -> c b (h w)")[:, bass.ds(2 * (i - first), 2), :],
                                     fT[:, :].rearrange("c (b n) -> c b n", n=N)).then_inc(s_store, 16)
                    sp.wait_ge(s_store, 16 * PAIRS + 1)

            @block.gpsimd
            def _(pool):
                pool.memset(xT[C:C + 1, :, :], 1.0).then_inc(s_ones, 1)
                if first == 0:
                    pool.sem_inc(s_xl, 1)
                with pool.Fori(first // 2, end // 2) as j:
                    for u in range(2):
                        tokens = bass.ds(Q * (2 * j + u - first), Q)
                        pool.wait_ge(s_gc, 2 * j + u + 1 + 1)
                        alone(pool, m)
                        pool.tensor_tensor(xl[:, tokens], xT[0:C, u, :], xh[:, tokens], ALU.subtract).then_inc(s_xl, 1)
                pool.wait_ge(s_w, 1 + 2 * last)
                pool.tensor_tensor(wl[:, :, :], f.w1[:, :, :], wh[:, :, :], ALU.subtract).then_inc(s_w, 1)
                pool.wait_ge(s_gd, GATE_STEPS * (1 + last))
                with pool.Fori(first, end) as i:
                    link = Link(pool, s_bc, i * (2 * E))
                    tok = m.tok[:, bass.ds(4 * (i - first), 4), :]
                    for e in range(E):
                        b2 = f.b2[:, e:e + 1, :]
                        alone(pool, m)
                        link(pool.tensor_tensor(bias[:, e % 2, :, :], gate[:, bass.ds(4 * (i - first), 4), e].to_broadcast([P, 4, C]),
                                                bass.AP(b2.tensor, b2.offset, [b2.ap[0], [0, 4], [1, C]]), ALU.mult))
                        alone(pool, m)
                        link(pool.tensor_tensor(tok, tok, bias[:, e % 2, :, :], ALU.add))
                    pool.sem_inc(s_bt, 1)

            @block.tensor
            def _(pe):
                for s in (s_T, s_gt, s_Y, s_OT):
                    if first == 0:
                        pe.sem_inc(s, 1)
                pe.wait_ge(s_ones, 1 + last)
                with pe.Fori(first // 2, end // 2) as j:
                    for u in range(2):
                        pe.wait_ge(s_xn, 2 * j + u + 1)
                        pe.wait_ge(s_xT, 2 * j + 1)
                        for t in range(4):
                            ins = nc.tensor.transpose(ps[0:C, u, P * t:P * (t + 1)], xn[:, u, t, :], m.ident[:, :])
                        ins.then_inc(s_T, 1)
                    for u in range(2):
                        pe.wait_ge(s_xT, 2 * j + u + 1 + 1)
                        pe.wait_ge(s_sc, 2 * j + 1)
                        for t in range(4):
                            ins = nc.tensor.matmul(ps[:, 2 + u, E * t:E * (t + 1)], xT[:, u, P * t:P * (t + 1)], f.gate[:, :],
                                                   start=True, stop=True)
                        ins.then_inc(s_gt, 1)

                def hidden(i, e):
                    for j in range(HC):
                        k = 3 * (e % 2) + j
                        if e >= 2:
                            pe.wait_ge(s_h, i * (E * HC) + ((e - 2) * HC + j + 1) + 1)
                        elif j == 0:
                            pe.wait_ge(s_h, i * (E * HC) + 1)
                        tokens = bass.ds(Q * (i - first), Q)
                        for n, (w, x) in enumerate(((wh, xh), (wh, xl), (wl, xh))):
                            ins = nc.tensor.matmul(ps[:, k, :], w[:, e, P * j:P * (j + 1)], x[:, tokens], start=(n == 0), stop=(n == 2))
                        ins.then_inc(s_F, 1)

                def result(i, e):
                    pe.wait_ge(s_h, i * (E * HC) + (e + 1) * HC + 1)
                    if e >= 2:
                        pe.wait_ge(s_ac, i * E + (e - 1) + 1)
                    else:
                        pe.wait_ge(s_ac, i * E + 1)
                    for t in range(4):
                        for j in range(HC):
                            ins = nc.tensor.matmul(ps[:, 6 + e % 2, C * t:C * (t + 1)], h[:, e % 2, j, P * t:P * (t + 1)],
                                                   f.w2[:, e * HC + j, :], start=(j == 0), stop=(j == HC - 1))
                    ins.then_inc(s_Y, 1)

                def turn_output(i):
                    pe.wait_ge(s_ac, i * E + E + 1)
                    for t in range(4):
                        ins = nc.tensor.transpose(ps[0:C, 6, P * t:P * (t + 1)], fin[:, t, :], m.ident[:, :])
                    ins.then_inc(s_OT, 1)

                def part(i, back):
                    hidden(i, 0)
                    hidden(i, 1)
                    if back:
                        turn_output(i - 1)
                        pe.wait_ge(s_oc, i - first)
                    result(i, 0)
                    hidden(i, 2)
                    result(i, 1)
                    hidden(i, 3)
                    result(i, 2)
                    result(i, 3)

                pe.wait_ge(s_sc, end + 1)
                pe.wait_ge(s_xl, end + 1)
                pe.wait_ge(s_w, 2 + 2 * last)
                if last:
                    part(first, False)
                    with pe.Fori(first + 1, end) as i:
                        part(i, True)
                    turn_output(end - 1)
                else:
                    with pe.Fori(first, end) as i:
                        part(i, False)

            @block.scalar
            def _(act):
                for s in (s_gc, s_h):
                    if first == 0:
                        act.sem_inc(s, 1)
                nc.scalar.preload_act_table(ACT.Exp)
                nc.scalar.copy(wh[:, :, :], f.w1[:, :, :]).then_inc(s_w, 1)
                with act.Fori(first // 2, end // 2) as j:
                    for u in range(2):
                        act.wait_ge(s_xT, 2 * j + u + 1 + 1)
                        nc.scalar.copy(xh[:, bass.ds(Q * (2 * j + u - first), Q)], xT[0:C, u, :]).then_inc(s_gc, 1)
                act.wait_ge(s_nm, 1 + last)
                nc.scalar.activation(pr[:, :, :], sc[:, :, :], ACT.Exp).then_inc(s_ex, 1)
                nc.scalar.preload_act_table(ACT.Gelu)

                def keep_output(i):
                    act.wait_ge(s_OT, i - first + 2)
                    act.wait_ge(s_store, (i - first) * 16 + 1)
                    nc.scalar.copy(fT[:, :], ps[0:C, 6, :]).then_inc(s_oc, 1)

                def part(i, back):
                    for e in range(E):
                        if back and e == 2:
                            keep_output(i - 1)
                        for j in range(HC):
                            act.wait_ge(s_F, i * (E * HC) + (e * HC + j + 1))
                            if j == 0:
                                act.wait_ge(s_Y, i * E + (e - 1) + 1) if e >= 2 else act.wait_ge(s_Y, i * E + 1)
                            nc.scalar.activation(h[:, e % 2, j, :], ps[:, 3 * (e % 2) + j, :], ACT.Gelu,
                                                 bias=f.b1[:, e * HC + j:e * HC + j + 1]).then_inc(s_h, 1)

                if last:
                    part(first, False)
                    with act.Fori(first + 1, end) as i:
                        part(i, True)
                    keep_output(end - 1)
                else:
                    with act.Fori(first, end) as i:
                        part(i, False)

            @block.vector
            def _(dve):
                for s in (s_xT, s_sc, s_ac):
                    if first == 0:
                        dve.sem_inc(s, 1)

                def normed(j):
                    dve.wait_ge(s_T, 2 * j + 1)
                    for u in range(2):
                        tiles = bass.ds(4 * (2 * j + u - first), 4)
                        nc.vector.tensor_tensor(xn[:, u, :, :], m.tok[:, tiles, :], m.mv[:, tiles, 0].to_broadcast([P, 4, C]),
                                                ALU.subtract).then_inc(s_own, 1)
                    for u in range(2):
                        tiles = bass.ds(4 * (2 * j + u - first), 4)
                        dve.wait_ge(s_own, 2 * j + u + 1)
                        nc.vector.tensor_tensor(xn[:, u, :, :], xn[:, u, :, :], m.rstd[:, tiles].to_broadcast([P, 4, C]),
                                                ALU.mult).then_inc(s_xn, 1)

                def turned(j):
                    for u in range(2):
                        dve.wait_ge(s_T, 2 * j + u + 1 + 1)
                        dve.wait_ge(s_gt, 2 * j + 1)
                        dve.wait_ge(s_xl, 2 * j + 1)
                        nc.vector.tensor_copy(xT[0:C, u, :], ps[0:C, u, :]).then_inc(s_xT, 1)

                def gate_scores(j):
                    for u in range(2):
                        dve.wait_ge(s_gt, 2 * j + u + 1 + 1)
                        nc.vector.tensor_copy(sc[:, bass.ds(4 * (2 * j + u - first), 4), :],
                                              ps[:, 2 + u, 0:4 * E].rearrange("p (t e) -> p t e", e=E)).then_inc(s_sc, 1)

                normed(first // 2)
                with dve.Fori(first // 2, end // 2 - 1) as j:
                    turned(j)
                    normed(j + 1)
                    gate_scores(j)
                turned(end // 2 - 1)
                gate_scores(end // 2 - 1)
                dve.wait_ge(s_sc, end + 1)
                link = Link(dve, s_gd, GATE_STEPS * last)
                link(nc.vector.tensor_reduce(one[:, 0, :], sc[:, :, :], AX.X, ALU.max))
                nc.vector.tensor_tensor(sc[:, :, :], sc[:, :, :], one[:, 0, :].to_broadcast([P, NT, E]), ALU.subtract).then_inc(s_nm, 1)
                dve.wait_ge(s_ex, 1 + last)
                link(nc.vector.tensor_reduce(one[:, 1, :], pr[:, :, :], AX.X, ALU.add))
                link(nc.vector.reciprocal(one[:, 2, :], one[:, 1, :]))
                link(nc.vector.tensor_tensor(pr[:, :, :], pr[:, :, :], one[:, 2, :].to_broadcast([P, NT, E]), ALU.mult))
                own = pr[:, :, :].to_broadcast([P, NT, E, E])
                other = bass.AP(pr[:, :, :].tensor, pr[:, :, :].offset, [pr[:, :, :].ap[0], [E, NT], [0, E], [1, E]])
                before = m.before[:, 0, :, :].rearrange("p a b -> p (a b)")
                link(nc.vector.tensor_tensor(eq[:, :, :, :], other, own, ALU.is_equal))
                link(nc.vector.tensor_tensor(eq[:, :, :, :].rearrange("p t a b -> p t (a b)"), eq[:, :, :, :].rearrange("p t a b -> p t (a b)"),
                                             bass.AP(before.tensor, before.offset, [before.ap[0], [0, NT], [1, E * E]]), ALU.mult))
                link(nc.vector.tensor_tensor(gt[:, :, :, :], other, own, ALU.is_gt))
                link(nc.vector.tensor_tensor(gt[:, :, :, :], gt[:, :, :, :], eq[:, :, :, :], ALU.add))
                link(nc.vector.tensor_reduce(gate[:, :, :], gt[:, :, :, :], AX.X, ALU.add))
                link(nc.vector.scalar_tensor_tensor(gate[:, :, :], gate[:, :, :], 1.5, pr[:, :, :], ALU.is_lt, ALU.mult))
                link(nc.vector.tensor_reduce(one[:, 0, :], gate[:, :, :], AX.X, ALU.add))
                link(nc.vector.tensor_scalar(one[:, 1, :], one[:, 0, :], 1e-9, None, ALU.add))
                link(nc.vector.reciprocal(one[:, 2, :], one[:, 1, :]))
                link(nc.vector.tensor_tensor(gate[:, :, :], gate[:, :, :], one[:, 2, :].to_broadcast([P, NT, E]), ALU.mult))
                assert link.n == GATE_STEPS
                with dve.Fori(first, end) as i:
                    dve.wait_ge(s_bt, i + 1)
                    for e in range(E):
                        dve.wait_ge(s_Y, i * E + (e + 1) + 1)
                        if last and e == E - 1:
                            dve.wait_ge(s_OT, i - first + 1)
                        if e:
                            dve.wait_ge(s_ac, i * E + e + 1)
                        for t in range(4):
                            tok = m.tok[:, bass.ds(4 * (i - first) + t, 1), :].rearrange("p t c -> p (t c)")
                            dst = fin[:, t, :] if last and e == E - 1 else tok
                            ins = nc.vector.scalar_tensor_tensor(
                                dst, ps[:, 6 + e % 2, C * t:C * (t + 1)],
                                gate[:, bass.ds(4 * (i - first) + t, 1), e], tok, ALU.mult, ALU.add)
                        ins.then_inc(s_ac, 1)
                    if not last:
                        dve.wait_ge(s_ac, i * E + E + 1)
                        statistics(nc, m, dve, i, i - first, st, mv, s_st, s_mv)
                if not last:
                    dve.wait_ge(s_mv, end)


GATE_STEPS = 14


def program(nc, a, out):
    with ExitStack() as ctx:
        m = buffers(nc, ctx)

        made = {}

        def sem(name):
            if name not in made:
                made[name] = ctx.enter_context(nc.semaphore(name))
            return made[name]
        with ExitStack() as early:
            early_buffers(nc, m, early)
            channel_attention(nc, m, a, sem)
            large_conv(nc, m, sem)
        token_attention(nc, m, sem, 2, [m.wT[0:C, M_QKV2 + t, :] for t in range(3)], m.wT[:, M_PROJ2, :])
        experts(nc, m, sem, 2, m.ffn[0])
        token_attention(nc, m, sem, 3, [m.qkv3[:, C * t:C * (t + 1)] for t in range(3)], m.proj3[:, :])
        experts(nc, m, sem, 3, m.ffn[1], out)


def kernel(**inputs):
    import numpy as np
    import concourse.bacc as bacc
    from concourse.bass_utils import run_bass_kernel_spmd

    nc = bacc.Bacc("TRN2", target_bir_lowering=False, num_devices=1)
    arrays, a = {}, {}
    for name in INS:
        arrays[f"in_{name}"] = np.ascontiguousarray(inputs[name])
        a[name] = nc.dram_tensor(f"in_{name}", arrays[f"in_{name}"].shape, F32, kind="ExternalInput").ap()
    out = nc.dram_tensor("out", (B, C, HH, WW), F32, kind="ExternalOutput").ap()
    program(nc, a, out)
    return run_bass_kernel_spmd(nc, [arrays], core_ids=[0]).results[0]["out"]
```

```python
from contextlib import ExitStack

import concourse.bass as bass
from concourse import mybir

F32 = mybir.dt.float32
BF16 = mybir.dt.bfloat16
F32R = mybir.dt.float32r
ALU = mybir.AluOpType
ACT = mybir.ActivationFunctionType
AX = mybir.AxisListType

P = 128
B, C, HH, WW = 16, 96, 16, 16
N = HH * WW
T = B * N
NT = T // P
TPI = N // P
PAIRS = B // 2
GN_CH = 3
CA_H, CA_D = 8, 12
H, D = 6, 16
VD = D + 1
MAX_ROWS = 3 * H
OW = H * VD
Q = 4 * P
E, HID = 4, 384
HC = HID // P
KW = 13
R = KW // 2
CG = P // WW
G = C // CG
WIN = WW * KW
LEAD = WW - 1 - R
LINE = (2 * WW - 1) * KW
MASKED = -1.0e30

INS = ['x', 'L0_conv_w_qkv', 'L0_conv_w_dw', 'L0_conv_w_proj', 'L0_conv_temperature', 'L1_conv_pw_w', 'L1_conv_pw_g',
       'L1_conv_pw_b', 'L1_conv_pw_m', 'L1_conv_pw_v', 'L1_conv_dwk_w', 'L1_conv_dwk_g', 'L1_conv_dwk_b',
       'L1_conv_dwk_m', 'L1_conv_dwk_v', 'L1_conv_dw1_w', 'L1_conv_dw1_g', 'L1_conv_dw1_b', 'L1_conv_dw1_m',
       'L1_conv_dw1_v', 'L2_attn_qkv_w', 'L2_attn_proj_w', 'L2_attn_proj_b', 'L2_attn_temperature', 'L2_ffn_gate_w',
       'L2_ffn_gate_b', 'L2_ffn_w1', 'L2_ffn_b1', 'L2_ffn_w2', 'L2_ffn_b2', 'L3_attn_w_qkv', 'L3_attn_w_proj',
       'L3_attn_b_proj', 'L3_ffn_gate_w', 'L3_ffn_gate_b', 'L3_ffn_w1', 'L3_ffn_b1', 'L3_ffn_w2', 'L3_ffn_b2']

VECTORS = ['L1_conv_pw_v', 'L1_conv_dwk_v', 'L1_conv_dw1_v', 'L1_conv_pw_g', 'L1_conv_dwk_g', 'L1_conv_dw1_g',
           'L1_conv_pw_b', 'L1_conv_dwk_b', 'L1_conv_dw1_b', 'L1_conv_pw_m', 'L1_conv_dwk_m', 'L1_conv_dw1_m',
           'L1_conv_dw1_w', 'L2_attn_proj_b']
V_VAR, V_G, V_B, V_M, V_DW1, V_PROJ, V_T0, V_T2 = 0, 3, 6, 9, 12, 13, 14, 15
NV = 16
M_QK0, M_V0, M_PROJ0, M_PW, M_QKV2, M_PROJ2 = 0, 2, 11, 12, 13, 16
NM = 17
SLOTS = 3
TAPS = [(0, 0)] + [(dy, dx) for dy in (-1, 0, 1) for dx in (-1, 0, 1) if dy or dx]


class Names:
    pass


class Link:

    def __init__(self, eng, sem, base=0):
        self.eng, self.sem, self.base, self.n = eng, sem, base, 0

    def __call__(self, ins):
        self.n += 1
        ins.then_inc(self.sem, 1)
        self.eng.wait_ge(self.sem, self.base + self.n)


def alone(eng, m):
    eng.sem_inc(m.s_waited, 1)


def buffers(nc, ctx):
    def sb(name, shape, dt=F32):
        return ctx.enter_context(nc.sbuf_tensor(name, shape, dt))

    m = Names()
    m.ps = ctx.enter_context(nc.psum_tensor("ps", [P, 8, 512], F32))
    m.ident = sb("ident", [P, P])
    m.ident_b = sb("ident_b", [P, P], BF16)
    m.diag_b = sb("diag_b", [P, P], BF16)
    m.later_b = sb("later_b", [P, P], BF16)
    m.heads_b = sb("heads_b", [C, C], BF16)
    m.groups = sb("groups", [C, C])
    m.before = sb("before", [P, 4, E, E])
    m.power = sb("power", [P, 32])
    m.tok = sb("tok", [P, NT, C])
    m.mv = sb("mv", [P, NT, 2])
    m.var = sb("var", [P, NT])
    m.eps = sb("eps", [P, 4])
    m.rstd = sb("rstd", [P, NT])
    m.ks = sb("keys", [C + MAX_ROWS, 2, H, 2, N], BF16)
    m.vp = sb("values", [P, 2, 2, TPI, H, OW])
    m.mxp = sb("maxima", [P, 2, TPI, C + MAX_ROWS], BF16)
    m.oT = sb("outT", [C + 1, 2, N])
    m.vec = sb("vec", [C, NV])
    m.bn = sb("bn", [C, 2, 3])
    m.wT = sb("wT", [C + 1, NM, C])
    m.dw0 = sb("dw0", [C, 3, 9])
    m.qkv3 = sb("qkv3", [C, 3 * C])
    m.proj3 = sb("proj3", [C + 1, C])
    m.ffn = []
    for l in (2, 3):
        f = Names()
        f.gate = sb(f"gate{l}", [C + 1, E])
        f.w1 = sb(f"w1_{l}", [C, E, HID])
        f.b1rows = sb(f"b1rows{l}", [E * HC, P])
        f.b1 = sb(f"b1_{l}", [P, E * HC])
        f.w2 = sb(f"w2_{l}", [P, E * HC, C])
        f.b2 = sb(f"b2_{l}", [P, E, C])
        m.ffn.append(f)
    return m


def early_buffers(nc, m, ctx):
    def sb(name, shape, dt=F32):
        return ctx.enter_context(nc.sbuf_tensor(name, shape, dt))

    m.pw = sb("pointwise", [C, T])
    m.chan = sb("chan", [C, T])
    m.x = m.chan[:, :].rearrange("c (b n) -> c b n", n=N)
    m.vecrows = sb("vecrows", [NV, C])
    m.raw = sb("raw", [C, NM, C + 1])
    m.rawv = sb("rawv", [C, C])
    m.dwk = sb("dwk", [C, KW * KW])
    m.lines = sb("lines", [C, LINE])
    m.win = sb("windows", [P, SLOTS, CG, WIN])
    m.cb = sb("conv_bias", [P, G])
    m.lines_d = nc.dram_tensor("lines_d", [C, LINE], F32, kind="Internal").ap()
    m.bias_d = nc.dram_tensor("bias_d", [C, 1], F32, kind="Internal").ap()


def load_windows(sp, m, s_win, g, k):
    for c in range(CG):
        sp.dma_start(m.win[WW * c:WW * (c + 1), k, c, :],
                     bass.AP(m.lines_d.tensor, g * (CG * LINE) + c * LINE, [[KW, WW], [1, WIN]])).then_inc(s_win, 16)


def channel_attention(nc, m, a, sem):
    s_x = [sem(f"in_x{k}") for k in range(4)]
    s_w0, s_vec, s_mat, s_b1, s_dwk, s_rest = (sem(f"in_{n}") for n in (
        "weights0", "vectors", "matrices", "b1", "dwk", "rest"))
    m.s_waited = sem("waited")
    s_const, s_pool, s_vecT, s_vecS, s_rstd = (sem(n) for n in ("constants", "pool_own", "vectors_turned", "vectors_kept", "bn_rstd"))
    s_dve, s_taps, s_fold, s_wps, s_wT, s_zero = (sem(n) for n in (
        "setup_dve", "v_taps", "folded", "weights_turned", "weights_kept", "windows_zeroed"))
    s_lines, s_bias = sem("lines_stored"), sem("conv_bias")
    s_ones, s_pt, s_ptk = (sem(n) for n in ("ones_row", "pointwise", "pointwise_kept"))
    s_win = [sem(f"windows{k}") for k in range(SLOTS)]
    s_st, s_gm, s_gdve, s_grs, s_shift = (sem(n) for n in ("gn_means", "gn_psum", "gn_dve", "gn_rstd", "gn_shift"))
    s_tap = [sem(f"ca_tap{t}") for t in range(2)]
    (s_xn, s_qk, s_raw, s_v, s_vc, s_ss, s_rn, s_kn, s_T, s_trs, s_sc, s_mx, s_nm, s_ex, s_rc, s_at, s_ap, s_aps, s_out, s_x1) = (
        sem(f"ca_{n}") for n in ("normed", "qk", "qk_kept", "v", "v_kept", "squares", "norms", "k_scaled", "turned", "turned_kept",
                                 "scores", "max", "shift", "exp", "recip", "attn", "attnproj", "attnproj_kept", "out", "x1"))
    n_vec = len(VECTORS) + 2
    ps = m.ps
    with ExitStack() as ctx:
        def sb(name, shape, dt=F32):
            return ctx.enter_context(nc.sbuf_tensor(name, shape, dt))
        st = sb("gn_stats", [C, B, 6])
        mv = sb("gn_mv", [C, B, 2])
        gm = sb("gn_gm", [C, 4, B])
        shift = sb("gn_shift", [C, B])
        xn = sb("ca_xn", [C, 2, N])
        raw = sb("ca_raw", [C, 2, 2, N])
        qkc = sb("ca_qk", [C, 2, 2, N])
        vc = sb("ca_v", [C, 2, N])
        sq = sb("ca_sq", [C, 2, N])
        ss = sb("ca_ss", [C, 2, 2])
        rn = sb("ca_rn", [C, 2, 3])
        kn = sb("ca_kn", [C, N])
        qkT = sb("ca_qkT", [P, 4, C])
        nm = sb("ca_nm", [C, 2])
        rs = sb("ca_rs", [C, 2])
        at = sb("ca_at", [C, 2, C])
        apT = sb("ca_apT", [C, C])
        x1 = sb("ca_x1", [C + 1, N])

        def steps(eng, step):
            step(0, 0, 0, 2)
            step(1, 1, 1, 2)
            with eng.Fori(1, B // 2 - 1) as j:
                step(2 * j, 0, 2, 2)
                step(2 * j + 1, 1, 2, 2)
            step(B - 2, 0, 2, 1)
            step(B - 1, 1, 2, 0)

        with nc.Block() as block:

            @block.sync
            def _(sp):
                for k in range(4):
                    sp.dma_start(m.x[:, 4 * k:4 * k + 4, :], a['x'].rearrange("b c h w -> c b (h w)")[:, 4 * k:4 * k + 4, :]).then_inc(s_x[k], 16)
                    if k == 0:
                        sp.dma_start(m.raw[:, M_QK0:M_QK0 + 2, 0:C], a['L0_conv_w_qkv'][0:2 * C, :].rearrange("(t o) c -> o t c", t=2)).then_inc(s_w0, 16)
                        sp.dma_start(m.rawv[:, :], a['L0_conv_w_qkv'][2 * C:3 * C, :]).then_inc(s_w0, 16)
                        sp.dma_start(m.dw0[:, :, :], a['L0_conv_w_dw'].rearrange("(t o) i h w -> o t (i h w)", t=3)).then_inc(s_w0, 16)
                        sp.dma_start(m.raw[:, M_PROJ0, 0:C], a['L0_conv_w_proj']).then_inc(s_w0, 16)
                for r, name in enumerate(VECTORS):
                    sp.dma_start(m.vecrows[r:r + 1, :], a[name].rearrange("(o n) -> o n", o=1)).then_inc(s_vec, 16)
                for r, (name, heads) in ((V_T0, ('L0_conv_temperature', CA_H)), (V_T2, ('L2_attn_temperature', H))):
                    sp.dma_start(m.vecrows[r:r + 1, :].rearrange("o (h d e) -> o h d e", h=heads, e=1),
                                 bass.AP(a[name].tensor, 0, [[0, 1], [1, heads], [0, C // heads], [1, 1]])).then_inc(s_vec, 16)
                sp.dma_start(m.dwk[:, :], a['L1_conv_dwk_w'].rearrange("c i h w -> c (i h w)")).then_inc(s_dwk, 16)
                sp.dma_start(m.raw[:, M_PW, 0:C], a['L1_conv_pw_w']).then_inc(s_mat, 16)
                sp.dma_start(m.raw[:, M_QKV2:M_QKV2 + 3, 0:C], a['L2_attn_qkv_w'].rearrange("(t o) c -> o t c", t=3)).then_inc(s_mat, 16)
                sp.dma_start(m.raw[:, M_PROJ2, 0:C], a['L2_attn_proj_w']).then_inc(s_mat, 16)
                for l, f in zip((2, 3), m.ffn):
                    sp.dma_start(f.b1rows[:, :], a[f'L{l}_ffn_b1'].rearrange("e (j p) -> (e j) p", p=P)).then_inc(s_b1, 16)
                sp.wait_ge(s_fold, 2)
                sp.dma_start(m.lines_d, m.lines[:, :]).then_inc(s_lines, 16)
                sp.dma_start(m.bias_d, m.bn[:, 1, 1:2]).then_inc(s_lines, 16)
                sp.dma_start(m.qkv3[:, :], a['L3_attn_w_qkv']).then_inc(s_rest, 16)
                sp.dma_start(m.proj3[0:C, :], a['L3_attn_w_proj']).then_inc(s_rest, 16)
                sp.dma_start(m.proj3[C:C + 1, :], a['L3_attn_b_proj'].rearrange("(o n) -> o n", o=1)).then_inc(s_rest, 16)
                for l, f in zip((2, 3), m.ffn):
                    sp.dma_start(f.gate[0:C, :], a[f'L{l}_ffn_gate_w']).then_inc(s_rest, 16)
                    sp.dma_start(f.gate[C:C + 1, :], a[f'L{l}_ffn_gate_b'].rearrange("(o n) -> o n", o=1)).then_inc(s_rest, 16)
                    sp.dma_start(f.w1[:, :, :], a[f'L{l}_ffn_w1'].rearrange("e d h -> d e h")).then_inc(s_rest, 16)
                    sp.dma_start(f.w2[:, :, :], a[f'L{l}_ffn_w2'].rearrange("e (j p) d -> p (e j) d", p=P)).then_inc(s_rest, 16)
                    sp.dma_start(f.b2[:, :, :], bass.AP(a[f'L{l}_ffn_b2'].tensor, 0, [[0, P], [C, E], [1, C]])).then_inc(s_rest, 16)
                sp.wait_ge(s_lines, 32)
                for c in range(CG):
                    sp.dma_start(m.cb[WW * c:WW * (c + 1), :], bass.AP(m.bias_d.tensor, c, [[0, WW], [CG, G]]),
                                 allow_slow_non_contiguous=True).then_inc(s_bias, 16)
                sp.wait_ge(s_zero, 1)
                for k in range(SLOTS):
                    load_windows(sp, m, s_win[k], k, k)
                sp.wait_ge(s_bias, 16 * CG)

            @block.gpsimd
            def _(pool):
                link = Link(pool, s_pool)
                link(pool.memset(m.ident[:, :], 1.0))
                link(pool.affine_select(out=m.ident[:, :], in_=m.ident[:, :], compare_op=ALU.is_equal, fill=0.0, base=0,
                                        pattern=[[-1, P]], channel_multiplier=1))
                pool.memset(m.power[:, :], -0.5)
                pool.memset(m.eps[:, :], 1e-5)
                link(pool.tensor_copy(m.ident_b[:, :], m.ident[:, :]))

                def blocks_of(tile, blocks, d, fill):
                    v = tile[:, :].rearrange("p (g d) -> p g d", d=d)
                    link(pool.memset(tile[:, :], 0.0 if fill else 1.0))
                    link(pool.affine_select(out=v, in_=v, compare_op=ALU.is_ge, fill=fill, base=0,
                                            pattern=[[-d, blocks], [0, d]], channel_multiplier=1))
                    link(pool.affine_select(out=v, in_=v, compare_op=ALU.is_ge, fill=fill, base=d - 1,
                                            pattern=[[d, blocks], [0, d]], channel_multiplier=-1))
                blocks_of(m.groups, C // GN_CH, GN_CH, 0.0)
                blocks_of(m.heads_b, CA_H, CA_D, MASKED)
                nc.gpsimd.sem_inc(s_const, 1)
                pool.wait_ge(s_gdve, 5)
                link(pool.tensor_scalar(gm[:, 3, :], gm[:, 3, :], 1e-5, 0.0, ALU.add, ALU.add))
                pool.tensor_tensor(gm[:, 1, :], gm[:, 3, :], m.power[0:C, 0:B], ALU.pow).then_inc(s_grs, 1)
                pool.wait_ge(s_vecS, 1)
                link(pool.tensor_scalar(m.bn[:, 0, :], m.vec[:, V_VAR:V_VAR + 3], 1e-5, 0.0, ALU.add, ALU.add))
                pool.tensor_tensor(m.bn[:, 1, :], m.bn[:, 0, :], m.power[0:C, 0:3], ALU.pow).then_inc(s_rstd, 1)

                def step(b, slot, back, ahead):
                    if back:
                        norms(b - 1, 1 - slot)

                def norms(c, slot):
                    pool.wait_ge(s_ss, 2 * c + 3)
                    alone(pool, m)
                    pool.tensor_scalar(rn[:, slot, 0:2], ss[:, slot, :], 1e-24, 1e-24, ALU.max, ALU.max).then_inc(s_rn, 1)
                    pool.wait_ge(s_rn, 3 * c + 1)
                    pool.tensor_tensor(rn[:, slot, 0:2], rn[:, slot, 0:2], m.power[0:C, 0:2], ALU.pow).then_inc(s_rn, 1)
                    pool.wait_ge(s_rn, 3 * c + 2)
                    pool.tensor_tensor(rn[:, slot, 2:3], rn[:, slot, 1:2], m.vec[:, V_T0:V_T0 + 1], ALU.mult).then_inc(s_rn, 1)

                pool.memset(x1[C:C + 1, :], 1.0).then_inc(s_ones, 1)
                pool.wait_ge(s_ones, 1)
                pool.memset(m.win[:, :, :, :], 0.0).then_inc(s_zero, 1)
                steps(pool, step)
                norms(B - 1, 1)
                link(pool.memset(m.diag_b[:, :], 0.0))
                link(pool.affine_select(out=m.diag_b[:, :], in_=m.diag_b[:, :], compare_op=ALU.not_equal, fill=MASKED,
                                        base=0, pattern=[[-1, P]], channel_multiplier=1))
                link(pool.memset(m.later_b[:, :], 0.0))
                link(pool.affine_select(out=m.later_b[:, :], in_=m.later_b[:, :], compare_op=ALU.is_ge, fill=MASKED,
                                        base=0, pattern=[[-1, P]], channel_multiplier=1))
                link(pool.memset(m.before[:, :, :, :], 1.0))
                link(pool.affine_select(out=m.before[:, :, :, :], in_=m.before[:, :, :, :], compare_op=ALU.is_gt, fill=0.0,
                                        base=0, pattern=[[0, 4], [1, E], [-1, E]], channel_multiplier=0))

            @block.tensor
            def _(pe):
                for s in (s_T, s_sc, s_ap, s_out, s_pt):
                    pe.sem_inc(s, 1)
                pe.wait_ge(s_const, 1)

                def turn_weights(first, count, bank):
                    for k in range(count):
                        ins = nc.tensor.transpose(ps[0:C + 1, bank, C * k:C * (k + 1)], m.raw[:, first + k, :], m.ident[0:C, 0:C])
                    ins.then_inc(s_wps, 1)
                pe.wait_ge(s_gdve, 1)
                nc.tensor.matmul(ps[0:C, 6, 0:B], m.groups[:, :], gm[:, 0, :], start=True, stop=True).then_inc(s_gm, 1)
                pe.wait_ge(s_taps, 9)
                pe.wait_ge(s_w0, 64)
                turn_weights(0, 5, 2)
                turn_weights(5, 5, 3)
                turn_weights(10, 2, 4)
                pe.wait_ge(s_gdve, 4)
                nc.tensor.matmul(ps[0:C, 7, 0:B], m.groups[:, :], gm[:, 3, :], start=True, stop=True).then_inc(s_gm, 1)
                pe.wait_ge(s_vec, 16 * n_vec)
                nc.tensor.transpose(ps[0:C, 0, 0:NV], m.vecrows[:, :], m.ident[0:NV, 0:NV]).then_inc(s_vecT, 1)
                pe.wait_ge(s_b1, 32)
                for k, f in enumerate(m.ffn):
                    nc.tensor.transpose(ps[:, 1, 16 * k:16 * k + E * HC], f.b1rows[:, :],
                                        m.ident[0:E * HC, 0:E * HC]).then_inc(s_vecT, 1)
                pe.wait_ge(s_wT, 5)

                def queries_keys(b, slot):
                    pe.wait_ge(s_xn, b + 1)
                    for t in range(2):
                        ins = nc.tensor.matmul(ps[0:C, slot, N * t:N * (t + 1)], m.wT[0:C, M_QK0 + t, :], xn[:, slot, :],
                                               start=True, stop=True)
                    ins.then_inc(s_qk, 1)

                def value_taps(slot, first, last):
                    x = xn[:, slot, :].rearrange("p (y x) -> p y x", x=WW)
                    dst = ps[0:C, 2 + slot, 0:N].rearrange("p (y x) -> p y x", x=WW)
                    for n in range(first, last):
                        dy, dx = TAPS[n]
                        y0, y1, x0, x1 = max(0, -dy), HH - max(0, dy), max(0, -dx), WW - max(0, dx)
                        ins = nc.tensor.matmul(dst[:, y0:y1, x0:x1], m.wT[0:C, M_V0 + 3 * (dy + 1) + dx + 1, :],
                                               x[:, y0 + dy:y1 + dy, x0 + dx:x1 + dx], start=(n == 0), stop=(n == len(TAPS) - 1))
                    return ins

                def step(b, slot, back, ahead):
                    c, other = b - 1, 1 - slot
                    if ahead:
                        if back:
                            pe.wait_ge(s_raw, b)
                        queries_keys(b + 1, other)
                        if back:
                            pe.wait_ge(s_vc, b)
                        value_taps(other, 0, 4)
                    if back:
                        turn(c, other)
                    if back == 2:
                        pointwise(c - 1)
                    if ahead:
                        value_taps(other, 4, 5)
                    if back:
                        scores(c)
                    if ahead:
                        value_taps(other, 5, 9).then_inc(s_v, 1)
                    if back:
                        result(c, other)

                def turn(c, slot):
                    pe.wait_ge(s_kn, c + 1)
                    pe.wait_ge(s_trs, c + 1)
                    for t, src in enumerate((qkc[:, slot, 0, :], kn[:, :])):
                        for h in range(2):
                            ins = nc.tensor.transpose(ps[:, 4, C * (2 * t + h):C * (2 * t + h + 1)], src[:, P * h:P * (h + 1)],
                                                      m.ident[0:C, 0:C])
                    ins.then_inc(s_T, 1)

                def scores(c):
                    pe.wait_ge(s_trs, c + 2)
                    pe.wait_ge(s_ex, c + 1)
                    for h in range(2):
                        nc.tensor.matmul(ps[0:C, 5, 0:C], qkT[:, h, :], qkT[:, 2 + h, :], start=(h == 0), stop=False)
                    nc.tensor.matmul(ps[0:C, 5, 0:C], m.ident_b[0:C, 0:C], m.heads_b[:, :], start=False, stop=True).then_inc(s_sc, 1)

                def result(c, slot):
                    pe.wait_ge(s_ptk, c + 1)
                    nc.tensor.matmul(ps[0:C, 7, 0:N], m.ident[0:C, 0:C], m.x[:, bass.ds(c, 1), :].rearrange("p b n -> p (b n)"),
                                     start=True, stop=False)
                    pe.wait_ge(s_at, c + 1)
                    pe.wait_ge(s_aps, c + 1)
                    nc.tensor.matmul(ps[0:C, 6, 0:C], at[:, 1, :], m.wT[0:C, M_PROJ0, :], start=True, stop=True).then_inc(s_ap, 1)
                    pe.wait_ge(s_aps, c + 2)
                    pe.wait_ge(s_vc, c + 1)
                    nc.tensor.matmul(ps[0:C, 7, 0:N], apT[:, :], vc[:, slot, :], start=False, stop=True).then_inc(s_out, 1)

                def pointwise(c):
                    pe.wait_ge(s_x1, c + 2)
                    nc.tensor.matmul(ps[0:C, 7, 0:N], m.wT[:, M_PW, :], x1[:, :], start=True, stop=True).then_inc(s_pt, 1)

                pe.wait_ge(s_ones, 1)
                queries_keys(0, 0)
                pe.wait_ge(s_fold, 2)
                turn_weights(M_PW, 5, 5)
                value_taps(0, 0, 9).then_inc(s_v, 1)
                pe.wait_ge(s_wT, 6)
                steps(pe, step)
                turn(B - 1, 1)
                pointwise(B - 2)
                scores(B - 1)
                result(B - 1, 1)
                pointwise(B - 1)

            @block.scalar
            def _(act):
                for s in (s_ss, s_trs, s_ex, s_aps, s_x1, s_ptk):
                    act.sem_inc(s, 1)
                nc.scalar.preload_act_table(ACT.Exp)

                def normed(b, slot):
                    nc.scalar.activation(xn[:, slot, :], m.x[:, bass.ds(b, 1), :].rearrange("p b n -> p (b n)"), ACT.Identity,
                                         bias=shift[:, bass.ds(b, 1)], scale=gm[:, 1, bass.ds(b, 1)]).then_inc(s_xn, 1)

                def keep(b, slot):
                    act.wait_ge(s_qk, b + 1)
                    nc.scalar.copy(raw[:, slot, :, :].rearrange("p t n -> p (t n)"), ps[0:C, slot, :]).then_inc(s_raw, 1)

                def squares(c, slot):
                    for t in range(2):
                        act.wait_ge(s_tap[t], 9 * c + 9)
                        act.wait_ge(s_ss, 2 * c + 1 + t)
                        nc.scalar.activation(sq[:, t, :], qkc[:, slot, t, :], ACT.Square, accum_out=ss[:, slot, t:t + 1]).then_inc(s_ss, 1)

                def keep_v(b, slot):
                    act.wait_ge(s_v, b + 1)
                    nc.scalar.copy(vc[:, slot, :], ps[0:C, 2 + slot, 0:N]).then_inc(s_vc, 1)

                def scale_k(c, slot):
                    act.wait_ge(s_rn, 3 * c + 3)
                    act.wait_ge(s_T, c + 1)
                    nc.scalar.activation(kn[:, :], qkc[:, slot, 1, :], ACT.Copy, scale=rn[:, slot, 2:3]).then_inc(s_kn, 1)

                def keep_turned(c):
                    act.wait_ge(s_T, c + 2)
                    act.wait_ge(s_sc, c + 1)
                    nc.scalar.copy(qkT[:, :, :].rearrange("p k c -> p (k c)"), ps[:, 4, 0:4 * C]).then_inc(s_trs, 1)

                def exponential(c, slot):
                    act.wait_ge(s_nm, c + 1)
                    nc.scalar.activation(at[:, 0, :], ps[0:C, 5, 0:C], ACT.Exp, bias=nm[:, 1:2], scale=rn[:, slot, 0:1],
                                         accum_out=rs[:, 0:1]).then_inc(s_ex, 1)

                def keep_product(c):
                    act.wait_ge(s_ap, c + 2)
                    act.wait_ge(s_out, c + 1)
                    nc.scalar.copy(apT[:, :], ps[0:C, 6, 0:C]).then_inc(s_aps, 1)

                def keep_result(c):
                    act.wait_ge(s_out, c + 2)
                    act.wait_ge(s_pt, c + 1)
                    nc.scalar.copy(x1[0:C, :], ps[0:C, 7, 0:N]).then_inc(s_x1, 1)

                def keep_pointwise(c):
                    act.wait_ge(s_pt, c + 2)
                    nc.scalar.copy(m.pw[:, :].rearrange("c (x b y) -> c b y x", b=B, y=HH)[:, bass.ds(c, 1), :, :],
                                   ps[0:C, 7, 0:N].rearrange("c (b y x) -> c b y x", b=1, x=WW)).then_inc(s_ptk, 1)

                def step(b, slot, back, ahead):
                    c, other = b - 1, 1 - slot
                    if back:
                        squares(c, other)
                        act.wait_ge(s_out, b)
                    keep_v(b, slot)
                    if back == 2:
                        keep_result(c - 1)
                    if back:
                        scale_k(c, other)
                    if ahead:
                        if back:
                            for t in range(2):
                                act.wait_ge(s_tap[t], 9 * b)
                        keep(b + 1, other)
                    if back:
                        keep_turned(c)
                    if ahead == 2:
                        act.wait_ge(s_v, b + 1)
                        normed(b + 2, slot)
                    if back == 2:
                        keep_pointwise(c - 1)
                    if back:
                        exponential(c, other)
                        keep_product(c)

                act.wait_ge(s_grs, 1)
                act.wait_ge(s_shift, 1)
                normed(0, 0)
                normed(1, 1)
                keep(0, 0)
                steps(act, step)
                squares(B - 1, 1)
                keep_result(B - 2)
                scale_k(B - 1, 1)
                keep_turned(B - 1)
                keep_pointwise(B - 2)
                exponential(B - 1, 1)
                keep_product(B - 1)
                keep_result(B - 1)
                keep_pointwise(B - 1)
                act.wait_ge(s_ptk, B + 1)

            @block.vector
            def _(dve):
                link = Link(dve, s_dve)
                for b in range(B):
                    if b % 4 == 0:
                        dve.wait_ge(s_x[b // 4], 16)
                    nc.vector.bn_stats(st[:, b, :], m.x[:, b, :]).then_inc(s_st, 1)
                dve.wait_ge(s_st, B)
                for b in range(B):
                    nc.vector.bn_aggr(mv[:, b, :], st[:, b, :]).then_inc(s_st, 1)
                dve.wait_ge(s_st, 2 * B)
                nc.vector.tensor_copy(gm[:, 0, :], mv[:, :, 0]).then_inc(s_gdve, 1)
                dve.wait_ge(s_w0, 64)
                link(nc.vector.memset(m.raw[:, :, C:C + 1], 0.0))
                for k in range(9):
                    nc.vector.tensor_scalar(m.raw[:, M_V0 + k, 0:C], m.rawv[:, :], m.dw0[:, 2, k:k + 1], None, ALU.mult).then_inc(s_taps, 1)
                group = Link(dve, s_gdve, 1)
                dve.wait_ge(s_gm, 1)
                group(nc.vector.tensor_scalar(gm[:, 2, :], ps[0:C, 6, 0:B], 1.0 / GN_CH, None, ALU.mult))
                group(nc.vector.tensor_tensor(gm[:, 3, :], gm[:, 0, :], gm[:, 2, :], ALU.subtract))
                nc.vector.tensor_tensor(gm[:, 1, :], gm[:, 3, :], gm[:, 3, :], ALU.mult).then_inc(s_st, 1)
                dve.wait_ge(s_st, 2 * B + 1)
                group(nc.vector.tensor_tensor(gm[:, 3, :], gm[:, 1, :], mv[:, :, 1], ALU.add))
                dve.wait_ge(s_gm, 2)
                group(nc.vector.tensor_scalar(gm[:, 3, :], ps[0:C, 7, 0:B], 1.0 / GN_CH, None, ALU.mult))
                for n, (first, count, bank) in enumerate(((0, 5, 2), (5, 5, 3), (10, 2, 4))):
                    dve.wait_ge(s_wps, n + 1)
                    nc.vector.tensor_copy(m.wT[:, first:first + count, :],
                                          ps[0:C + 1, bank, 0:count * C].rearrange("p (k c) -> p k c", c=C)).then_inc(s_wT, 1)
                dve.wait_ge(s_grs, 1)
                nc.vector.scalar_tensor_tensor(shift[:, :], gm[:, 2, :], -1.0, gm[:, 1, :], ALU.mult, ALU.mult).then_inc(s_shift, 1)
                dve.wait_ge(s_vecT, 1)
                nc.vector.tensor_copy(m.vec[:, :], ps[0:C, 0, 0:NV]).then_inc(s_vecS, 1)
                dve.wait_ge(s_vecT, 3)
                for k, f in enumerate(m.ffn):
                    nc.vector.tensor_copy(f.b1[:, :], ps[:, 1, 16 * k:16 * k + E * HC]).then_inc(s_wT, 1)
                dve.wait_ge(s_rstd, 1)
                link(nc.vector.tensor_tensor(m.bn[:, 0, :], m.bn[:, 1, :], m.vec[:, V_G:V_G + 3], ALU.mult))
                link(nc.vector.tensor_tensor(m.bn[:, 1, :], m.bn[:, 0, :], m.vec[:, V_M:V_M + 3], ALU.mult))
                link(nc.vector.tensor_tensor(m.bn[:, 1, :], m.vec[:, V_B:V_B + 3], m.bn[:, 1, :], ALU.subtract))
                dve.wait_ge(s_mat, 16 * 3)
                link(nc.vector.scalar_tensor_tensor(m.raw[:, M_PW, 0:C], m.raw[:, M_PW, 0:C], m.bn[:, 0, 0:1],
                                                    m.ident[0:C, 0:C], ALU.mult, ALU.add))
                link(nc.vector.tensor_copy(m.raw[:, M_PW, C:C + 1], m.bn[:, 1, 0:1]))
                link(nc.vector.tensor_copy(m.raw[:, M_PROJ2, C:C + 1], m.vec[:, V_PROJ:V_PROJ + 1]))
                link(nc.vector.reciprocal(m.vec[:, V_T2:V_T2 + 1], m.vec[:, V_T2:V_T2 + 1]))
                link(nc.vector.tensor_scalar(m.raw[:, M_QKV2, 0:C], m.raw[:, M_QKV2, 0:C], m.vec[:, V_T2:V_T2 + 1],
                                             float(C) ** -0.5, ALU.mult, ALU.mult))
                dve.wait_ge(s_dwk, 16)
                link(nc.vector.tensor_scalar(m.dwk[:, :], m.dwk[:, :], m.bn[:, 0, 1:2], None, ALU.mult))
                centre = R * KW + R
                link(nc.vector.scalar_tensor_tensor(m.dwk[:, centre:centre + 1], m.vec[:, V_DW1:V_DW1 + 1], m.bn[:, 0, 2:3],
                                                    m.dwk[:, centre:centre + 1], ALU.mult, ALU.add))
                link(nc.vector.memset(m.lines[:, :], 0.0))
                nc.vector.tensor_copy(m.lines[:, LEAD * KW:(LEAD + KW) * KW].rearrange("c (k j) -> c k j", j=KW),
                                      m.dwk[:, :].rearrange("c (j k) -> c k j", k=KW)).then_inc(s_fold, 1)
                nc.vector.tensor_tensor(m.bn[:, 1, 1:2], m.bn[:, 1, 1:2], m.bn[:, 1, 2:3], ALU.add).then_inc(s_fold, 1)
                dve.wait_ge(s_wps, 4)
                nc.vector.tensor_copy(m.wT[:, M_PW:NM, :], ps[0:C + 1, 5, 0:5 * C].rearrange("p (k c) -> p k c", c=C)).then_inc(s_wT, 1)

                def convolve(b, slot, first, last):
                    for n in range(first, last):
                        dy, dx = TAPS[n]
                        y0, y1, x0, x1 = max(0, -dy), HH - max(0, dy), max(0, -dx), WW - max(0, dx)
                        k = 3 * (dy + 1) + dx + 1
                        for t in range(2):
                            src = raw[:, slot, t, :].rearrange("p (y x) -> p y x", x=WW)
                            dst = qkc[:, slot, t, :].rearrange("p (y x) -> p y x", x=WW)
                            if n == 0:
                                nc.vector.tensor_scalar(dst, src, m.dw0[:, t, k:k + 1], None, ALU.mult).then_inc(s_tap[t], 1)
                                continue
                            dve.wait_ge(s_tap[t], 9 * b + n)
                            nc.vector.scalar_tensor_tensor(
                                dst[:, y0:y1, x0:x1], src[:, y0 + dy:y1 + dy, x0 + dx:x1 + dx], m.dw0[:, t, k:k + 1],
                                dst[:, y0:y1, x0:x1], ALU.mult, ALU.add).then_inc(s_tap[t], 1)

                def maximum(c, slot):
                    dve.wait_ge(s_sc, c + 2)
                    nc.vector.tensor_reduce(nm[:, 0:1], ps[0:C, 5, 0:C], AX.X, ALU.max, negate=True).then_inc(s_mx, 1)
                    dve.wait_ge(s_mx, c + 1)
                    nc.vector.tensor_tensor(nm[:, 1:2], nm[:, 0:1], rn[:, slot, 0:1], ALU.mult).then_inc(s_nm, 1)

                def attention(c):
                    dve.wait_ge(s_ex, c + 2)
                    nc.vector.reciprocal(rs[:, 1:2], rs[:, 0:1]).then_inc(s_rc, 1)
                    dve.wait_ge(s_rc, c + 1)
                    dve.wait_ge(s_ap, c + 1)
                    nc.vector.tensor_scalar(at[:, 1, :], at[:, 0, :], rs[:, 1:2], None, ALU.mult).then_inc(s_at, 1)

                def step(b, slot, back, ahead):
                    c = b - 1
                    dve.wait_ge(s_raw, b + 1)
                    convolve(b, slot, 0, 7)
                    if back:
                        maximum(c, 1 - slot)
                    convolve(b, slot, 7, 8)
                    if back:
                        attention(c)
                    convolve(b, slot, 8, 9)

                steps(dve, step)
                maximum(B - 1, 1)
                attention(B - 1)
                dve.wait_ge(s_rest, 16 * 13)
                link(nc.vector.tensor_scalar(m.qkv3[:, 0:C], m.qkv3[:, 0:C], float(D) ** -0.5, None, ALU.mult))


def large_conv(nc, m, sem):
    s_win = [sem(f"windows{k}") for k in range(SLOTS)]
    s_pw, s_pwk, s_ct, s_cin = (sem(n) for n in (
        "cv_pointwise", "cv_pointwise_kept", "cv_turned", "cv_columns"))
    s_cmk_dve = sem("cv_chan_kept_dve")
    s_cv, s_gl, s_bt, s_btk, s_cm, s_cmk, s_tm, s_tmk, s_st, s_mv = (sem(n) for n in (
        "cv_conv", "cv_gelu", "cv_back", "cv_back_kept", "cv_chan", "cv_chan_kept", "cv_tok", "cv_tok_kept", "cv_stats", "cv_mv"))
    ps = m.ps
    win, cb = m.win, m.cb
    with ExitStack() as ctx:
        def sb(name, shape, dt=F32):
            return ctx.enter_context(nc.sbuf_tensor(name, shape, dt))
        rows = sb("cv_rows", [P, 2, C, WW])
        cin = sb("cv_cin", [P, G, B, HH])
        gl = sb("cv_gl", [P, G, 2, P])
        back = sb("cv_backs", [P, 2, WW, C])
        st = sb("cv_st", [P, NT, 6])

        with nc.Block() as block:

            @block.sync
            def _(sp):
                with sp.Fori(1, G // SLOTS) as i:
                    for k in range(SLOTS):
                        sp.wait_ge(s_cv, i * SLOTS + (k + 1 - SLOTS))
                        load_windows(sp, m, s_win[k], i * SLOTS + k, k)

            @block.gpsimd
            def _(pool):
                attention_constants(m, pool, sem("at_constants"))

            @block.tensor
            def _(pe):
                pw = m.pw[:, :].rearrange("c (x h n) -> c h x n", h=2, x=WW)
                for h in range(2):
                    for x in range(WW):
                        nc.tensor.transpose(ps[:, 4 * h + x // 4, C * (x % 4):C * (x % 4 + 1)], pw[:, h, x, :],
                                            m.ident[0:C, 0:C]).then_inc(s_pw, 1)
                for g in range(G):
                    if g % 2 == 0:
                        pe.wait_ge(s_pwk, 8)
                        if g >= 8:
                            pe.wait_ge(s_cin, g // 2 - 3)
                    for h in range(2):
                        k = 2 * (g % 2) + h
                        nc.tensor.transpose(ps[:, g // 2 % 4, P * k:P * (k + 1)],
                                            rows[:, h, CG * g:CG * (g + 1), :].rearrange("p c x -> p (c x)"),
                                            m.ident[:, :]).then_inc(s_ct, 1)
                pe.wait_ge(s_cin, G // 2)
                with pe.Fori(0, G // SLOTS) as i:
                    for k in range(SLOTS):
                        pe.wait_ge(s_win[k], (i + 1) * (16 * CG))
                        pe.wait_ge(s_gl, i * SLOTS + 1)
                        order = [R] + [j for j in range(KW) if j != R]
                        for n, j in enumerate(order):
                            y0, y1 = max(0, R - j), HH - max(0, j - R)
                            ins = nc.tensor.matmul(
                                ps[:, 4 + k, 0:B * HH].rearrange("p (b y) -> p b y", y=HH)[:, :, y0:y1],
                                win[:, k, :, :].rearrange("p c w -> p (c w)")[:, j:CG * WIN:KW],
                                cin[:, bass.ds(i * SLOTS + k, 1), :, y0 + j - R:y1 + j - R].rearrange("p g b y -> p (g b) y"),
                                start=(n == 0), stop=(n == KW - 1))
                        ins.then_inc(s_cv, 1)
                for g in range(G):
                    pe.wait_ge(s_gl, g + 1 + 1)
                    if g % 2 == 0 and g >= 8:
                        pe.wait_ge(s_btk, g // 2 - 3)
                    for h in range(2):
                        k = 2 * h + g % 2
                        nc.tensor.transpose(ps[:, g // 2 % 4, P * k:P * (k + 1)], gl[:, g, h, :], m.ident[:, :]).then_inc(s_bt, 1)
                pe.wait_ge(s_btk, G // 2)
                for h in range(2):
                    for x in range(WW):
                        nc.tensor.transpose(ps[0:C, 4 * h + x // 4, P * (x % 4):P * (x % 4 + 1)], back[:, h, WW - 1 - x, :],
                                            m.ident[:, :]).then_inc(s_cm, 1)
                for t in range(NT):
                    if t % 16 == 0:
                        pe.wait_ge(s_cmk, 2 + t // 8)
                        pe.wait_ge(s_cmk_dve, 2 + t // 8)
                    nc.tensor.transpose(ps[:, t // 4, C * (t % 4):C * (t % 4 + 1)], m.chan[0:C, P * t:P * (t + 1)],
                                        m.ident[0:C, 0:C]).then_inc(s_tm, 1)

            @block.scalar
            def _(act):
                for s in (s_gl,):
                    act.sem_inc(s, 1)
                nc.scalar.preload_act_table(ACT.Gelu)
                for q in range(0, 8, 2):
                    act.wait_ge(s_pw, 4 * (q + 1))
                    nc.scalar.copy(rows[:, q // 4, :, 4 * (q % 4):4 * (q % 4 + 1)].rearrange("p c x -> p x c"),
                                   ps[:, q, 0:4 * C].rearrange("p (x c) -> p x c", c=C)).then_inc(s_pwk, 1)
                with act.Fori(0, G // SLOTS) as i:
                    for k in range(SLOTS):
                        act.wait_ge(s_cv, i * SLOTS + k + 1)
                        nc.scalar.activation(gl[:, bass.ds(i * SLOTS + k, 1), :, :].rearrange("p g h n -> p (g h n)"),
                                             ps[:, 4 + k, 0:B * HH], ACT.Gelu,
                                             bias=cb[:, bass.ds(i * SLOTS + k, 1)]).then_inc(s_gl, 1)

                for q in range(0, 8, 2):
                    act.wait_ge(s_cm, 4 * (q + 1))
                    nc.scalar.copy(m.chan[0:C, :].rearrange("c (h n x) -> c h x n", h=2, x=WW)[:, q // 4, 4 * (q % 4):4 * (q % 4 + 1), :],
                                   ps[0:C, q, :].rearrange("p (x n) -> p x n", x=4)).then_inc(s_cmk, 1)
                for q in range(8):
                    act.wait_ge(s_tm, 4 * (q + 1))
                    nc.scalar.copy(m.tok[:, 4 * q:4 * (q + 1), :].rearrange("p t c -> p (t c)"), ps[:, q, 0:4 * C]).then_inc(s_tmk, 1)

            @block.vector
            def _(dve):
                for q in range(1, 8, 2):
                    dve.wait_ge(s_pw, 4 * (q + 1))
                    nc.vector.tensor_copy(rows[:, q // 4, :, 4 * (q % 4):4 * (q % 4 + 1)].rearrange("p c x -> p x c"),
                                          ps[:, q, 0:4 * C].rearrange("p (x c) -> p x c", c=C)).then_inc(s_pwk, 1)
                for q in range(G // 2):
                    dve.wait_ge(s_ct, 4 * (q + 1))
                    nc.vector.tensor_copy(cin[:, 2 * q:2 * q + 2, :, :].rearrange("p g b y -> p (g b y)"), ps[:, q % 4, :]).then_inc(s_cin, 1)
                for q in range(G // 2):
                    dve.wait_ge(s_bt, 4 * (q + 1))
                    for h in range(2):
                        ins = nc.vector.tensor_copy(
                            back[:, h, :, 2 * CG * q:2 * CG * (q + 1)].rearrange("p x c -> p c x"),
                            ps[:, q % 4, 2 * P * h:2 * P * (h + 1)].rearrange("p (c x) -> p c x", x=WW))
                    ins.then_inc(s_btk, 1)
                for q in range(1, 8, 2):
                    dve.wait_ge(s_cm, 4 * (q + 1))
                    nc.vector.tensor_copy(m.chan[0:C, :].rearrange("c (h n x) -> c h x n", h=2, x=WW)[:, q // 4, 4 * (q % 4):4 * (q % 4 + 1), :],
                                          ps[0:C, q, :].rearrange("p (x n) -> p x n", x=4)).then_inc(s_cmk_dve, 1)

                def moments(q):
                    dve.wait_ge(s_st, 4 * q + 4)
                    for t in range(4 * q, 4 * q + 4):
                        nc.vector.bn_aggr(m.mv[:, t, :], st[:, t, :]).then_inc(s_mv, 1)

                for q in range(8):
                    dve.wait_ge(s_tmk, q + 1)
                    for t in range(4 * q, 4 * q + 4):
                        nc.vector.bn_stats(st[:, t, :], m.tok[:, t, :]).then_inc(s_st, 1)
                    if q:
                        moments(q - 1)
                moments(7)
                dve.wait_ge(s_mv, NT)


def attention_constants(m, pool, s_c):
    link = Link(pool, s_c)
    for slot in range(2):
        ones = m.ks[C:, slot, :, :, :]
        link(pool.memset(ones, 0.0))
        for k in range(3):
            link(pool.affine_select(out=ones, in_=ones, compare_op=ALU.not_equal, fill=1.0,
                                    base=-H * k, pattern=[[-1, H], [0, 2], [0, N]], channel_multiplier=1))
    link(pool.memset(m.oT[C:C + 1, :, :], 1.0))
    link(pool.memset(m.mxp[:, :, :, :], 0.0))
    link(pool.memset(m.vp[:, :, :, :, :, :], 0.0))
    for slot in range(2):
        for k in range(2 * TPI):
            blocks = m.vp[:, slot, k // TPI, k % TPI, :, :].rearrange("p h w -> p (h w)")
            link(pool.memset(bass.AP(blocks.tensor, blocks.offset + D, [blocks.ap[0], [OW + VD, H], [1, 1]]), 1.0))


def token_rstd(m, pool, i, n, s_rstd, s_mv=None):
    tiles = bass.ds(4 * i, 4)
    if s_mv is not None:
        pool.wait_ge(s_mv, n + 1)
        alone(pool, m)
    pool.tensor_tensor(m.var[:, tiles], m.mv[:, tiles, 1], m.eps[:, :], ALU.add).then_inc(s_rstd, 1)
    pool.wait_ge(s_rstd, 2 * n + 1)
    alone(pool, m)
    pool.tensor_tensor(m.rstd[:, tiles], m.var[:, tiles], m.power[:, 0:4], ALU.pow).then_inc(s_rstd, 1)


def layer_norm(m, pool, n, i, xn, s_own, s_xn, s_free):
    tiles = bass.ds(4 * i, 4)
    pool.wait_ge(*s_free)
    alone(pool, m)
    pool.tensor_tensor(xn[:, :, :], m.tok[:, tiles, :], m.mv[:, tiles, 0].to_broadcast([P, 4, C]),
                       ALU.subtract).then_inc(s_own, 1)
    pool.wait_ge(s_own, n + 1)
    alone(pool, m)
    pool.tensor_tensor(xn[:, :, :], xn[:, :, :], m.rstd[:, tiles].to_broadcast([P, 4, C]), ALU.mult).then_inc(s_xn, 1)


def statistics(nc, m, dve, n, i, st, mv, s_st, s_mv):
    alone(dve, m)
    for t in range(4):
        nc.vector.bn_stats(st[:, t, :], m.tok[:, bass.ds(4 * i + t, 1), :].rearrange("p t c -> p (t c)")).then_inc(s_st, 1)
    dve.wait_ge(s_st, n * 8 + 4)
    alone(dve, m)
    for t in range(4):
        nc.vector.bn_aggr(mv[:, t, :], st[:, t, :]).then_inc(s_st, 1)
    dve.wait_ge(s_st, n * 8 + 8)
    nc.vector.tensor_copy(m.mv[:, bass.ds(4 * i, 4), :], mv[:, :, :]).then_inc(s_mv, 1)


def token_attention(nc, m, sem, layer, w, proj):
    (s_own, s_xn, s_T, s_xT, s_qk, s_p1, s_r1, s_p2, s_p3, s_v, s_vp, s_S, s_mx, s_mp, s_M, s_mr0, s_mr1, s_ST, s_ex, s_O, s_rc,
     s_on, s_OT, s_oT, s_pr, s_tk, s_st, s_mv, s_rstd, s_part) = (sem(f"at_{n}") for n in (
         "pool_own", "normed", "normed_turned", "xT", "qk", "part1", "rest1", "part2", "part3", "v", "v_kept", "scores",
         "max", "max_parts", "max_turned", "max_rows0", "max_rows1", "scoresT", "exp", "out", "recip", "out_normed", "out_turned", "outT",
         "proj", "tok", "stats", "mv", "rstd", "parts_stored"))
    s_rstd_in, s_zero = sem("at_rstd_in"), sem("at_masked")
    s_stack = [sem(f"at_stacks{k}") for k in range(2)]
    s_own_dve = sem("at_dve_own")
    causal = layer == 3
    first = PAIRS if causal else 0
    end = first + PAIRS
    mask = m.later_b if causal else m.diag_b
    ps = m.ps
    KR = C + MAX_ROWS
    W = 2 * N
    ks, vp, mxp, oT = m.ks, m.vp, m.mxp, m.oT
    with ExitStack() as ctx:
        def sb(name, shape, dt=F32):
            return ctx.enter_context(nc.sbuf_tensor(f"at{layer}_b_{name}", shape, dt))
        xn = sb("xn", [P, 4, C])
        xT = sb("xT", [C, 2, 2, N])
        part = sb("part", [C, 3, 2, 2, N], BF16)
        rest = sb("rest", [C, 2, 2, N])
        qs = sb("qs", [KR, 2, H, 2, N], BF16)
        mf = sb("mf", [P, 2, 2, TPI, H])
        pT = sb("pT", [P, 2, TPI, H, N])
        rec = sb("rec", [P, 2, TPI, H])
        on = sb("on", [P, 2, TPI, C])
        st = sb("st", [P, 4, 6])
        mv = sb("mv", [P, 4, 2])
        parts_d = nc.dram_tensor(f"at{layer}_parts", [2, 3, D, PAIRS, H, W], BF16, kind="Internal").ap()

        def heads(k):
            return ps[:, k:k + 3, :].rearrange("p k n -> p (k n)").rearrange("p (h n) -> p h n", h=H)

        turned_max = ps[0:KR, 6, 0:P].bitcast(BF16)

        def max_rows():
            rows = turned_max[C:KR, :]
            return bass.AP(rows.tensor, rows.offset, [rows.ap[0], [0, H], [1, N]])

        with nc.Block() as block:

            @block.sync
            def _(sp):
                def stacks(i, slot):
                    for k, s in enumerate((s_p1, s_p2, s_p3)):
                        sp.wait_ge(s, 2 * i + 2)
                        for t in range(2):
                            sp.dma_start(parts_d[t, 2 - k if t else k, :, bass.ds(i - first, 1), :, :].rearrange("d i h n -> h (d i) n"),
                                         part[:, k, t, :, :].rearrange("c u n -> c (u n)")).then_inc(s_part, 16)
                    sp.wait_ge(s_part, 96 * i + 96)
                    for row, count in ((0, 3), (3, 2), (5, 1)):
                        for t, stack in enumerate((qs, ks)):
                            start = 3 - count if t else 0
                            sp.dma_start(stack[D * row:D * (row + count), slot, :, :, :].rearrange("r h u n -> r (h u n)"),
                                         parts_d[t, start:start + count, :, bass.ds(i - first, 1), :, :].rearrange(
                                             "k d i h n -> (k d) (i h n)")).then_inc(s_stack[slot], 16)

                with sp.Fori(first // 2, end // 2) as j:
                    for slot in range(2):
                        stacks(2 * j + slot, slot)

            @block.gpsimd
            def _(pool):
                def normed(i):
                    token_rstd(m, pool, i - first, i, s_rstd_in)
                    pool.wait_ge(s_rstd_in, 2 * i + 2)
                    layer_norm(m, pool, i, i - first, xn, s_own, s_xn, (s_T, i + 1))

                def masked(i, u):
                    for t in range(TPI):
                        block = pT[:, u, t, :, P * t:P * (t + 1)]
                        pool.wait_ge(s_ex, 4 * i + 2 * u + t + 1)
                        alone(pool, m)
                        pool.affine_select(out=block, in_=block, compare_op=ALU.is_ge if causal else ALU.not_equal, fill=0.0,
                                           base=0, pattern=[[0, H], [1, P]], channel_multiplier=-1).then_inc(s_zero, 1)

                def step(i, ahead, nxt=True):
                    masked(i, 1)
                    if ahead:
                        normed(i + 3)
                    if nxt:
                        masked(i + 1, 0)
                    token_rstd(m, pool, i - first, i, s_rstd, s_mv)

                for i in range(first, first + 3):
                    normed(i)
                masked(first, 0)
                with pool.Fori(first, end - 3) as i:
                    step(i, True)
                step(end - 3, False)
                step(end - 2, False)
                step(end - 1, False, False)
                pool.wait_ge(s_rstd, 2 * end)

            @block.tensor
            def _(pe):
                if first == 0:
                    pe.sem_inc(s_T, 1)

                def turn(i):
                    pe.wait_ge(s_xn, i + 1)
                    for t in range(4):
                        ins = nc.tensor.transpose(ps[0:C, 6, P * t:P * (t + 1)], xn[:, t, :], m.ident[:, :])
                    ins.then_inc(s_T, 1)

                def queries_keys(i, slot):
                    pe.wait_ge(s_xT, i + 1)
                    for u in range(2):
                        for t in range(2):
                            ins = nc.tensor.matmul(ps[0:C, 3 * u, N * t:N * (t + 1)], w[t], xT[:, slot, u, :], start=True, stop=True)
                        ins.then_inc(s_qk, 1)

                def values(i, slot):
                    for u in range(2):
                        for t in range(TPI):
                            ins = nc.tensor.matmul(ps[:, 3 * u + 1, C * t:C * (t + 1)], xT[:, slot, u, P * t:P * (t + 1)], w[2],
                                                   start=True, stop=True)
                        ins.then_inc(s_v, 1)

                def scores(i, slot, u, t):
                    bank = heads(3 * t)
                    nk = P if causal and t == 0 else N
                    for h in range(H):
                        nc.tensor.matmul(bank[:, h, 0:nk], qs[0:C, slot, h, u, P * t:P * (t + 1)], ks[0:C, slot, h, u, 0:nk],
                                         start=True, stop=False)
                        ins = nc.tensor.matmul(bank[:, h, P * t:P * (t + 1)], m.ident_b[:, :], mask[:, :],
                                               start=False, stop=True)
                    ins.then_inc(s_S, 1)

                def transposed_scores(i, slot, u, t):
                    bank = heads(3 * t)
                    n0 = P if causal and t == 1 else 0
                    for h in range(H):
                        ins = nc.tensor.matmul(bank[:, h, n0:N], ks[:, slot, h, u, P * t:P * (t + 1)],
                                               qs[:, slot, h, u, n0:N], start=True, stop=True)
                    ins.then_inc(s_ST, 1)

                def turn_maxima(i, u):
                    pe.wait_ge(s_mp, 2 * i + u + 1)
                    for t in range(TPI):
                        ins = nc.tensor.transpose(turned_max[:, P * t:P * (t + 1)], mxp[:, u, t, :], m.ident_b[:, :])
                    ins.then_inc(s_M, 1)

                def weighted_values(i, slot, u, t):
                    if t == 0:
                        pe.wait_ge(s_zero, 4 * i + 2 * u + 2)
                    terms = [(k, h) for k in range(1 if causal and t == 0 else TPI) for h in range(H)]
                    for n, (k, h) in enumerate(terms):
                        ins = nc.tensor.matmul(ps[:, 6 + u, OW * t:OW * (t + 1)], pT[:, u, k, h, P * t:P * (t + 1)],
                                               vp[:, slot, u, k, h, :], start=(n == 0), stop=(n == len(terms) - 1))
                    if t == TPI - 1:
                        ins.then_inc(s_O, 1)

                def turn_out(i, u):
                    pe.wait_ge(s_on, 2 * i + u + 1)
                    for t in range(TPI):
                        ins = nc.tensor.transpose(ps[0:C, 6 + u, P * t:P * (t + 1)], on[:, u, t, :], m.ident[:, :])
                    ins.then_inc(s_OT, 1)

                def project(i, u):
                    pe.wait_ge(s_oT, 2 * i + u + 1)
                    for t in range(TPI):
                        ins = nc.tensor.matmul(ps[:, 6 + u, C * t:C * (t + 1)], oT[:, u, P * t:P * (t + 1)], proj,
                                               start=True, stop=True)
                    ins.then_inc(s_pr, 1)

                def back_and_front(i, slot):
                    back = i is not first
                    pe.wait_ge(s_stack[slot], 48 * (i - slot) + 96)
                    pe.wait_ge(s_vp, 2 * i + 1)
                    scores(i, slot, 0, 0)
                    if back:
                        turn_out(i - 1, 0)
                    pe.wait_ge(s_vp, 2 * i + 2)
                    scores(i, slot, 0, 1)
                    if back:
                        project(i - 1, 0)
                        weighted_values(i - 1, 1 - slot, 1, 0)
                    pe.wait_ge(s_mx, 4 * i + 1)
                    scores(i, slot, 1, 0)
                    if back:
                        pe.wait_ge(s_tk, 2 * i - 1)
                    pe.wait_ge(s_mx, 4 * i + 2)
                    scores(i, slot, 1, 1)
                    turn_maxima(i, 0)
                    if back:
                        weighted_values(i - 1, 1 - slot, 1, 1)
                    pe.wait_ge(s_mx, 4 * i + 3)
                    pe.wait_ge(s_mr0, i + 1)
                    transposed_scores(i, slot, 0, 0)
                    turn_maxima(i, 1)
                    if back:
                        turn_out(i - 1, 1)
                    pe.wait_ge(s_mx, 4 * i + 4)
                    transposed_scores(i, slot, 0, 1)
                    if back:
                        project(i - 1, 1)
                    pe.wait_ge(s_mr1, i + 1)

                def middle(i, slot, ahead):
                    if ahead == 2:
                        turn(i + 2)
                    pe.wait_ge(s_ex, 4 * i + 1)
                    transposed_scores(i, slot, 1, 0)
                    pe.wait_ge(s_ex, 4 * i + 2)
                    transposed_scores(i, slot, 1, 1)
                    if ahead == 2:
                        pe.wait_ge(s_xT, i + 3)
                    weighted_values(i, slot, 0, 0)
                    pe.wait_ge(s_ex, 4 * i + 4)
                    if ahead == 2:
                        queries_keys(i + 2, slot)
                    if ahead:
                        values(i + 1, 1 - slot)
                    weighted_values(i, slot, 0, 1)

                turn(first)
                queries_keys(first, 0)
                values(first, 0)
                turn(first + 1)
                pe.wait_ge(s_r1, 2 * first + 2)
                queries_keys(first + 1, 1)
                pe.wait_ge(s_r1, 2 * first + 4)
                back_and_front(first, 0)
                with pe.Fori(first // 2, end // 2 - 1) as j:
                    for slot in range(2):
                        middle(2 * j + slot, slot, 2)
                        back_and_front(2 * j + slot + 1, 1 - slot)
                middle(end - 2, 0, 1)
                back_and_front(end - 1, 1)
                middle(end - 1, 1, 0)
                weighted_values(end - 1, 1, 1, 0)
                turn_out(end - 1, 0)
                weighted_values(end - 1, 1, 1, 1)
                project(end - 1, 0)
                turn_out(end - 1, 1)
                project(end - 1, 1)

            @block.scalar
            def _(act):
                nc.scalar.preload_act_table(ACT.Exp)

                def parts(i, waits=True):
                    if waits:
                        act.wait_ge(s_part, 96 * i)
                    for u in range(2):
                        act.wait_ge(s_qk, 2 * i + u + 1)
                        nc.scalar.copy(part[:, 0, :, u, :], ps[0:C, 3 * u, :].rearrange("c (t n) -> c t n", t=2)).then_inc(s_p1, 1)
                    for u in range(2):
                        act.wait_ge(s_r1, 2 * i + u + 1)
                        nc.scalar.copy(part[:, 1, :, u, :], rest[:, u, :, :]).then_inc(s_p2, 1)

                def weights(i, u, tiles=range(TPI)):
                    for t in tiles:
                        n0 = P if causal and t == 1 else 0
                        act.wait_ge(s_ST, 4 * i + 2 * u + t + 1)
                        nc.scalar.activation(pT[:, u, t, :, n0:N], heads(3 * t)[:, :, n0:N], ACT.Exp).then_inc(s_ex, 1)

                def rows(i, slot):
                    act.wait_ge(s_M, 2 * i + 1)
                    nc.scalar.copy(qs[C:KR, slot, :, 0, :], max_rows()).then_inc(s_mr0, 1)

                def out(i, u):
                    act.wait_ge(s_OT, 2 * i + u + 1)
                    nc.scalar.copy(oT[0:C, u, :], ps[0:C, 6 + u, 0:N]).then_inc(s_oT, 1)

                def step(i, slot, ahead):
                    weights(i, 1)
                    if ahead == 2:
                        parts(i + 2)
                    out(i, 0)
                    if ahead:
                        rows(i + 1, 1 - slot)
                        weights(i + 1, 0, (0,))
                    out(i, 1)
                    if ahead:
                        weights(i + 1, 0, (1,))

                parts(first, waits=first > 0)
                parts(first + 1)
                rows(first, 0)
                weights(first, 0)
                with act.Fori(first // 2, end // 2 - 1) as j:
                    for slot in range(2):
                        step(2 * j + slot, slot, 2)
                step(end - 2, 0, 1)
                step(end - 1, 1, 0)

            @block.vector
            def _(dve):

                def normed(i, slot):
                    dve.wait_ge(s_T, i + 2)
                    nc.vector.tensor_copy(xT[:, slot, :, :].rearrange("c u n -> c (u n)"), ps[0:C, 6, :]).then_inc(s_xT, 1)

                def parts(i):
                    for u in range(2):
                        dve.wait_ge(s_p1, 2 * i + u + 1)
                        nc.vector.tensor_tensor(rest[:, u, :, :], ps[0:C, 3 * u, :].rearrange("c (t n) -> c t n", t=2),
                                                part[:, 0, :, u, :], ALU.subtract).then_inc(s_r1, 1)
                    for u in range(2):
                        dve.wait_ge(s_p2, 2 * i + u + 1)
                        nc.vector.tensor_tensor(part[:, 2, :, u, :], rest[:, u, :, :], part[:, 1, :, u, :],
                                                ALU.subtract).then_inc(s_p3, 1)

                def values(i, slot):
                    for u in range(2):
                        dve.wait_ge(s_v, 2 * i + u + 1)
                        for t in range(TPI):
                            blocks = vp[:, slot, u, t, :, :].rearrange("p h w -> p (h w)")
                            ins = nc.vector.tensor_copy(
                                bass.AP(blocks.tensor, blocks.offset, [blocks.ap[0], [OW + VD, H], [1, D]]),
                                ps[:, 3 * u + 1, C * t:C * (t + 1)].rearrange("p (h d) -> p h d", d=D))
                        ins.then_inc(s_vp, 1)

                def maximum(i, u, t):
                    nk = P if causal and t == 0 else N
                    dve.wait_ge(s_S, 4 * i + 2 * u + t + 1)
                    nc.vector.tensor_reduce(mf[:, u, 0, t, :], heads(3 * t)[:, :, 0:nk], AX.X, ALU.max,
                                            negate=True).then_inc(s_mx, 1)

                def maxima_parts(i, u):
                    own = 6 * i + 3 * u
                    dve.wait_ge(s_mx, 4 * i + 2 * u + 2)
                    nc.vector.tensor_copy(mxp[:, u, :, C:C + H], mf[:, u, 0, :, :]).then_inc(s_own_dve, 1)
                    dve.wait_ge(s_own_dve, own + 1)
                    nc.vector.tensor_tensor(mf[:, u, 1, :, :], mf[:, u, 0, :, :], mxp[:, u, :, C:C + H],
                                            ALU.subtract).then_inc(s_own_dve, 1)
                    dve.wait_ge(s_own_dve, own + 2)
                    nc.vector.tensor_copy(mxp[:, u, :, C + H:C + 2 * H], mf[:, u, 1, :, :]).then_inc(s_own_dve, 1)
                    dve.wait_ge(s_own_dve, own + 3)
                    nc.vector.tensor_tensor(mxp[:, u, :, C + 2 * H:KR], mf[:, u, 1, :, :], mxp[:, u, :, C + H:C + 2 * H],
                                            ALU.subtract).then_inc(s_mp, 1)

                def rows(i, slot):
                    dve.wait_ge(s_M, 2 * i + 2)
                    nc.vector.tensor_copy(qs[C:KR, slot, :, 1, :], max_rows()).then_inc(s_mr1, 1)

                def out(i, u):
                    dve.wait_ge(s_O, 2 * i + u + 1)
                    o = ps[:, 6 + u, 0:TPI * OW].rearrange("p (t h w) -> p t h w", t=TPI, h=H)
                    nc.vector.reciprocal(rec[:, u, :, :], o[:, :, :, D]).then_inc(s_rc, 1)
                    dve.wait_ge(s_rc, 2 * i + u + 1)
                    nc.vector.tensor_tensor(on[:, u, :, :].rearrange("p t (h d) -> p t h d", d=D), o[:, :, :, 0:D],
                                            rec[:, u, :, :].to_broadcast([P, TPI, H, D]), ALU.mult).then_inc(s_on, 1)

                def add(i, u):
                    dve.wait_ge(s_pr, 2 * i + u + 1)
                    tok = m.tok[:, bass.ds(4 * (i - first) + 2 * u, 2), :]
                    nc.vector.tensor_tensor(tok, ps[:, 6 + u, 0:2 * C].rearrange("p (t c) -> p t c", c=C), tok,
                                            ALU.add).then_inc(s_tk, 1)

                def moments(i):
                    dve.wait_ge(s_tk, 2 * i + 2)
                    statistics(nc, m, dve, i, i - first, st, mv, s_st, s_mv)

                def maxima(i, slot):
                    back = i is not first
                    maximum(i, 0, 0)
                    if back:
                        add(i - 1, 0)
                    maximum(i, 0, 1)
                    maxima_parts(i, 0)
                    maximum(i, 1, 0)
                    maximum(i, 1, 1)
                    maxima_parts(i, 1)
                    if back:
                        out(i - 1, 1)
                    rows(i, slot)
                    if back:
                        add(i - 1, 1)

                normed(first, 0)
                parts(first)
                values(first, 0)
                normed(first + 1, 1)
                parts(first + 1)
                maxima(first, 0)
                normed(first + 2, 0)

                def step(i, slot, ahead):
                    if ahead >= 2:
                        parts(i + 2)
                    values(i + 1, 1 - slot)
                    out(i, 0)
                    maxima(i + 1, 1 - slot)
                    if ahead >= 3:
                        normed(i + 3, 1 - slot)
                    moments(i)

                with dve.Fori(first // 2, end // 2 - 2) as j:
                    for slot in range(2):
                        step(2 * j + slot, slot, 3)
                for i in range(end - 4, end - 1):
                    step(i, i % 2, end - 1 - i)
                for u in range(2):
                    out(end - 1, u)
                for u in range(2):
                    add(end - 1, u)
                moments(end - 1)
                dve.wait_ge(s_mv, end)


def experts(nc, m, sem, layer, f, out=None):
    (s_ones, s_xn, s_own, s_T, s_xT, s_xh, s_xl, s_w, s_gt, s_nm, s_ex, s_gd, s_own_pool, s_bt, s_tb, s_F, s_h, s_Y, s_ac,
     s_st, s_mv, s_OT, s_oc, s_store) = (sem(f"ff_{n}") for n in (
         "ones", "normed", "dve_own", "normed_turned", "xT", "x_high", "x_low", "w_parts", "gate_products", "gate_shifted",
         "gate_exp", "gate_dve", "pool_own", "bias", "tok_biased", "hidden", "gelu", "result", "added", "stats", "mv",
         "out_turned", "out_kept", "stored"))
    last = out is not None
    first = PAIRS if last else 0
    end = first + PAIRS
    ps = m.ps
    with ExitStack() as ctx:
        def sb(name, shape, dt=F32):
            return ctx.enter_context(nc.sbuf_tensor(f"ff{layer}_b_{name}", shape, dt))
        xn = sb("xn", [P, 4, C])
        xT = sb("xT", [C + 1, Q])
        xh = sb("xh", [C, Q], F32R)
        xl = sb("xl", [C, Q], F32R)
        wh = sb("wh", [C, E, HID], F32R)
        wl = sb("wl", [C, E, HID], F32R)
        sc = sb("sc", [P, 4, E])
        pr = sb("pr", [P, 4, E])
        gt = sb("gt", [P, 4, E, E])
        eq = sb("eq", [P, 4, E, E])
        one = sb("one", [P, 3, 4])
        gate = sb("gate", [P, NT, E])
        bias = sb("bias", [P, 4, C])
        term = sb("term", [P, 4, C])
        h = sb("h", [P, 2, HC, Q])
        st = sb("st", [P, 4, 6])
        mv = sb("mv", [P, 4, 2])
        fin = sb("fin", [P, 4, C])
        fT = sb("fT", [C, Q])

        def tiles(i):
            return bass.ds(4 * (i - first), 4)

        def parts(eng, part):
            if last:
                part(first, False, True)
            with eng.Fori(first + last, end - 1) as i:
                part(i, last, True)
            part(end - 1, last, False)

        with nc.Block() as block:

            if last:
                @block.sync
                def _(sp):
                    sp.sem_inc(s_store, 1)
                    with sp.Fori(first, end) as i:
                        sp.wait_ge(s_oc, i - first + 1)
                        sp.dma_start(out.rearrange("b c h w -> c b (h w)")[:, bass.ds(2 * (i - first), 2), :],
                                     fT[:, :].rearrange("c (b n) -> c b n", n=N)).then_inc(s_store, 16)
                    sp.wait_ge(s_store, 16 * PAIRS + 1)

            @block.gpsimd
            def _(pool):
                if first == 0:
                    pool.sem_inc(s_xl, 1)
                pool.memset(xT[C:C + 1, :], 1.0).then_inc(s_ones, 1)

                def low(i):
                    pool.wait_ge(s_xh, i + 1)
                    pool.tensor_tensor(xl[:, :], xT[0:C, :], xh[:, :], ALU.subtract).then_inc(s_xl, 1)

                def biases(i):
                    link = Link(pool, s_own_pool, i * (2 * E - 2))
                    pool.wait_ge(s_gd, GATE_STEPS * (i + 1))
                    for e in range(E):
                        b2 = f.b2[:, e:e + 1, :]
                        if e == 0:
                            pool.wait_ge(s_tb, i + 1)
                        alone(pool, m)
                        product = pool.tensor_tensor((term if e else bias)[:, :, :], gate[:, tiles(i), e].to_broadcast([P, 4, C]),
                                                     bass.AP(b2.tensor, b2.offset, [b2.ap[0], [0, 4], [1, C]]), ALU.mult)
                        link(product)
                        if e == E - 1:
                            pool.tensor_tensor(bias[:, :, :], bias[:, :, :], term[:, :, :], ALU.add).then_inc(s_bt, 1)
                        elif e:
                            link(pool.tensor_tensor(bias[:, :, :], bias[:, :, :], term[:, :, :], ALU.add))

                def part(i, back, ahead):
                    if ahead:
                        low(i + 1)
                        biases(i + 1)

                pool.wait_ge(s_w, 1 + 2 * last)
                pool.tensor_tensor(wl[:, :, :], f.w1[:, :, :], wh[:, :, :], ALU.subtract).then_inc(s_w, 1)
                low(first)
                biases(first)
                parts(pool, part)

            @block.tensor
            def _(pe):
                if first == 0:
                    for s in (s_T, s_gt, s_Y, s_OT):
                        pe.sem_inc(s, 1)

                def turn(i):
                    pe.wait_ge(s_xn, i + 1)
                    for t in range(4):
                        ins = nc.tensor.transpose(ps[0:C, 0, P * t:P * (t + 1)], xn[:, t, :], m.ident[:, :])
                    ins.then_inc(s_T, 1)

                def gate_products(i):
                    pe.wait_ge(s_xT, i + 1)
                    for t in range(4):
                        ins = nc.tensor.matmul(ps[:, 1, E * t:E * (t + 1)], xT[:, P * t:P * (t + 1)], f.gate[:, :],
                                               start=True, stop=True)
                    ins.then_inc(s_gt, 1)

                def hidden(i, e):
                    for j in range(HC):
                        k = 3 * (e % 2) + j
                        if e >= 2:
                            pe.wait_ge(s_h, i * (E * HC) + ((e - 2) * HC + j + 1) + 1)
                        elif j == 0:
                            pe.wait_ge(s_h, i * (E * HC) + 1)
                        for n, (w, x) in enumerate(((wh, xh), (wh, xl), (wl, xh))):
                            ins = nc.tensor.matmul(ps[:, k, :], w[:, e, P * j:P * (j + 1)], x[:, :], start=(n == 0), stop=(n == 2))
                        ins.then_inc(s_F, 1)

                def result(i, e):
                    pe.wait_ge(s_h, i * (E * HC) + (e + 1) * HC + 1)
                    pe.wait_ge(s_ac, i * E + e + 1)
                    for t in range(4):
                        for j in range(HC):
                            ins = nc.tensor.matmul(ps[:, 6 + e % 2, C * t:C * (t + 1)], h[:, e % 2, j, P * t:P * (t + 1)],
                                                   f.w2[:, e * HC + j, :], start=(j == 0), stop=(j == HC - 1))
                    ins.then_inc(s_Y, 1)

                def turn_output(i):
                    pe.wait_ge(s_ac, i * E + E + 2)
                    for t in range(4):
                        ins = nc.tensor.transpose(ps[0:C, 6, P * t:P * (t + 1)], fin[:, t, :], m.ident[:, :])
                    ins.then_inc(s_OT, 1)

                def part(i, back, ahead):
                    pe.wait_ge(s_xl, i + 2)
                    pe.wait_ge(s_nm, i + 1)
                    hidden(i, 0)
                    hidden(i, 1)
                    if back:
                        turn_output(i - 1)
                        pe.wait_ge(s_oc, i - first)
                    result(i, 0)
                    hidden(i, 2)
                    result(i, 1)
                    hidden(i, 3)
                    if ahead:
                        pe.wait_ge(s_h, i * (E * HC) + 3 * HC + 1)
                        turn(i + 1)
                    result(i, 2)
                    if ahead:
                        gate_products(i + 1)
                    result(i, 3)

                pe.wait_ge(s_ones, 1 + last)
                turn(first)
                gate_products(first)
                pe.wait_ge(s_w, 2 + 2 * last)
                parts(pe, part)
                if last:
                    turn_output(end - 1)

            @block.scalar
            def _(act):
                if first == 0:
                    act.sem_inc(s_h, 1)
                nc.scalar.copy(wh[:, :, :], f.w1[:, :, :]).then_inc(s_w, 1)
                nc.scalar.preload_act_table(ACT.Exp)

                def high(i):
                    act.wait_ge(s_xT, i + 1)
                    nc.scalar.copy(xh[:, :], xT[0:C, :]).then_inc(s_xh, 1)

                def gate_exponential(i):
                    act.wait_ge(s_nm, i + 1)
                    nc.scalar.activation(pr[:, :, :], sc[:, :, :], ACT.Exp).then_inc(s_ex, 1)

                def keep_output(i):
                    act.wait_ge(s_OT, i - first + 2)
                    act.wait_ge(s_store, (i - first) * 16 + 1)
                    nc.scalar.copy(fT[:, :], ps[0:C, 6, :]).then_inc(s_oc, 1)

                def part(i, back, ahead):
                    for e in range(E):
                        if back and e == 2:
                            keep_output(i - 1)
                        for j in range(HC):
                            act.wait_ge(s_F, i * (E * HC) + (e * HC + j + 1))
                            if j == 0:
                                act.wait_ge(s_Y, i * E + (e - 1) + 1) if e >= 2 else act.wait_ge(s_Y, i * E + 1)
                            nc.scalar.activation(h[:, e % 2, j, :], ps[:, 3 * (e % 2) + j, :], ACT.Gelu,
                                                 bias=f.b1[:, e * HC + j:e * HC + j + 1]).then_inc(s_h, 1)
                    if ahead:
                        nc.scalar.preload_act_table(ACT.Exp)
                        high(i + 1)
                        gate_exponential(i + 1)
                        nc.scalar.preload_act_table(ACT.Gelu)

                high(first)
                gate_exponential(first)
                nc.scalar.preload_act_table(ACT.Gelu)
                parts(act, part)
                if last:
                    keep_output(end - 1)

            @block.vector
            def _(dve):
                if first == 0:
                    for s in (s_ac, s_tb):
                        dve.sem_inc(s, 2 if s is s_ac else 1)

                def normed(i):
                    dve.wait_ge(s_T, i + 1)
                    nc.vector.tensor_tensor(xn[:, :, :], m.tok[:, tiles(i), :], m.mv[:, tiles(i), 0].to_broadcast([P, 4, C]),
                                            ALU.subtract).then_inc(s_own, 1)
                    dve.wait_ge(s_own, i + 1)
                    nc.vector.tensor_tensor(xn[:, :, :], xn[:, :, :], m.rstd[:, tiles(i)].to_broadcast([P, 4, C]),
                                            ALU.mult).then_inc(s_xn, 1)

                def turned(i):
                    dve.wait_ge(s_T, i + 1 + 1)
                    dve.wait_ge(s_gt, i + 1)
                    dve.wait_ge(s_xl, i + 1)
                    nc.vector.tensor_copy(xT[0:C, :], ps[0:C, 0, :]).then_inc(s_xT, 1)

                def gate_scores(i):
                    link = Link(dve, s_gd, GATE_STEPS * i)
                    dve.wait_ge(s_gt, i + 1 + 1)
                    scores = ps[:, 1, 0:4 * E].rearrange("p (t e) -> p t e", e=E)
                    link(nc.vector.tensor_reduce(one[:, 0, :], scores, AX.X, ALU.max))
                    nc.vector.tensor_tensor(sc[:, :, :], scores, one[:, 0, :].to_broadcast([P, 4, E]), ALU.subtract).then_inc(s_nm, 1)

                def gates(i):
                    link = Link(dve, s_gd, GATE_STEPS * i + 1)
                    dve.wait_ge(s_ex, i + 1)
                    link(nc.vector.tensor_reduce(one[:, 1, :], pr[:, :, :], AX.X, ALU.add))
                    link(nc.vector.reciprocal(one[:, 2, :], one[:, 1, :]))
                    link(nc.vector.tensor_tensor(pr[:, :, :], pr[:, :, :], one[:, 2, :].to_broadcast([P, 4, E]), ALU.mult))
                    own = pr[:, :, :].to_broadcast([P, 4, E, E])
                    other = bass.AP(pr[:, :, :].tensor, pr[:, :, :].offset, [pr[:, :, :].ap[0], [E, 4], [0, E], [1, E]])
                    link(nc.vector.tensor_tensor(eq[:, :, :, :], other, own, ALU.is_equal))
                    link(nc.vector.tensor_tensor(eq[:, :, :, :], eq[:, :, :, :], m.before[:, :, :, :], ALU.mult))
                    link(nc.vector.tensor_tensor(gt[:, :, :, :], other, own, ALU.is_gt))
                    link(nc.vector.tensor_tensor(gt[:, :, :, :], gt[:, :, :, :], eq[:, :, :, :], ALU.add))
                    link(nc.vector.tensor_reduce(sc[:, :, :], gt[:, :, :, :], AX.X, ALU.add))
                    link(nc.vector.scalar_tensor_tensor(sc[:, :, :], sc[:, :, :], 1.5, pr[:, :, :], ALU.is_lt, ALU.mult))
                    link(nc.vector.tensor_reduce(one[:, 0, :], sc[:, :, :], AX.X, ALU.add))
                    link(nc.vector.tensor_scalar(one[:, 1, :], one[:, 0, :], 1e-9, None, ALU.add))
                    link(nc.vector.reciprocal(one[:, 2, :], one[:, 1, :]))
                    link(nc.vector.tensor_tensor(gate[:, tiles(i), :], sc[:, :, :], one[:, 2, :].to_broadcast([P, 4, E]), ALU.mult))
                    assert link.n == GATE_STEPS - 1

                def add(i, e):
                    dve.wait_ge(s_Y, i * E + (e + 1) + 1)
                    if last and e == E - 1:
                        dve.wait_ge(s_OT, i - first + 1)
                    dve.wait_ge(s_ac, i * E + e + 2)
                    for t in range(4):
                        tile = bass.ds(4 * (i - first) + t, 1)
                        tok = m.tok[:, tile, :].rearrange("p t c -> p (t c)")
                        ins = nc.vector.scalar_tensor_tensor(
                            fin[:, t, :] if last and e == E - 1 else tok, ps[:, 6 + e % 2, C * t:C * (t + 1)],
                            gate[:, tile, e], tok, ALU.mult, ALU.add)
                    ins.then_inc(s_ac, 1)

                def add_bias(i):
                    dve.wait_ge(s_bt, i + 1)
                    dve.wait_ge(s_ac, i * E + 4)
                    nc.vector.tensor_tensor(m.tok[:, tiles(i), :], m.tok[:, tiles(i), :], bias[:, :, :], ALU.add).then_inc(s_tb, 1)
                    dve.wait_ge(s_tb, i + 2)

                def part(i, back, ahead):
                    add(i, 0)
                    if ahead:
                        normed(i + 1)
                    add(i, 1)
                    add_bias(i)
                    if ahead:
                        turned(i + 1)
                    add(i, 2)
                    if ahead:
                        gate_scores(i + 1)
                    add(i, 3)
                    if ahead:
                        gates(i + 1)
                    if not last:
                        dve.wait_ge(s_ac, i * E + E + 2)
                        statistics(nc, m, dve, i, i - first, st, mv, s_st, s_mv)

                normed(first)
                turned(first)
                gate_scores(first)
                gates(first)
                parts(dve, part)
                if not last:
                    dve.wait_ge(s_mv, end)


GATE_STEPS = 14


def program(nc, a, out):
    with ExitStack() as ctx:
        m = buffers(nc, ctx)

        made = {}

        def sem(name):
            if name not in made:
                made[name] = ctx.enter_context(nc.semaphore(name))
            return made[name]
        with ExitStack() as early:
            early_buffers(nc, m, early)
            channel_attention(nc, m, a, sem)
            large_conv(nc, m, sem)
        token_attention(nc, m, sem, 2, [m.wT[0:C, M_QKV2 + t, :] for t in range(3)], m.wT[:, M_PROJ2, :])
        experts(nc, m, sem, 2, m.ffn[0])
        token_attention(nc, m, sem, 3, [m.qkv3[:, C * t:C * (t + 1)] for t in range(3)], m.proj3[:, :])
        experts(nc, m, sem, 3, m.ffn[1], out)


def kernel(**inputs):
    import numpy as np
    import concourse.bacc as bacc
    from concourse.bass_utils import run_bass_kernel_spmd

    nc = bacc.Bacc("TRN2", target_bir_lowering=False, num_devices=1)
    arrays, a = {}, {}
    for name in INS:
        arrays[f"in_{name}"] = np.ascontiguousarray(inputs[name])
        a[name] = nc.dram_tensor(f"in_{name}", arrays[f"in_{name}"].shape, F32, kind="ExternalInput").ap()
    out = nc.dram_tensor("out", (B, C, HH, WW), F32, kind="ExternalOutput").ap()
    program(nc, a, out)
    return run_bass_kernel_spmd(nc, [arrays], core_ids=[0]).results[0]["out"]
```
